# Optimizing a Trainium2 kernel written in Bass

```python
import numpy as np
import jax
import jax.numpy as jnp

def _softmax(x, axis=-1):
    return jax.nn.softmax(x, axis=axis)

def _gelu(x):
    return jax.nn.gelu(x, approximate=True)

def _silu(x):
    return jax.nn.silu(x)

def _sigmoid(x):
    return jax.nn.sigmoid(x)

def _layernorm(x, axis=-1, eps=1e-05):
    m = jnp.mean(x, axis=axis, keepdims=True)
    v = jnp.var(x, axis=axis, keepdims=True)
    return (x - m) / jnp.sqrt(v + eps)

def _scatter_add(tgt, idx, src, axis=0):
    return tgt.at[idx].add(src)

def _segment_sum(src, seg, n):
    return jax.ops.segment_sum(src, seg, n)
kernel_name = 'mk_audio_tower_d1_tok_audfeat1024_r4_880198'

def setup_inputs(seed: int=0):
    np.random.seed(seed)
    _w = jnp.asarray

    def _rec_inputs():
        import jax
        import jax.numpy as jnp
        _rk = jax.random.key(seed)
        x = -0.000125008 + 0.999885 * jax.random.normal(jax.random.fold_in(_rk, 1), (8, 750, 256), jnp.float32)
        return x
    x = _rec_inputs()

    def _L0_tok_setup():
        import jax, jax.numpy as jnp
        import numpy as np
        D_MODEL = 256
        STRIDE = 2
        KERNEL = 2
        INIT_STD = 0.02
        EPS = 1e-05
        key = jax.random.key(seed)
        k1, k2 = jax.random.split(key)
        hidden_states = jax.random.normal(k1, (4, 2048, D_MODEL), dtype=jnp.float32)
        conv_w = INIT_STD * jax.random.normal(k2, (D_MODEL, D_MODEL, KERNEL), dtype=jnp.float32)
        conv_b = jnp.zeros((D_MODEL,), dtype=jnp.float32)
        ln_gamma = jnp.ones((D_MODEL,), dtype=jnp.float32)
        ln_beta = jnp.zeros((D_MODEL,), dtype=jnp.float32)
        return {'hidden_states': hidden_states, 'conv_w': conv_w, 'conv_b': conv_b, 'ln_gamma': ln_gamma, 'ln_beta': ln_beta}
    _L0_tok_all = _L0_tok_setup()
    _L0_tok_in = {k: v for k, v in _L0_tok_all.items() if k in ('conv_w', 'conv_b', 'ln_gamma', 'ln_beta')}
    del _L0_tok_all

    def _L0_attn_setup():
        import jax, jax.numpy as jnp
        import numpy as np
        B, L, IN_DIM = (4, 512, 256)
        H, D = (16, 64)
        OUT_DIM = 256
        key = jax.random.key(seed)
        k1, k2, k3 = jax.random.split(key, 3)
        inputs = jax.random.normal(k1, (B, L, IN_DIM), dtype=jnp.float32)
        W_qkv = jax.random.normal(k2, (IN_DIM, 3 * H * D), dtype=jnp.float32) * IN_DIM ** (-0.5)
        W_out = jax.random.normal(k3, (H * D, OUT_DIM), dtype=jnp.float32) * (H * D) ** (-0.5)
        return {'inputs': inputs, 'W_qkv': W_qkv, 'W_out': W_out}
    _L0_attn_all = _L0_attn_setup()
    _L0_attn_in = {k: v for k, v in _L0_attn_all.items() if k in ('W_qkv', 'W_out')}
    del _L0_attn_all

    def _L0_ffn_setup():
        import jax, jax.numpy as jnp
        import numpy as np
        DIM = 256
        HIDDEN = 1024
        E = 8
        B, S = (2, 1024)
        key = jax.random.key(seed)
        ks = jax.random.split(key, 8)
        sd = 1.0 / np.sqrt(DIM)
        sh = 1.0 / np.sqrt(HIDDEN)
        return {'x': jax.random.normal(ks[0], (B, S, DIM), dtype=jnp.float32), 'router_w': jax.random.uniform(ks[1], (DIM, E), jnp.float32, -sd, sd), 'router_b': jax.random.uniform(ks[2], (E,), jnp.float32, -sd, sd), 'w1': jax.random.uniform(ks[3], (E, DIM, 2 * HIDDEN), jnp.float32, -sd, sd), 'b1': jax.random.uniform(ks[4], (E, 2 * HIDDEN), jnp.float32, -sd, sd), 'w2': jax.random.uniform(ks[5], (E, HIDDEN, DIM), jnp.float32, -sh, sh), 'b2': jax.random.uniform(ks[6], (E, DIM), jnp.float32, -sh, sh)}
    _L0_ffn_all = _L0_ffn_setup()
    _L0_ffn_in = {k: v for k, v in _L0_ffn_all.items() if k in ('router_w', 'router_b', 'w1', 'b1', 'w2', 'b2')}
    del _L0_ffn_all
    return {'x': x, 'L0_tok_conv_w': _L0_tok_in['conv_w'], 'L0_tok_conv_b': _L0_tok_in['conv_b'], 'L0_tok_ln_gamma': _L0_tok_in['ln_gamma'], 'L0_tok_ln_beta': _L0_tok_in['ln_beta'], 'L0_attn_W_qkv': _L0_attn_in['W_qkv'], 'L0_attn_W_out': _L0_attn_in['W_out'], 'L0_ffn_router_w': _L0_ffn_in['router_w'], 'L0_ffn_router_b': _L0_ffn_in['router_b'], 'L0_ffn_w1': _L0_ffn_in['w1'], 'L0_ffn_b1': _L0_ffn_in['b1'], 'L0_ffn_w2': _L0_ffn_in['w2'], 'L0_ffn_b2': _L0_ffn_in['b2']}

def reference(x, L0_tok_conv_w, L0_tok_conv_b, L0_tok_ln_gamma, L0_tok_ln_beta, L0_attn_W_qkv, L0_attn_W_out, L0_ffn_router_w, L0_ffn_router_b, L0_ffn_w1, L0_ffn_b1, L0_ffn_w2, L0_ffn_b2):
    import jax
    import jax.numpy as jnp

    def _L0_tok_ref(hidden_states, conv_w, conv_b, ln_gamma, ln_beta):
        import jax, jax.numpy as jnp
        import numpy as np
        D_MODEL = 256
        STRIDE = 2
        KERNEL = 2
        INIT_STD = 0.02
        EPS = 1e-05
        B, L, D = hidden_states.shape
        pad_len = -L % STRIDE
        if pad_len:
            hidden_states = jnp.pad(hidden_states, ((0, 0), (0, pad_len), (0, 0)))
            L = L + pad_len
        xb = hidden_states.reshape(B, L // STRIDE, STRIDE, D)
        x = jnp.einsum('btki,oik->bto', xb, conv_w) + conv_b
        x = x + xb.mean(axis=2)
        mu = x.mean(axis=-1, keepdims=True)
        var = jnp.mean(jnp.square(x - mu), axis=-1, keepdims=True)
        x = (x - mu) * jax.lax.rsqrt(var + EPS) * ln_gamma + ln_beta
        return x

    def _L0_attn_ref(inputs, W_qkv, W_out):
        import jax, jax.numpy as jnp
        import numpy as np
        B, L, IN_DIM = (4, 512, 256)
        H, D = (16, 64)
        OUT_DIM = 256
        b, l, _ = inputs.shape
        qkv = inputs @ W_qkv
        q, k, v = jnp.split(qkv, 3, axis=-1)
        q = q.reshape(b, l, H, D)
        k = k.reshape(b, l, H, D)
        v = v.reshape(b, l, H, D)
        score = jnp.einsum('bihd,bjhd->bijh', q, k) / D ** 0.5
        mask = jnp.tril(jnp.ones((l, l), dtype=score.dtype))[None, :, :, None]
        masked_score = score * mask + 1e+30 * (mask - 1.0)
        wmat = jax.nn.softmax(masked_score, axis=2)
        out = jnp.einsum('bijh,bjhd->bihd', wmat, v).reshape(b, l, H * D)
        return out @ W_out

    def _L0_ffn_ref(x, router_w, router_b, w1, b1, w2, b2):
        import jax, jax.numpy as jnp
        import numpy as np
        DIM = 256
        HIDDEN = 1024
        E = 8
        B, S = (2, 1024)
        logits = jnp.einsum('bsd,de->bse', x, router_w) + router_b
        probs = jax.nn.softmax(logits, axis=-1)
        top1 = jnp.argmax(probs, axis=-1)
        out = jnp.zeros_like(x)
        for i in range(E):
            h = jnp.einsum('bsd,df->bsf', x, w1[i]) + b1[i]
            a, g = jnp.split(h, 2, axis=-1)
            y = jnp.einsum('bsh,hd->bsd', a * jax.nn.sigmoid(g), w2[i]) + b2[i]
            out = out + jnp.where((top1 == i)[..., None], y, 0.0)
        return out
    h = _L0_tok_ref(x, L0_tok_conv_w, L0_tok_conv_b, L0_tok_ln_gamma, L0_tok_ln_beta)
    h = h + _L0_attn_ref(_layernorm(h, axis=-1), L0_attn_W_qkv, L0_attn_W_out)
    h = h + _L0_ffn_ref(_layernorm(h, axis=-1), L0_ffn_router_w, L0_ffn_router_b, L0_ffn_w1, L0_ffn_b1, L0_ffn_w2, L0_ffn_b2)
    return h

_drawn_inputs = setup_inputs


def setup_inputs(seed=0):
    import zlib

    import numpy as np

    out = dict(_drawn_inputs(seed))
    spreads = {'L0_tok_conv_b': (0.0, 0.1), 'L0_tok_ln_gamma': (1.0, 0.2), 'L0_tok_ln_beta': (0.0, 0.1)}
    factors = {'L0_ffn_b1': 5.639, 'L0_ffn_b2': 3.364}
    for name, (base, spread) in spreads.items():
        noise = np.random.default_rng([zlib.crc32(name.encode()), seed]).standard_normal(out[name].shape)
        drawn = base * np.exp(spread * noise) if base else spread * noise
        out[name] = jnp.asarray(drawn.astype(out[name].dtype))
    for name, factor in factors.items():
        out[name] = (out[name] * factor).astype(out[name].dtype)
    return out
```

```python
from contextlib import ExitStack

import concourse.bass as bass
from concourse import mybir
from concourse.alu_op_type import AluOpType as ALU

ACT = mybir.ActivationFunctionType
AX = mybir.AxisListType
F32 = mybir.dt.float32
F32R = mybir.dt.float32r
BF16 = mybir.dt.bfloat16
I32 = mybir.dt.int32
U32 = mybir.dt.uint32

B, L, D = 8, 375, 256
T = B * L
TP, NT = 125, 3
LP = L + 1
H, HD = 16, 64
NP = H // 2
NG = NP // 2
HID = 1024
E = 8
SLOT = 128
STRIDE = T + SLOT
N_SLOTS = (T + E * (SLOT - 1)) // SLOT
MIN_SLOTS = -(-T // SLOT)
SPARE = N_SLOTS - MIN_SLOTS
ROWS = E * STRIDE + SPARE * SLOT
ROW = 516
NO_TOKEN = 2 * T
EPS = 1e-5
MASKED = -1e30

W1C = 2 * 2 * HID
WCOLS = W1C + HID // 128 * D

UNITS = [
    [[("q", 1, 0)], [("k", 1, 0)], [("q", 2, 0), ("v", (0, 2), 0)], [("k", 2, 0)]],
    [[], [("wout", 0, -1)], [("wout", 1, -1)], [("wout", 2, -1)]],
    [[("q", 3, 0)], [("conv", 0, 1)], [("k", 3, 0)], [("conv", 1, 1)]],
    [[("conv", 2, 1)], [("q", 4, 0), ("v", (1, 0), 0)], [("k", 4, 0), ("v", (1, 1), 0)], [("v", (1, 2), 0)]],
    [[("q", 5, 0)], [("nT2", 0, -1), ("v", (2, 0), 0), ("nT2", 1, -1)], [("k", 5, 0), ("nT2", 2, -1)],
     [("v", (2, 1), 0)]],
    [[("q", 6, 0)], [("v", (2, 2), 0), ("logits", 0, -1)], [("k", 6, 0)], [("v", (3, 0), 0)]],
    [[("q", 7, 0)], [("k", 7, 0)], [("v", (3, 1), 0), ("v", (3, 2), 0)], [("nT", 0, 1), ("nT", 1, 1)]],
    [[("nT", 2, 1)], [("rank", 0, -1)], [("q", 0, 1), ("v", (0, 0), 1)], [("k", 0, 1), ("v", (0, 1), 1)]],
]
ORDER = [u for pair in UNITS for place in pair for u in place]
PER_BATCH = {"q": NP, "k": NP, "v": NG * NT, "wout": NT, "nT2": NT, "conv": NT, "nT": NT,
             "logits": 1, "rank": 1}
N_AUX = 3


def event(kind, index):
    return index[0] * NT + index[1] if kind == "v" else index


def tower(nc, xT, x, conv_w, conv_b, gamma, beta, w_qkv, w_out, router_w, router_b,
          w1, b1, w2, b2, out):
    ctx = ExitStack()
    with ctx:
        rows = nc.dram_tensor("token_rows", [ROWS, ROW], F32)
        rows = rows.ap()

        cursor = [nc.sbuf_base + (-nc.sbuf_base) % 64]

        def at_offset(name, shape, dt, offset):
            return nc.alloc_sbuf_tensor_at(name, shape, dt, offset=offset)

        def size(shape, dt):
            n = 2 if dt == BF16 else 4
            for s in shape[1:]:
                n *= s
            return n + (-n) % 32

        def sb(name, shape, dt=F32):
            o = cursor[0]
            cursor[0] += size(shape, dt)
            return at_offset(name, shape, dt, o)

        def bank(name):
            return ctx.enter_context(nc.psum_tensor(name, [128, 512], F32))

        def sem(name):
            return ctx.enter_context(nc.semaphore(name))

        ident = sb("ident", [128, 128])
        endw = sb("endw", [1, E], I32)
        table = sb("table", [1, 4, 32], I32)
        padrow = sb("padrow", [1, E], I32)
        phase_start = cursor[0]

        wq_hi = sb("wq_hi", [128, 2, 3 * H * HD], F32R)
        wq_lo = sb("wq_lo", [128, 2, 3 * H * HD], F32R)
        ffn_start = cursor[0]
        wo_hi = sb("wo_hi", [128, NP, D], F32R)
        wo_lo = sb("wo_lo", [128, NP, D], F32R)
        xT_in = sb("xT_in", [128, 4, L])
        x_in = sb("x_in", [TP, NT, 2 * D])
        wc = sb("wc", [128, 4, D])
        rw = sb("rw", [128, 2, E])
        bias2 = sb("bias2", [128, D])
        gam = sb("gam", [128, D])
        bet = sb("bet", [128, D])
        rb = sb("rb", [128, E])
        mask = sb("mask", [128, L])
        tri = sb("tri", [128, 128], BF16)
        ones = sb("ones", [128, 128], BF16)
        rev = sb("rev", [128, E])
        token_of = sb("token_of", [128, NT])
        halfs = sb("halfs", [128, NT])
        xsum = sb("xsum", [TP, NT, D])
        u = sb("u", [TP, NT, D])
        z = sb("z", [TP, NT, D])
        h1 = sb("h1", [TP, 2 * NT * D])
        n1 = sb("n1", [TP, NT, D])
        nT_hi = sb("nT_hi", [128, 2, LP], F32R)
        nT_lo = sb("nT_lo", [128, 2, LP], F32R)
        qz = sb("qz", [128, 4, 2, LP])
        kk = sb("kk", [128, 4, LP])
        vv = sb("vv", [TP, 2, NT, D])
        probs = sb("probs", [TP, 4, 2 * L])
        probsT = sb("probsT", [TP, 2, 2 * L])
        n2T = sb("n2T", [128, 2, L])
        small_start = cursor[0]
        rowbuf = sb("rowbuf", [TP, NT, ROW])
        cnt = sb("cnt", [128, E])
        eoff = sb("eoff", [128, E])
        iot = sb("iot", [128, 64], I32)
        st6 = sb("st6", [TP, 3, NT, 6])
        mv = sb("mv", [TP, 3, NT, 2])
        veps = sb("veps", [TP, 3, NT])
        rstd = sb("rstd", [TP, 3, NT])
        rmax = sb("rmax", [TP, 4, NT])
        nmax = sb("nmax", [TP, 4, NT])
        rsum = sb("rsum", [TP, 4, NT])
        rinv = sb("rinv", [TP, 4, NT])
        lg = sb("lg", [TP, NT, E])
        r1 = sb("r1", [TP, NT, E])
        r2 = sb("r2", [TP, NT, E])
        rm = sb("rm", [TP, 4, NT])
        onehot = sb("onehot", [TP, NT, E], BF16)
        pos = sb("pos", [TP, NT], U32)
        cnt_new = sb("cnt_new", [128, E])
        tb = sb("tb", [1, 4, 64])
        tbi = sb("tbi", [1, 2, 64], I32)
        slotf = sb("slotf", [1, N_SLOTS])
        reached = sb("reached", [1, N_SLOTS, E])
        jump = sb("jump", [1, N_SLOTS, E])
        attn_start = cursor[0]
        aT_hi = sb("aT_hi", [128, NP, L], F32R)
        aT_lo = sb("aT_lo", [128, NP, L], F32R)
        assert cursor[0] <= nc.sbuf_usable_end, cursor[0]
        cursor[0] = attn_start
        wq_raw = sb("wq_raw", [128, 2, 3 * H * HD])
        wo_raw = sb("wo_raw", [128, NP, D])
        pad = sb("pad", [128, ROW])
        assert cursor[0] <= nc.sbuf_usable_end, (cursor[0], nc.sbuf_usable_end)

        cursor[0] = phase_start
        ew = sb("ew", [128, 2 * WCOLS])
        cursor[0] = ffn_start
        eb1 = sb("eb1", [128, 2 * 2 * HID])
        eb2 = sb("eb2", [128, 2 * D])
        xs = sb("xs", [128, D])
        hs = sb("hs", [128, D + 4])
        xsT = sb("xsT", [128, 2, 128])
        gs = sb("gs", [128, 2, 512])
        sg = sb("sg", [128, 2, 512])
        as_ = sb("as_", [128, 2, 512])
        act = sb("act", [128, 2, 512])
        actT = sb("actT", [128, 2, 512])
        ys = sb("ys", [128, D])
        yo = sb("yo", [128, D])
        ids = sb("ids", [128, 1], U32)
        pad2 = sb("pad2", [128, ROW])
        assert cursor[0] <= small_start, (cursor[0], small_start)

        sA, sB, tA, tB, pv = (bank(n) for n in ("sA", "sB", "tA", "tB", "pv"))
        aux = [bank(f"aux{i}") for i in range(N_AUX)]
        up_bank = [sA, sB, aux[1], aux[2]]
        y_bank = aux[0]

        score_cols = {0: (0, TP), 2: (TP, 3 * TP), 1: (4 * TP, 2 * TP)}
        score_bank = {0: (sA, 0), 2: (sA, TP), 1: (sB, 0)}

        xT_landed, x_landed = sem("xT_landed"), sem("x_landed")
        wc_landed, consts_landed = sem("wc_landed"), sem("consts_landed")
        wq_landed, wo_landed = sem("wq_landed"), sem("wo_landed")
        pool_const, dve_const = sem("pool_const"), sem("dve_const")
        w_hi_made, w_lo_made = sem("w_hi_made"), sem("w_lo_made")
        xsum_step = sem("xsum_step")
        pe_done = {k: sem(f"pe_{k}") for k in PER_BATCH}
        q_taken_act, q_taken_dve = sem("q_taken_act"), sem("q_taken_dve")
        k_taken, v_taken = sem("k_taken"), sem("v_taken")
        nT_hi_taken, nT_lo_taken = sem("nT_hi_taken"), sem("nT_lo_taken")
        conv_taken, wout_taken, nT2_taken = sem("conv_taken"), sem("wout_taken"), sem("nT2_taken")
        logits_taken, rank_taken = sem("logits_taken"), sem("rank_taken")
        stats_made, veps_made, rstd_made = sem("stats_made"), sem("veps_made"), sem("rstd_made")
        normed = sem("normed")
        affine = sem("affine")
        scores_done, masked, nmax_made = sem("scores_done"), sem("masked"), sem("nmax_made")
        exp_done, rinv_made, probs_ready = sem("exp_done"), sem("rinv_made"), sem("probs_ready")
        probsT_done, probsT_act, probsT_dve = sem("probsT_done"), sem("probsT_act"), sem("probsT_dve")
        pv_done, aT_hi_made, aT_lo_made = sem("pv_done"), sem("aT_hi_made"), sem("aT_lo_made")
        route_step = sem("route_step")
        onehot_made, pos_made, cnt_made = sem("onehot_made"), sem("pos_made"), sem("cnt_made")
        place_step = sem("place_step")
        waits_passed = sem("waits_passed")
        stats_out, veps_out, rstd_out, normed_out = (sem(n) for n in ("stats_out", "veps_out", "rstd_out", "normed_out"))
        aggr_made = [sem(f"aggr_made{i}") for i in range(3)]
        rows_sent, pads_sent = sem("rows_sent"), sem("pads_sent")
        table_step, table_made = sem("table_step"), sem("table_made")
        slots_done, weights_landed, weights_ready = sem("slots_done"), sem("weights_landed"), sem("weights_ready")
        out_sent = sem("out_sent")
        xs_landed, hs_landed = sem("xs_landed"), sem("hs_landed")
        pe_xsT, xsT_taken = sem("pe_xsT"), sem("xsT_taken")
        pe_up, g_added, a_added = sem("pe_up"), sem("g_added"), sem("a_added")
        gated, act_ready = sem("gated"), sem("act_ready")
        pe_actT, actT_taken = sem("pe_actT"), sem("actT_taken")
        pe_y, y_biased, y_ready = sem("pe_y"), sem("y_biased"), sem("y_ready")


        taken = {
            "q": [q_taken_act, q_taken_dve], "k": [k_taken], "v": [v_taken], "wout": [wout_taken],
            "nT2": [nT2_taken], "conv": [conv_taken], "nT": [nT_lo_taken],
            "logits": [logits_taken], "rank": [rank_taken],
        }

        def nth(batch, per, k):
            return batch * per + (k + 1)

        def count_of(kind, index, batch):
            return nth(batch, PER_BATCH[kind], event(kind, index))

        def bank_of(unit):
            return aux[ORDER.index(unit) % N_AUX]

        def before(p, b, n):
            return (p - n, b, 0) if p >= n else (NP + p - n, b - 1, -1)

        def units_of(place, rels):
            return [u_ for u_ in place if u_[2] in rels]

        def phase_one(engine, emit):
            emit(-1, (1,))
            emit(0, (0, 1))
            with engine.Fori(1, B - 1) as b:
                emit(b, (-1, 0, 1))
            emit(B - 1, (-1, 0))
            emit(B, (-1,))

        N_CONST = 10

        def stand_alone(engine):
            engine.sem_inc(waits_passed, 1)

        block = ctx.enter_context(nc.Block())

        @block.sync
        def _(sp):
            def load_x(b, first):
                src_T = xT[:, :, 0:L] if first else xT[:, :, bass.ds(b * L, L)]
                src = x[0] if first else x[bass.ds(b, 1)].rearrange("a t p d -> (a t) p d")
                sp.dma_start(xT_in[:, :, :], src_T).then_inc(xT_landed, 16)
                sp.dma_start(x_in[:, :, :], src.rearrange("t p d -> p t d")).then_inc(x_landed, 16)

            load_x(0, True)
            sp.dma_start(wc[:, :, :], conv_w).then_inc(wc_landed, 16)
            for dst, src, n in ((bias2, conv_b, D), (gam, gamma, D), (bet, beta, D), (rb, router_b, E)):
                sp.dma_start(dst[:, 0:n], src.partition_broadcast(128)).then_inc(consts_landed, 16)
            sp.dma_start(rw[:, :, :], router_w.rearrange("(c p) e -> p c e", p=128)).then_inc(consts_landed, 16)
            sp.dma_start(wq_raw[:, :, :], w_qkv.rearrange("(c p) n -> p c n", p=128)).then_inc(wq_landed, 16)
            sp.dma_start(wo_raw[:, :, :], w_out.rearrange("(c p) n -> p c n", p=128)).then_inc(wo_landed, 16)
            with sp.Fori(1, B) as b:
                sp.wait_ge(pe_done["conv"], b * NT)
                sp.wait_ge(xsum_step, b * 3)
                load_x(b, False)
            sp.wait_ge(table_made, 1)
            sp.wait_ge(rows_sent, (B * NT + SPARE) * 16)
            for e in range(E):
                r = sp.value_load(padrow[0:1, e:e + 1], min_val=e * STRIDE, max_val=e * STRIDE + T)
                sp.dma_start(rows[bass.ds(r, SLOT), :], pad2[:, :]).then_inc(pads_sent, 16)
            for e in range(E):
                if e >= 2:
                    done = sp.value_load(endw[0:1, e - 2:e - 1], min_val=1, max_val=N_SLOTS + 1)
                    sp.wait_ge(slots_done, done)
                o = (e % 2) * WCOLS
                sp.dma_start(ew[:, o:o + W1C].rearrange("p (c n) -> p c n", c=2),
                             w1[e].rearrange("(c p) n -> p c n", p=128)).then_inc(weights_landed, 16)
                sp.dma_start(ew[:, o + W1C:o + WCOLS].rearrange("p (c n) -> p c n", c=HID // 128),
                             w2[e].rearrange("(c p) n -> p c n", p=128)).then_inc(weights_landed, 16)
                sp.dma_start(eb1[:, (e % 2) * 2 * HID:(e % 2 + 1) * 2 * HID],
                             b1[e].partition_broadcast(128)).then_inc(weights_landed, 16)
                sp.dma_start(eb2[:, (e % 2) * D:(e % 2 + 1) * D],
                             b2[e].partition_broadcast(128)).then_inc(weights_landed, 16)
                sp.wait_ge(weights_landed, 64 * (e + 1))
                sp.sem_inc(weights_ready, 1)
            sp.wait_ge(out_sent, 16 * N_SLOTS)

        @block.gpsimd
        def _(pool):
            pool.memset(ident[:, :], 0.0).then_inc(pool_const, 1)
            pool.memset(mask[:, :], 0.0).then_inc(pool_const, 1)
            pool.memset(tri[:, :], 1.0).then_inc(pool_const, 1)
            pool.iota(iot[:, 0:NT], pattern=[[TP, NT]], base=0, channel_multiplier=1).then_inc(pool_const, 1)
            pool.iota(iot[:, 8:8 + E], pattern=[[-1, E]], base=E, channel_multiplier=0).then_inc(pool_const, 1)
            pool.iota(iot[:, 16:16 + E], pattern=[[STRIDE, E]], base=0, channel_multiplier=0).then_inc(pool_const, 1)
            pool.iota(iot[:, 32:63], pattern=[[1, 31]], base=0, channel_multiplier=0).then_inc(pool_const, 1)
            pool.wait_ge(pool_const, 7)
            pool.affine_select(out=ident[:, :], in_=ident[:, :], compare_op=ALU.not_equal, fill=1.0,
                               base=0, pattern=[[-1, 128]], channel_multiplier=1).then_inc(pool_const, 1)
            pool.affine_select(out=mask[:, 2 * TP:], in_=mask[:, 2 * TP:], compare_op=ALU.is_ge, fill=MASKED,
                               base=0, pattern=[[-1, TP]], channel_multiplier=1).then_inc(pool_const, 1)
            pool.affine_select(out=tri[:, :], in_=tri[:, :], compare_op=ALU.is_gt, fill=0.0,
                               base=0, pattern=[[1, 128]], channel_multiplier=-1).then_inc(pool_const, 1)

            def emit(b, rels):
                if 1 in rels:
                    pool.wait_ge(x_landed, nth(b + 1, 1, 0) * 16)
                    if not (isinstance(b, int) and b < 0):
                        pool.wait_ge(conv_taken, nth(b, NT, NT - 1))
                    pool.tensor_tensor(xsum[:, :, :], x_in[:, :, 0:D], x_in[:, :, D:], ALU.add).then_inc(xsum_step, 1)
                    pool.wait_ge(xsum_step, nth(b + 1, 3, 0))
                    pool.tensor_tensor(xsum[:, :, :], xsum[:, :, :],
                                       bias2[0:TP, :].unsqueeze(1).to_broadcast([TP, NT, D]), ALU.add)\
                        .then_inc(xsum_step, 1)
                    pool.wait_ge(xsum_step, nth(b + 1, 3, 1))
                    pool.tensor_tensor(xsum[:, :, :], xsum[:, :, :],
                                       bias2[0:TP, :].unsqueeze(1).to_broadcast([TP, NT, D]), ALU.add)\
                        .then_inc(xsum_step, 1)
                if -1 in rels:
                    pool.wait_ge(veps_out, nth(b - 1, 1, 0))
                    pool.tensor_tensor(rstd[:, 2, :], veps[:, 2, :], halfs[0:TP, :], ALU.pow).then_inc(rstd_out, 1)
                if 1 in rels:
                    pool.wait_ge(veps_made, nth(b + 1, 2, 0))
                    pool.tensor_tensor(rstd[:, 0, :], veps[:, 0, :], halfs[0:TP, :], ALU.pow).then_inc(rstd_made, 1)
                    pool.wait_ge(normed, nth(b + 1, 2, 0))
                    pool.tensor_tensor(z[:, :, :], z[:, :, :],
                                       gam[0:TP, :].unsqueeze(1).to_broadcast([TP, NT, D]), ALU.mult)\
                        .then_inc(affine, 1)
                    pool.wait_ge(affine, nth(b + 1, 2, 0))
                    o = ((b + 1) % 2) * (NT * D)
                    pool.tensor_tensor(h1[:, bass.ds(o, NT * D)].rearrange("p (t d) -> p t d", t=NT), z[:, :, :],
                                       bet[0:TP, :].unsqueeze(1).to_broadcast([TP, NT, D]), ALU.add)\
                        .then_inc(affine, 1)
                    pool.wait_ge(veps_made, nth(b + 1, 2, 1))
                    pool.tensor_tensor(rstd[:, 1, :], veps[:, 1, :], halfs[0:TP, :], ALU.pow).then_inc(rstd_made, 1)
                if -1 in rels:
                    pool.wait_ge(pos_made, nth(b - 1, 1, 0))
                    stand_alone(pool)
                    for t in range(NT):
                        pool.indirect_dma_start(rows, bass.IndirectOffsetOnAxis(pos[:, t:t + 1], 0),
                                                rowbuf[:, t, :], None).then_inc(rows_sent, 16)

            pool.wait_ge(dve_const, 3)
            for s in range(SPARE):
                r = E * STRIDE + s * SLOT
                pool.dma_start(rows[r:r + SLOT, :], pad[:, :]).then_inc(rows_sent, 16)
            pool.wait_ge(consts_landed, 80)
            phase_one(pool, emit)

            with pool.Fori(0, N_SLOTS) as s:
                pool.wait_ge(y_ready, s + 1)
                stand_alone(pool)
                pool.indirect_dma_start(out, bass.IndirectOffsetOnAxis(ids[:, 0:1], 0), yo[:, :], None,
                                        bounds_check=T - 1, oob_is_err=False).then_inc(out_sent, 16)

        @block.scalar
        def _(ac):
            def copy(dst, src):
                return nc.scalar.activation(dst, src, ACT.Copy)

            ac.wait_ge(wq_landed, 16)
            for c in range(2):
                for i in range(3):
                    cols = slice(i * H * HD, (i + 1) * H * HD)
                    copy(wq_hi[:, c, cols], wq_raw[:, c, cols]).then_inc(w_hi_made, 1)

            def take(unit, b):
                kind, index, rel = unit
                src = bank_of(unit)
                if kind in ("conv", "wout", "logits", "rank"):
                    return
                ac.wait_ge(pe_done[kind], count_of(kind, index, b + rel))
                if kind == "q":
                    copy(qz[0:HD, index % 4, 0, :], src[0:HD, 0:LP]).then_inc(q_taken_act, 1)
                elif kind == "k":
                    copy(kk[:, index % 4, :], src[:, 0:LP]).then_inc(k_taken, 1)
                elif kind == "v":
                    copy(vv[:, index[0] % 2, index[1], :], src[0:TP, 0:D]).then_inc(v_taken, 1)
                elif kind == "nT":
                    copy(nT_hi[:, :, index * TP:(index + 1) * TP],
                         src[:, 0:2 * TP].rearrange("p (c t) -> p c t", c=2)).then_inc(nT_hi_taken, 1)
                elif kind == "nT2":
                    copy(n2T[:, :, index * TP:(index + 1) * TP],
                         src[:, 0:2 * TP].rearrange("p (c t) -> p c t", c=2)).then_inc(nT2_taken, 1)

            def exps(h, b):
                ac.wait_ge(nmax_made, nth(b, H, h))
                for t in range(NT):
                    o, n = score_cols[t]
                    s = probs[:, h % 4, o:o + n]
                    last = nc.scalar.activation(s, s, ACT.Exp, bias=nmax[:, h % 4, t:t + 1], scale=HD ** -0.5,
                                                accum_out=rsum[:, h % 4, t:t + 1])
                last.then_inc(exp_done, 1)

            def probs_T(h, b):
                ac.wait_ge(probsT_done, nth(b, H, h))
                copy(probsT[:, h % 2, 0:L], tA[0:TP, 0:L]).then_inc(probsT_act, 1)

            def emit(b, rels):
                for p in range(NP):
                    pp, pb, prel = before(p, b, 1)
                    vp, vb, vrel = before(p, b, 2)
                    places = UNITS[p]
                    if vrel in rels:
                        ac.wait_ge(pv_done, nth(vb, NP, vp))
                        copy(aT_hi[:, vp, :], pv[:, 0:L]).then_inc(aT_hi_made, 1)
                    for un in units_of(places[0], rels):
                        take(un, b)
                    if 0 in rels:
                        exps(2 * p, b)
                    if prel in rels:
                        probs_T(2 * pp, pb)
                    for un in units_of(places[1], rels):
                        take(un, b)
                    for un in units_of(places[2], rels):
                        take(un, b)
                    if 0 in rels:
                        exps(2 * p + 1, b)
                    if prel in rels:
                        probs_T(2 * pp + 1, pb)
                    for un in units_of(places[3], rels):
                        take(un, b)
                if 0 not in rels and 1 in rels:
                    ac.wait_ge(wo_landed, 16)
                    copy(wo_hi[:, :, :], wo_raw[:, :, :]).then_inc(w_hi_made, 1)

            phase_one(ac, emit)

            def load_xs(s):
                row = ac.value_load(table[0:1, 3, bass.ds(s, 1)], min_val=0, max_val=ROWS - SLOT)
                ac.dma_start(xs[:, :], rows[bass.ds(row, SLOT), 0:D]).then_inc(xs_landed, 16)

            def load_hs(s):
                row = ac.value_load(table[0:1, 3, bass.ds(s, 1)], min_val=0, max_val=ROWS - SLOT)
                ac.dma_start(hs[:, :], rows[bass.ds(row, SLOT), D:2 * D + 4]).then_inc(hs_landed, 16)

            def gate(s, j):
                ac.wait_ge(g_added, 2 * s + j + 1)
                nc.scalar.activation(sg[:, j, :], gs[:, j, :], ACT.Sigmoid).then_inc(gated, 1)

            def take_actT(s, j):
                ac.wait_ge(pe_actT, 2 * s + j + 1)
                copy(actT[:, j, :], (tA, tB)[j][:, :]).then_inc(actT_taken, 1)

            def take_xsT(s):
                ac.wait_ge(pe_xsT, s + 1)
                copy(xsT[:, :, :], pv[:, 0:256].rearrange("p (c t) -> p c t", c=2)).then_inc(xsT_taken, 1)

            ac.wait_ge(table_made, 1)
            ac.wait_ge(rows_sent, (B * NT + SPARE) * 16)
            ac.wait_ge(pads_sent, E * 16)
            load_xs(0)
            take_xsT(0)

            def slot(s, prev, cur, nxt):
                if nxt:
                    load_xs(s + 1)
                if prev:
                    if not (isinstance(s, int) and s < 2):
                        ac.wait_ge(y_ready, s - 1)
                    load_hs(s - 1)
                if cur:
                    gate(s, 0)
                if prev:
                    take_actT(s - 1, 1)
                if cur:
                    gate(s, 1)
                if nxt:
                    take_xsT(s + 1)
                if cur:
                    take_actT(s, 0)

            slot(0, False, True, True)
            slot(1, True, True, True)
            with ac.Fori(2, N_SLOTS - 1) as s:
                slot(s, True, True, True)
            slot(N_SLOTS - 1, True, True, False)
            slot(N_SLOTS, True, False, False)

        @block.vector
        def _(ve):
            V = nc.vector
            V.memset(pad[:, :], 0.0).then_inc(dve_const, 1)
            V.memset(halfs[:, :], -0.5).then_inc(dve_const, 1)
            ve.wait_ge(dve_const, 2)
            V.memset(pad[:, 2 * D:2 * D + 1].bitcast(I32), NO_TOKEN).then_inc(dve_const, 1)
            V.memset(ones[:, :], 1.0)
            V.memset(qz[HD:, :, 0, :], 0.0)
            V.memset(qz[0:HD, :, 1, :], 0.0)
            V.memset(nT_hi[:, :, L:LP].bitcast(F32), 0.0)
            V.memset(nT_lo[:, :, L:LP].bitcast(F32), 0.0)
            V.memset(rowbuf[:, :, 2 * D:], 0.0)
            ve.wait_ge(pool_const, 7)
            V.tensor_copy(token_of[:, :], iot[:, 0:NT])
            V.tensor_copy(rev[:, :], iot[:, 8:8 + E])
            V.tensor_copy(eoff[:, :], iot[:, 16:16 + E])
            V.tensor_copy(cnt[:, :], iot[:, 16:16 + E])
            V.memset(rsum[:, :, :], 0.0).then_inc(dve_const, 1)

            def low_halves(chunks):
                for n in chunks:
                    c, i = divmod(n, 3)
                    cols = slice(i * H * HD, (i + 1) * H * HD)
                    ve.wait_ge(w_hi_made, n + 1)
                    V.tensor_tensor(wq_lo[:, c, cols], wq_raw[:, c, cols], wq_hi[:, c, cols].bitcast(F32),
                                    ALU.subtract).then_inc(w_lo_made, 1)

            def take(unit, b):
                kind, index, rel = unit
                src = bank_of(unit)
                if kind in ("k", "v", "nT2"):
                    return
                bb = b + rel
                ve.wait_ge(pe_done[kind], count_of(kind, index, bb))
                if kind == "q":
                    V.tensor_copy(qz[HD:, index % 4, 1, :], src[HD:, 0:LP]).then_inc(q_taken_dve, 1)
                elif kind == "nT":
                    cols = slice(index * TP, (index + 1) * TP)
                    ve.wait_ge(nT_hi_taken, count_of(kind, index, bb))
                    V.tensor_tensor(nT_lo[:, :, cols], src[:, 0:2 * TP].rearrange("p (c t) -> p c t", c=2),
                                    nT_hi[:, :, cols].bitcast(F32), ALU.subtract).then_inc(nT_lo_taken, 1)
                elif kind == "conv":
                    ve.wait_ge(xsum_step, nth(bb, 3, 2))
                    V.scalar_tensor_tensor(out=u[:, index, :], in0=xsum[:, index, :], scalar=0.5,
                                           in1=src[0:TP, 0:D], op0=ALU.mult, op1=ALU.add).then_inc(conv_taken, 1)
                    ve.wait_ge(conv_taken, nth(bb, NT, index))
                    V.bn_stats(st6[:, 0, index, :], u[:, index, :]).then_inc(stats_made, 1)
                    if index == NT - 1:
                        norm_stats(0, bb, stats_made, nth(bb, 2 * NT, NT - 1), veps_made)
                elif kind == "wout":
                    if index == 0:
                        ve.wait_ge(rows_sent, bb * (NT * 16) + SPARE * 16)
                    o = (bb % 2) * (NT * D) + index * D
                    V.tensor_tensor(rowbuf[:, index, D:2 * D], src[0:TP, 0:D], h1[:, bass.ds(o, D)], ALU.add)\
                        .then_inc(wout_taken, 1)
                    ve.wait_ge(wout_taken, nth(bb, NT, index))
                    V.bn_stats(st6[:, 2, index, :], rowbuf[:, index, D:2 * D]).then_inc(stats_out, 1)
                    if index == NT - 1:
                        norm_stats(2, bb, stats_out, nth(bb, NT, NT - 1), veps_out)
                elif kind == "logits":
                    V.tensor_tensor(lg[:, :, :], src[0:TP, 0:NT * E].rearrange("p (t e) -> p t e", t=NT),
                                    rb[0:TP, :].unsqueeze(1).to_broadcast([TP, NT, E]), ALU.add)\
                        .then_inc(logits_taken, 1)
                    choose(bb)
                elif kind == "rank":
                    place_rows(src, bb)

            def norm_stats(which, batch, stats, n, made):
                ve.wait_ge(stats, n)
                stand_alone(ve)
                for t in range(NT):
                    V.bn_aggr(mv[:, which, t, :], st6[:, which, t, :]).then_inc(aggr_made[which], 1)
                ve.wait_ge(aggr_made[which], nth(batch, NT, NT - 1))
                V.tensor_scalar(veps[:, which, :], mv[:, which, :, 1], EPS, None, ALU.add).then_inc(made, 1)

            def normalise(dst, src, which):
                for t in range(NT):
                    last = V.tensor_scalar(dst[:, t, 0:D], src(t), mv[:, which, t, 0:1], rstd[:, which, t:t + 1],
                                           ALU.subtract, ALU.mult)
                return last

            def choose(bb):
                def link(ins, k):
                    ins.then_inc(route_step, 1)
                    ve.wait_ge(route_step, nth(bb, 4, k))
                ve.wait_ge(logits_taken, nth(bb, 1, 0))
                link(V.tensor_reduce(rm[:, 0, :], lg[:, :, :], AX.X, ALU.max), 0)
                link(V.tensor_tensor(r1[:, :, :], lg[:, :, :], rm[:, 0, :].unsqueeze(2).to_broadcast([TP, NT, E]),
                                     ALU.is_equal), 1)
                revb = rev[0:TP, :].unsqueeze(1).to_broadcast([TP, NT, E])
                link(V.tensor_tensor(r2[:, :, :], r1[:, :, :], revb, ALU.mult), 2)
                link(V.tensor_reduce(rm[:, 1, :], r2[:, :, :], AX.X, ALU.max), 3)
                V.tensor_tensor(onehot[:, :, :], revb, rm[:, 1, :].unsqueeze(2).to_broadcast([TP, NT, E]),
                                ALU.is_equal).then_inc(onehot_made, 1)

            def place_rows(src, bb):
                def link(ins, k):
                    ins.then_inc(place_step, 1)
                    ve.wait_ge(place_step, nth(bb, 5, k))
                link(V.tensor_tensor(r1[:, :, :], src[0:TP, 0:NT * E].rearrange("p (t e) -> p t e", t=NT),
                                     cnt[0:TP, :].unsqueeze(1).to_broadcast([TP, NT, E]), ALU.add), 0)
                link(V.tensor_tensor(cnt_new[:, :], cnt[:, :], src[:, NT * E:(NT + 1) * E], ALU.add), 1)
                V.tensor_copy(cnt[:, :], cnt_new[:, :]).then_inc(cnt_made, 1)
                link(V.tensor_tensor(r2[:, :, :], r1[:, :, :], onehot[:, :, :], ALU.mult), 2)
                link(V.tensor_reduce(rm[:, 2, :], r2[:, :, :], AX.X, ALU.add), 3)
                V.tensor_copy(rowbuf[:, :, 2 * D].bitcast(I32), token_of[0:TP, :]).then_inc(rank_taken, 1)
                link(V.tensor_copy(pos[:, :], rm[:, 2, :]), 4)
                ve.wait_ge(rank_taken, nth(bb, 1, 0))
                V.tensor_scalar(token_of[:, :], token_of[:, :], float(L), None, ALU.add).then_inc(pos_made, 1)
                ve.wait_ge(cnt_made, nth(bb, 1, 0))
                ve.wait_ge(pos_made, nth(bb, 1, 0))

            def mask_max(h, b):
                ve.wait_ge(scores_done, nth(b, H, h))
                stand_alone(ve)
                for t in range(NT):
                    o, n = score_cols[t]
                    bk, bo = score_bank[t]
                    V.tensor_tensor_reduce(out=probs[:, h % 4, o:o + n], in0=bk[0:TP, bo:bo + n],
                                           in1=mask[0:TP, L - n:L], scale=1.0, scalar=-3e38, op0=ALU.add,
                                           op1=ALU.max, accum_out=rmax[:, h % 4, t:t + 1]).then_inc(masked, 1)
                ve.wait_ge(masked, nth(b, NT * H, NT * h + 2))
                V.tensor_scalar(nmax[:, h % 4, :], rmax[:, h % 4, :], -HD ** -0.5, None, ALU.mult)\
                    .then_inc(nmax_made, 1)

            def divide(h, b):
                ve.wait_ge(exp_done, nth(b, H, h))
                V.reciprocal(rinv[:, h % 4, :], rsum[:, h % 4, :]).then_inc(rinv_made, 1)
                ve.wait_ge(rinv_made, nth(b, H, h))
                for t in range(NT):
                    o, n = score_cols[t]
                    s = probs[:, h % 4, o:o + n]
                    last = V.tensor_scalar(s, s, rinv[:, h % 4, t:t + 1], None, ALU.mult)
                last.then_inc(probs_ready, 1)

            def probs_T(h, b):
                ve.wait_ge(probsT_done, nth(b, H, h))
                V.tensor_copy(probsT[:, h % 2, L:2 * L], tB[0:TP, 0:L]).then_inc(probsT_dve, 1)

            def emit(b, rels):
                for p in range(NP):
                    pp, pb, prel = before(p, b, 1)
                    vp, vb, vrel = before(p, b, 2)
                    places = UNITS[p]
                    if 0 in rels:
                        mask_max(2 * p, b)
                    if vrel in rels:
                        ve.wait_ge(pv_done, nth(vb, NP, vp))
                        ve.wait_ge(aT_hi_made, nth(vb, NP, vp))
                        V.tensor_tensor(aT_lo[:, vp, :], pv[:, 0:L], aT_hi[:, vp, :].bitcast(F32), ALU.subtract)\
                            .then_inc(aT_lo_made, 1)
                    for un in units_of(places[0], rels):
                        take(un, b)
                    if prel in rels:
                        probs_T(2 * pp, pb)
                    for un in units_of(places[1], rels):
                        take(un, b)
                    if p == 4 and 1 in rels:
                        ve.wait_ge(rstd_made, nth(b + 1, 2, 0))
                        normalise(z, lambda t: u[:, t, :], 0).then_inc(normed, 1)
                    if p == 2 and -1 in rels:
                        ve.wait_ge(rstd_out, nth(b - 1, 1, 0))
                        normalise(rowbuf, lambda t: rowbuf[:, t, D:2 * D], 2).then_inc(normed_out, 1)
                    if p == 5 and 1 in rels:
                        ve.wait_ge(affine, nth(b + 1, 2, 1))
                        for t in range(NT):
                            V.bn_stats(st6[:, 1, t, :], h1[:, bass.ds(((b + 1) % 2) * (NT * D) + t * D, D)])\
                                .then_inc(stats_made, 1)
                        norm_stats(1, b + 1, stats_made, nth(b + 1, 2 * NT, 2 * NT - 1), veps_made)
                    if prel in rels:
                        divide(2 * pp + 1, pb)
                    if 0 in rels:
                        mask_max(2 * p + 1, b)
                    for un in units_of(places[2], rels):
                        take(un, b)
                    if prel in rels:
                        probs_T(2 * pp + 1, pb)
                    for un in units_of(places[3], rels):
                        take(un, b)
                    if 0 in rels:
                        divide(2 * p, b)
                    if p == 5 and 1 in rels:
                        ve.wait_ge(rstd_made, nth(b + 1, 2, 1))
                        normalise(n1, lambda t: h1[:, bass.ds(((b + 1) % 2) * (NT * D) + t * D, D)], 1)\
                            .then_inc(normed, 1)
                    if 0 not in rels and 1 in rels and p == 5:
                        low_halves(range(2 * 3))
                if 0 not in rels and 1 in rels:
                    ve.wait_ge(w_hi_made, 7)
                    V.tensor_tensor(wo_lo[:, :, :], wo_raw[:, :, :], wo_hi[:, :, :].bitcast(F32),
                                    ALU.subtract).then_inc(w_lo_made, 1)

            ve.wait_ge(pool_const, N_CONST)
            phase_one(ve, emit)

            steps = [0]

            def link(ins):
                steps[0] += 1
                ins.then_inc(table_step, 1)
                ve.wait_ge(table_step, steps[0])

            V.memset(pad2[:, :], 0.0).then_inc(dve_const, 1)
            ve.wait_ge(cnt_made, B)
            link(V.tensor_copy(padrow[:, :], cnt[0:1, :]))
            ve.wait_ge(dve_const, 5)
            link(V.memset(pad2[:, 2 * D:2 * D + 1].bitcast(I32), NO_TOKEN))
            c8 = lambda i: tb[:, i, 0:E]
            link(V.tensor_tensor(c8(0), cnt[0:1, :], eoff[0:1, :], ALU.subtract))
            link(V.tensor_scalar(tbi[:, 0, 0:E], c8(0), float(SLOT - 1), None, ALU.add))
            link(V.tensor_scalar(tbi[:, 1, 0:E], tbi[:, 0, 0:E], 7, None, ALU.arith_shift_right))
            link(V.tensor_copy(c8(1), tbi[:, 1, 0:E]))
            link(V.tensor_scalar(c8(2), c8(1), float(-SLOT), float(STRIDE), ALU.mult, ALU.add))
            link(V.tensor_copy(tb[:, 3, 0:1], tb[:, 1, 0:1]))
            for e in range(1, E):
                link(V.tensor_tensor(tb[:, 3, e:e + 1], tb[:, 3, e - 1:e], tb[:, 1, e:e + 1], ALU.add))
            link(V.tensor_scalar(endw[:, :], tb[:, 3, 0:E], 1.0, None, ALU.add))
            link(V.tensor_copy(slotf[:, :], iot[0:1, 32:63]))
            NS = N_SLOTS
            link(V.tensor_tensor(reached[:, :, :], slotf[:, :].unsqueeze(2).to_broadcast([1, NS, E]),
                                 tb[:, 3, 0:E].unsqueeze(1).to_broadcast([1, NS, E]), ALU.is_ge))
            link(V.tensor_tensor(jump[:, :, :], reached[:, :, :], tb[:, 2, 0:E].unsqueeze(1).to_broadcast([1, NS, E]), ALU.mult))
            link(V.tensor_reduce(tb[:, 0, 32:32 + NS], reached[:, :, :], AX.X, ALU.add))
            link(V.tensor_reduce(tb[:, 1, 32:32 + NS], jump[:, :, :], AX.X, ALU.add))
            link(V.tensor_scalar(tb[:, 2, 32:32 + NS], slotf[:, :], float(SLOT), None, ALU.mult))
            link(V.tensor_tensor(table[:, 3, 0:NS], tb[:, 1, 32:32 + NS], tb[:, 2, 32:32 + NS], ALU.add))
            link(V.tensor_scalar(tbi[:, 0, 32:32 + NS], tb[:, 0, 32:32 + NS], float(E - 1), None, ALU.min))
            link(V.tensor_scalar(table[:, 0, 0:NS], tbi[:, 0, 32:32 + NS], 1, None, ALU.add))
            link(V.tensor_scalar(table[:, 1, 0:NS], tbi[:, 0, 32:32 + NS], 1, None, ALU.bitwise_and))
            V.tensor_scalar(table[:, 2, 0:NS], table[:, 1, 0:NS], float(WCOLS), None, ALU.mult).then_inc(table_made, 1)
            V.memset(ys[:, 0:1], 0.0).then_inc(slots_done, 1)

            def parity(s):
                return ve.value_load(table[0:1, 1, bass.ds(s, 1)], min_val=0, max_val=1)

            def up(s, j, par):
                if j == 0:
                    e1 = ve.value_load(table[0:1, 0, bass.ds(s, 1)], min_val=1, max_val=E)
                    ve.wait_ge(weights_ready, e1)
                ve.wait_ge(pe_up, 4 * s + 2 * j + 1)
                V.tensor_tensor(gs[:, j, :], up_bank[2 * j][:, :], eb1[:, bass.ds(par * (2 * HID) + (HID + 512 * j), 512)],
                                ALU.add).then_inc(g_added, 1)
                ve.wait_ge(pe_up, 4 * s + 2 * j + 2)
                V.tensor_tensor(as_[:, j, :], up_bank[2 * j + 1][:, :], eb1[:, bass.ds(par * (2 * HID) + 512 * j, 512)],
                                ALU.add).then_inc(a_added, 1)
                ve.wait_ge(a_added, 2 * s + j + 1)
                ve.wait_ge(gated, 2 * s + j + 1)
                V.tensor_tensor(act[:, j, :], as_[:, j, :], sg[:, j, :], ALU.mult).then_inc(act_ready, 1)

            def finish(s, par):
                ve.wait_ge(pe_y, s + 1)
                ve.wait_ge(hs_landed, 16 * (s + 1))
                V.tensor_tensor(ys[:, :], y_bank[:, 0:D], eb2[:, bass.ds(par * D, D)], ALU.add).then_inc(y_biased, 1)
                ve.wait_ge(y_biased, s + 1)
                if not (isinstance(s, int) and s < 1):
                    ve.wait_ge(out_sent, 16 * s)
                V.tensor_copy(ids[:, :], hs[:, D:D + 1].bitcast(U32)).then_inc(slots_done, 1)
                V.tensor_tensor(yo[:, :], ys[:, :], hs[:, 0:D], ALU.add).then_inc(y_ready, 1)

            par = parity(0)
            up(0, 0, par)
            up(0, 1, par)
            par = parity(1)
            up(1, 0, par)
            up(1, 1, par)
            finish(0, parity(0))
            with ve.Fori(2, N_SLOTS) as s:
                par = parity(s)
                up(s, 0, par)
                up(s, 1, par)
                finish(s - 1, parity(s - 1))
            finish(N_SLOTS - 1, parity(N_SLOTS - 1))

        @block.tensor
        def _(pe):
            def mm(o, l, r, start, stop):
                return nc.tensor.matmul(o, l, r, start=start, stop=stop)

            def mm3(o, lh, ll, rh, rl, start, stop):
                mm(o, lh, rh, start, False)
                mm(o, lh, rl, False, False)
                return mm(o, ll, rh, False, stop)

            def unit(un, b):
                kind, index, rel = un
                i = ORDER.index(un)
                dst = bank_of(un)
                bb = b + rel
                for back in range(1, 2 * len(ORDER)):
                    j = i - back
                    it = b if j >= 0 else b - 1
                    other = ORDER[j % len(ORDER)]
                    if bank_of(other) is not dst:
                        continue
                    if isinstance(b, int) and not 0 <= it + other[2] < B:
                        if it < -1:
                            break
                        continue
                    for s_ in taken[other[0]]:
                        pe.wait_ge(s_, count_of(other[0], other[1], it + other[2]))
                    break
                if kind in ("q", "k", "v"):
                    pe.wait_ge(nT_lo_taken, nth(bb, NT, NT - 1))
                    if isinstance(b, int) and b < 0:
                        pe.wait_ge(w_lo_made, 6)
                if kind in ("q", "k"):
                    o = index * 2 * HD + (H * HD if kind == "k" else 0)
                    for c in range(2):
                        last = mm3(dst[:, 0:LP], wq_hi[:, c, o:o + 128], wq_lo[:, c, o:o + 128],
                                   nT_hi[:, c, :], nT_lo[:, c, :], c == 0, c == 1)
                elif kind == "v":
                    g, t = index
                    o = 2 * H * HD + g * D
                    tok = slice(t * TP, (t + 1) * TP)
                    for c in range(2):
                        last = mm3(dst[0:TP, 0:D], nT_hi[:, c, tok], nT_lo[:, c, tok],
                                   wq_hi[:, c, o:o + D], wq_lo[:, c, o:o + D], c == 0, c == 1)
                elif kind == "conv":
                    pe.wait_ge(xT_landed, nth(bb, 1, 0) * 16)
                    if isinstance(b, int) and b < 0:
                        pe.wait_ge(wc_landed, 16)
                    for c in range(4):
                        last = mm(dst[0:TP, 0:D], xT_in[:, c, index * TP:(index + 1) * TP], wc[:, c, :],
                                  c == 0, c == 3)
                elif kind in ("nT", "nT2"):
                    if kind == "nT":
                        pe.wait_ge(normed, nth(bb, 2, 1))
                    else:
                        pe.wait_ge(normed_out, nth(bb, 1, 0))
                    src = n1 if kind == "nT" else rowbuf
                    for c in range(2):
                        last = nc.tensor.transpose(dst[:, c * TP:(c + 1) * TP], src[:, index, c * 128:(c + 1) * 128],
                                                   ident[0:TP, 0:TP])
                elif kind == "wout":
                    pe.wait_ge(aT_lo_made, nth(bb, NP, NP - 1))
                    if isinstance(b, int) and b < 2:
                        pe.wait_ge(w_lo_made, 7)
                    tok = slice(index * TP, (index + 1) * TP)
                    for c in range(NP):
                        last = mm3(dst[0:TP, 0:D], aT_hi[:, c, tok], aT_lo[:, c, tok], wo_hi[:, c, :], wo_lo[:, c, :],
                                   c == 0, c == NP - 1)
                elif kind == "logits":
                    pe.wait_ge(nT2_taken, nth(bb, NT, NT - 1))
                    for t in range(NT):
                        for c in range(2):
                            last = mm(dst[0:TP, t * E:(t + 1) * E], n2T[:, c, t * TP:(t + 1) * TP], rw[:, c, :],
                                      c == 0, c == 1)
                elif kind == "rank":
                    pe.wait_ge(onehot_made, nth(bb, 1, 0))
                    for t in range(NT + 1):
                        o = dst[:, t * E:(t + 1) * E]
                        for t2 in range(min(t, NT)):
                            last = mm(o, ones[0:TP, :], onehot[:, t2, :], t2 == 0, t == NT and t2 == NT - 1)
                        if t < NT:
                            last = mm(o, tri[0:TP, :], onehot[:, t, :], t == 0, True)
                last.then_inc(pe_done[kind], 1)

            def scores(h, b):
                p = h // 2
                pe.wait_ge(q_taken_act, nth(b, NP, p))
                pe.wait_ge(q_taken_dve, nth(b, NP, p))
                pe.wait_ge(k_taken, nth(b, NP, p))
                if not (isinstance(b, int) and b == 0 and h == 0):
                    pe.wait_ge(masked, b * (NT * H) + NT * h)
                for t in (0, 2, 1):
                    bk, o = score_bank[t]
                    n = (t + 1) * TP
                    last = mm(bk[0:TP, o:o + n], qz[:, p % 4, h % 2, t * TP:n], kk[:, p % 4, 0:n], True, True)
                last.then_inc(scores_done, 1)

            def transposes(h, b):
                pe.wait_ge(probs_ready, nth(b, H, h))
                if not (isinstance(b, int) and b == 0 and h == 0):
                    pe.wait_ge(probsT_act, b * H + h)
                    pe.wait_ge(probsT_dve, b * H + h)
                for j in range(NT):
                    for t in range(j, NT):
                        bk, o = ((tA, t * TP), (tB, (t - 1) * TP), (tB, 2 * TP))[j]
                        c = score_cols[t][0] + j * TP
                        last = nc.tensor.transpose(bk[0:TP, o:o + TP], probs[:, h % 4, c:c + TP], ident[0:TP, 0:TP])
                last.then_inc(probsT_done, 1)

            def values(p, b):
                pe.wait_ge(probsT_act, nth(b, H, 2 * p + 1))
                pe.wait_ge(probsT_dve, nth(b, H, 2 * p + 1))
                pe.wait_ge(v_taken, nth(b, NG * NT, p // 2 * NT + 2))
                if not (isinstance(b, int) and b == 0 and p == 0):
                    pe.wait_ge(aT_lo_made, b * NP + p)
                for j, (o, n, first) in enumerate(((0, L, 0), (L, 2 * TP, TP), (L + 2 * TP, TP, 2 * TP))):
                    for a in range(2):
                        c = (p % 2) * 2 * HD + a * HD
                        last = nc.tensor.matmul(pv[a * HD:(a + 1) * HD, first:L], vv[:, p // 2 % 2, j, c:c + HD],
                                                probsT[:, a, o:o + n], start=(j == 0), stop=(j == NT - 1))
                last.then_inc(pv_done, 1)

            def emit(b, rels):
                for p in range(NP):
                    pp, pb, prel = before(p, b, 1)
                    vp, vb, vrel = before(p, b, 2)
                    places = UNITS[p]
                    if 0 in rels:
                        scores(2 * p, b)
                    if vrel in rels:
                        values(vp, vb)
                    for un in units_of(places[0], rels):
                        unit(un, b)
                    if prel in rels:
                        transposes(2 * pp, pb)
                    for un in units_of(places[1], rels):
                        unit(un, b)
                    if 0 in rels:
                        scores(2 * p + 1, b)
                    for un in units_of(places[2], rels):
                        unit(un, b)
                    if prel in rels:
                        transposes(2 * pp + 1, pb)
                    for un in units_of(places[3], rels):
                        unit(un, b)

            pe.wait_ge(pool_const, N_CONST)
            pe.wait_ge(dve_const, 4)
            pe.wait_ge(consts_landed, 80)
            phase_one(pe, emit)

            pe.wait_ge(table_made, 1)

            def weights(s):
                return pe.value_load(table[0:1, 2, bass.ds(s, 1)], min_val=0, max_val=WCOLS)

            def transpose_x(s):
                pe.wait_ge(xs_landed, (s + 1) * 16)
                for c in range(2):
                    last = nc.tensor.transpose(pv[:, c * 128:(c + 1) * 128], xs[:, c * 128:(c + 1) * 128], ident[:, :])
                last.then_inc(pe_xsT, 1)

            def up(s, j, w):
                if j == 0:
                    e1 = pe.value_load(table[0:1, 0, bass.ds(s, 1)], min_val=1, max_val=E)
                    pe.wait_ge(weights_ready, e1)
                    pe.wait_ge(xsT_taken, s + 1)
                for i, col in enumerate((HID + 512 * j, 512 * j)):
                    if not (isinstance(s, int) and s == 0):
                        pe.wait_ge((g_added, a_added)[i], 2 * s + j - 1)
                    for c in range(2):
                        last = mm(up_bank[2 * j + i][:, :], xsT[:, c, :], ew[:, bass.ds(w + (c * 2 * HID + col), 512)],
                                  c == 0, c == 1)
                    last.then_inc(pe_up, 1)

            def transpose_act(s, j):
                pe.wait_ge(act_ready, 2 * s + j + 1)
                if not (isinstance(s, int) and s == 0):
                    pe.wait_ge(actT_taken, 2 * s + j - 1)
                for c in range(4):
                    cols = slice(c * 128, (c + 1) * 128)
                    last = nc.tensor.transpose((tA, tB)[j][:, cols], act[:, j, cols], ident[:, :])
                last.then_inc(pe_actT, 1)

            def down(s, j, w):
                pe.wait_ge(actT_taken, 2 * s + j + 1)
                if j == 0 and not (isinstance(s, int) and s == 0):
                    pe.wait_ge(y_biased, s)
                for c in range(4):
                    last = mm(y_bank[:, 0:D], actT[:, j, c * 128:(c + 1) * 128],
                              ew[:, bass.ds(w + (W1C + (4 * j + c) * D), D)], j == 0 and c == 0, j == 1 and c == 3)
                if j == 1:
                    last.then_inc(pe_y, 1)

            def slot(s, prev, cur, nxt):
                if cur:
                    w = weights(s)
                    up(s, 0, w)
                if prev:
                    w_prev = weights(s - 1)
                    transpose_act(s - 1, 1)
                    down(s - 1, 0, w_prev)
                if cur:
                    up(s, 1, w)
                if nxt:
                    transpose_x(s + 1)
                if cur:
                    transpose_act(s, 0)
                if prev:
                    down(s - 1, 1, w_prev)

            transpose_x(0)
            slot(0, False, True, True)
            with pe.Fori(1, N_SLOTS - 1) as s:
                slot(s, True, True, True)
            slot(N_SLOTS - 1, True, True, False)
            slot(N_SLOTS, True, False, False)


INS = ["xT", "x", "conv_w", "conv_b", "gamma", "beta", "w_qkv", "w_out", "router_w", "router_b",
       "w1", "b1", "w2", "b2"]


def kernel(x, L0_tok_conv_w, L0_tok_conv_b, L0_tok_ln_gamma, L0_tok_ln_beta, L0_attn_W_qkv, L0_attn_W_out,
           L0_ffn_router_w, L0_ffn_router_b, L0_ffn_w1, L0_ffn_b1, L0_ffn_w2, L0_ffn_b2):
    import numpy as np
    import concourse.bacc as bacc
    from concourse.bass_utils import run_bass_kernel_spmd

    x = np.asarray(x)
    pairs = x.reshape(T, 2 * D)
    values = {
        "xT": pairs.T.reshape(4, 128, T).transpose(1, 0, 2),
        "x": pairs.reshape(B, NT, TP, 2 * D),
        "conv_w": np.asarray(L0_tok_conv_w).transpose(2, 1, 0).reshape(4, 128, D).transpose(1, 0, 2),
        "conv_b": L0_tok_conv_b, "gamma": L0_tok_ln_gamma, "beta": L0_tok_ln_beta,
        "w_qkv": L0_attn_W_qkv, "w_out": L0_attn_W_out,
        "router_w": L0_ffn_router_w, "router_b": L0_ffn_router_b,
        "w1": L0_ffn_w1, "b1": L0_ffn_b1, "w2": L0_ffn_w2, "b2": L0_ffn_b2,
    }
    nc = bacc.Bacc("TRN2", target_bir_lowering=False, num_devices=1)
    arrays, args = {}, []
    for name in INS:
        a = np.ascontiguousarray(values[name])
        arrays[f"in_{name}"] = a
        args.append(nc.dram_tensor(f"in_{name}", a.shape, mybir.dt.from_np(a.dtype), kind="ExternalInput").ap())
    args.append(nc.dram_tensor("out_rows", (T, D), F32, kind="ExternalOutput").ap())
    tower(nc, *args)
    r = run_bass_kernel_spmd(nc, [arrays], core_ids=[0])
    return r.results[0]["out_rows"].reshape(B, L, D)
```

```python
from contextlib import ExitStack

import concourse.bass as bass
from concourse import mybir
from concourse.alu_op_type import AluOpType as ALU

ACT = mybir.ActivationFunctionType
AX = mybir.AxisListType
F32 = mybir.dt.float32
F32R = mybir.dt.float32r
BF16 = mybir.dt.bfloat16
I32 = mybir.dt.int32
U32 = mybir.dt.uint32

B, L, D = 8, 375, 256
T = B * L
TP, NT = 125, 3
LP = L + 1
H, HD = 16, 64
NP = H // 2
NG = NP // 2
HID = 1024
E = 8
SLOT = 128
STRIDE = T + SLOT
N_SLOTS = (T + E * (SLOT - 1)) // SLOT
MIN_SLOTS = -(-T // SLOT)
SPARE = N_SLOTS - MIN_SLOTS
ROWS = E * STRIDE + SPARE * SLOT
ROW = 516
NO_TOKEN = 2 * T
EPS = 1e-5
MASKED = -1e30

W1C = 2 * 2 * HID
WCOLS = W1C + HID // 128 * D
N_EW = 3
BLOCK = 2 * WCOLS + 2 * HID + D
CHUNK = 512
N_CHUNKS = WCOLS // CHUNK
N_SPLIT = 4

UNITS = [
    [[("q", 1, 0)], [("k", 1, 0)], [("q", 2, 0), ("v", (0, 2), 0)], [("k", 2, 0)]],
    [[], [("wout", 0, -1)], [("wout", 1, -1)], [("wout", 2, -1)]],
    [[("q", 3, 0)], [("conv", 0, 1)], [("k", 3, 0)], [("conv", 1, 1)]],
    [[("conv", 2, 1)], [("q", 4, 0), ("v", (1, 0), 0)], [("k", 4, 0), ("v", (1, 1), 0)], [("v", (1, 2), 0)]],
    [[("q", 5, 0)], [("nT2", 0, -1), ("v", (2, 0), 0), ("nT2", 1, -1)], [("k", 5, 0), ("nT2", 2, -1)],
     [("v", (2, 1), 0)]],
    [[("q", 6, 0)], [("v", (2, 2), 0), ("logits", 0, -1)], [("k", 6, 0)], [("v", (3, 0), 0)]],
    [[("q", 7, 0)], [("k", 7, 0)], [("v", (3, 1), 0)], [("v", (3, 2), 0), ("nT", 0, 1), ("nT", 1, 1)]],
    [[("nT", 2, 1)], [("rank", 0, -1)], [("q", 0, 1), ("k", 0, 1)], [("v", (0, 0), 1), ("v", (0, 1), 1)]],
]
ORDER = [u for pair in UNITS for place in pair for u in place]
PER_BATCH = {"q": NP, "k": NP, "v": NG * NT, "wout": NT, "nT2": NT, "conv": NT, "nT": NT,
             "logits": 1, "rank": 1}
N_AUX = 3


def event(kind, index):
    return index[0] * NT + index[1] if kind == "v" else index


def tower(nc, xT, x, conv_w, conv_b, gamma, beta, w_qkv, w_out, router_w, router_b,
          w1, b1, w2, b2, out):
    ctx = ExitStack()
    with ctx:
        rows = nc.dram_tensor("token_rows", [ROWS, ROW], F32)
        rows = rows.ap()
        halves = [nc.dram_tensor(f"expert_w_{n}", [E, 128, WCOLS], F32).ap() for n in ("hi", "lo")]

        cursor = [nc.sbuf_base + (-nc.sbuf_base) % 64]

        def at_offset(name, shape, dt, offset):
            return nc.alloc_sbuf_tensor_at(name, shape, dt, offset=offset)

        def size(shape, dt):
            n = 2 if dt == BF16 else 4
            for s in shape[1:]:
                n *= s
            return n + (-n) % 32

        def sb(name, shape, dt=F32):
            o = cursor[0]
            cursor[0] += size(shape, dt)
            return at_offset(name, shape, dt, o)

        def bank(name):
            return ctx.enter_context(nc.psum_tensor(name, [128, 512], F32))

        def sem(name):
            return ctx.enter_context(nc.semaphore(name))

        ident = sb("ident", [128, 128])
        endw = sb("endw", [1, E], I32)
        table = sb("table", [1, 3, 32], I32)
        padrow = sb("padrow", [1, E], I32)
        phase_start = cursor[0]

        wq_hi = sb("wq_hi", [128, 2, 3 * H * HD], F32R)
        wq_lo = sb("wq_lo", [128, 2, 3 * H * HD], F32R)
        xT_in = sb("xT_in", [128, 4, L])
        x_in = sb("x_in", [TP, NT, 2 * D])
        x_end = cursor[0]
        wc = sb("wc", [128, 4, D])
        xsum = sb("xsum", [TP, NT, D])
        u = sb("u", [TP, NT, D])
        z = sb("z", [TP, NT, D])
        n1 = sb("n1", [TP, NT, D])
        nT_hi = sb("nT_hi", [128, 2, LP], F32R)
        nT_lo = sb("nT_lo", [128, 2, LP], F32R)
        qz = sb("qz", [128, 4, 2, LP])
        kk = sb("kk", [128, 4, LP])
        vv = sb("vv", [TP, 2, NT, D])
        probs = sb("probs", [TP, 4, 2 * L])
        attention_end = cursor[0]
        probsT = sb("probsT", [TP, 2, 2 * L])
        n2T_start = cursor[0]
        n2T = sb("n2T", [128, 2, L])
        wo_hi = sb("wo_hi", [128, NP, D], F32R)
        wo_lo = sb("wo_lo", [128, NP, D], F32R)
        h1 = sb("h1", [TP, 2 * NT * D])
        rw = sb("rw", [128, 2, E])
        bias2 = sb("bias2", [128, D])
        gam = sb("gam", [128, D])
        bet = sb("bet", [128, D])
        rb = sb("rb", [128, E])
        mask = sb("mask", [128, L])
        tri = sb("tri", [128, 128], BF16)
        ones = sb("ones", [128, 128], BF16)
        rev = sb("rev", [128, E])
        token_of = sb("token_of", [128, NT])
        halfs = sb("halfs", [128, NT])
        rowbuf = sb("rowbuf", [TP, NT, ROW])
        cnt = sb("cnt", [128, E])
        eoff = sb("eoff", [128, E])
        iot = sb("iot", [128, 64], I32)
        st6 = sb("st6", [TP, 3, NT, 6])
        mv = sb("mv", [TP, 3, NT, 2])
        veps = sb("veps", [TP, 3, NT])
        rstd = sb("rstd", [TP, 3, NT])
        rmax = sb("rmax", [TP, 4, NT])
        nmax = sb("nmax", [TP, 4, NT])
        rsum = sb("rsum", [TP, 4, NT])
        rinv = sb("rinv", [TP, 4, NT])
        lg = sb("lg", [TP, NT, E])
        r1 = sb("r1", [TP, NT, E])
        r2 = sb("r2", [TP, NT, E])
        rm = sb("rm", [TP, 4, NT])
        onehot = sb("onehot", [TP, NT, E], BF16)
        pos = sb("pos", [TP, NT], U32)
        cnt_new = sb("cnt_new", [128, E])
        tb = sb("tb", [1, 4, 64])
        tbi = sb("tbi", [1, 2, 64], I32)
        slotf = sb("slotf", [1, N_SLOTS])
        slot_rows = sb("slot_rows", [1, N_SLOTS])
        upto = sb("upto", [1, E, E])
        ends8 = sb("ends8", [1, E, E])
        reached = sb("reached", [1, N_SLOTS, E])
        jump = at_offset("jump", [1, N_SLOTS, E], F32, n2T_start)
        attn_start = cursor[0]
        assert x_end - phase_start >= BLOCK * 4 and attention_end - phase_start >= 2 * BLOCK * 4
        aT_hi = sb("aT_hi", [128, NP, L], F32R)
        aT_lo = sb("aT_lo", [128, NP, L], F32R)
        attn_end = cursor[0]
        cursor[0] = attn_start
        wq_raw = sb("wq_raw", [128, 2, 3 * H * HD])
        wo_raw = sb("wo_raw", [128, NP, D])
        pad_start = cursor[0]
        pad = sb("pad", [128, ROW])
        raw = sb("raw", [128, N_SPLIT, CHUNK])
        assert cursor[0] <= nc.sbuf_usable_end, (cursor[0], nc.sbuf_usable_end)
        raw_hi = at_offset("raw_hi", [128, N_SPLIT, CHUNK], F32R, attn_end)
        assert attn_end + N_SPLIT * CHUNK * 4 <= pad_start

        cursor[0] = phase_start
        ew = sb("ew", [128, N_EW * BLOCK])
        xs = sb("xs", [128, 2, D])
        hs = sb("hs", [128, 2, D + 4])
        xsT_hi = sb("xsT_hi", [128, 4, 128], F32R)
        xsT_lo = sb("xsT_lo", [128, 4, 128], F32R)
        gs = sb("gs", [128, 2, 512])
        sg = sb("sg", [128, 2, 512])
        as_ = sb("as_", [128, 2, 512])
        act = sb("act", [128, 2, 512])
        actT_hi = sb("actT_hi", [128, 2, 512], F32R)
        actT_lo = sb("actT_lo", [128, 2, 512], F32R)
        ys = sb("ys", [128, D])
        yo = sb("yo", [128, 2, D])
        ids = sb("ids", [128, 2], U32)
        assert attn_start <= phase_start + N_EW * BLOCK * 4 and cursor[0] <= nc.sbuf_usable_end, cursor[0]

        sA, sB, tA, tB, pv = (bank(n) for n in ("sA", "sB", "tA", "tB", "pv"))
        aux = [bank(f"aux{i}") for i in range(N_AUX)]
        up_bank = [sA, sB, aux[1], aux[2]]
        y_bank = aux[0]

        score_cols = {0: (0, TP), 2: (TP, 3 * TP), 1: (4 * TP, 2 * TP)}
        score_bank = {0: (sA, 0), 2: (sA, TP), 1: (sB, 0)}

        xT_landed, x_landed = sem("xT_landed"), sem("x_landed")
        wc_landed, affine_landed, router_landed = sem("wc_landed"), sem("affine_landed"), sem("router_landed")
        bias_landed, bias_doubled = sem("bias_landed"), sem("bias_doubled")
        wq_landed, wo_landed = [sem(f"wq_landed{i}") for i in range(6)], sem("wo_landed")
        pool_const, dve_const = sem("pool_const"), sem("dve_const")
        w_hi_made, w_lo_made = sem("w_hi_made"), sem("w_lo_made")
        xsum_step, wo_halved = sem("xsum_step"), sem("wo_halved")
        pe_done = {k: sem(f"pe_{k}") for k in PER_BATCH}
        q_taken_act, q_taken_dve = sem("q_taken_act"), sem("q_taken_dve")
        k_taken, v_taken = sem("k_taken"), sem("v_taken")
        nT_hi_taken, nT_lo_taken = sem("nT_hi_taken"), sem("nT_lo_taken")
        conv_taken, wout_taken, nT2_taken = sem("conv_taken"), sem("wout_taken"), sem("nT2_taken")
        logits_taken, rank_taken = sem("logits_taken"), sem("rank_taken")
        stats_made, veps_made, rstd_made = sem("stats_made"), sem("veps_made"), sem("rstd_made")
        normed = sem("normed")
        affine = sem("affine")
        scores_done, masked, nmax_made = sem("scores_done"), sem("masked"), sem("nmax_made")
        exp_done, rinv_made, probs_ready = sem("exp_done"), sem("rinv_made"), sem("probs_ready")
        probsT_done, probsT_act, probsT_dve = sem("probsT_done"), sem("probsT_act"), sem("probsT_dve")
        pv_done, aT_hi_made, aT_lo_made = sem("pv_done"), sem("aT_hi_made"), sem("aT_lo_made")
        route_step = sem("route_step")
        onehot_made, pos_made, cnt_made = sem("onehot_made"), sem("pos_made"), sem("cnt_made")
        place_step, token_made = sem("place_step"), sem("token_made")
        waits_passed = sem("waits_passed")
        stats_out, veps_out, rstd_out, normed_out = (sem(n) for n in ("stats_out", "veps_out", "rstd_out", "normed_out"))
        aggr_made = [sem(f"aggr_made{i}") for i in range(3)]
        rows_sent, pads_sent = sem("rows_sent"), sem("pads_sent")
        table_step, table_made = sem("table_step"), sem("table_made")
        padrow_made, slot_rows_made = sem("padrow_made"), sem("slot_rows_made")
        slots_done, weights_ready = sem("slots_done"), sem("weights_ready")
        weights_landed = [sem(f"weights_landed{i}") for i in range(N_EW)]
        out_sent = [sem("out_sent_even"), sem("out_sent_odd")]
        xs_landed = [sem("xs_landed_even"), sem("xs_landed_odd")]
        hs_landed = [sem("hs_landed_even"), sem("hs_landed_odd")]
        pe_xsT, xsT_hi_taken, xsT_lo_taken = sem("pe_xsT"), sem("xsT_hi_taken"), sem("xsT_lo_taken")
        chunk_landed = [sem(f"chunk_landed{i}") for i in range(N_SPLIT)]
        chunk_stored = [sem(f"chunk_stored{i}") for i in range(N_SPLIT)]
        chunk_hi_made, chunk_lo_made = sem("chunk_hi_made"), sem("chunk_lo_made")
        pe_up, g_added, a_added = sem("pe_up"), sem("g_added"), sem("a_added")
        gated, act_ready = sem("gated"), sem("act_ready")
        pe_actT, actT_hi_taken, actT_lo_taken = sem("pe_actT"), sem("actT_hi_taken"), sem("actT_lo_taken")
        pe_y, y_biased, y_ready = sem("pe_y"), sem("y_biased"), sem("y_ready")


        taken = {
            "q": [q_taken_act, q_taken_dve], "k": [k_taken], "v": [v_taken], "wout": [wout_taken],
            "nT2": [nT2_taken], "conv": [conv_taken], "nT": [nT_lo_taken],
            "logits": [logits_taken], "rank": [rank_taken],
        }

        def nth(batch, per, k):
            return batch * per + (k + 1)

        def in_place(e, k):
            return e * (N_CHUNKS // N_SPLIT) + (k // N_SPLIT + 1)

        def count_of(kind, index, batch):
            return nth(batch, PER_BATCH[kind], event(kind, index))

        def bank_of(unit):
            return aux[ORDER.index(unit) % N_AUX]

        def before(p, b, n):
            return (p - n, b, 0) if p >= n else (NP + p - n, b - 1, -1)

        def units_of(place, rels):
            return [u_ for u_ in place if u_[2] in rels]

        def phase_one(engine, emit):
            emit(-1, (1,))
            emit(0, (0, 1))
            with engine.Fori(1, B - 1) as b:
                emit(b, (-1, 0, 1))
            emit(B - 1, (-1, 0))
            emit(B, (-1,))

        def phase_two(engine, slot):
            for s in range(4):
                slot(s, s % 2, s // 2)
            pairs = (N_SLOTS - 3) // 2
            with engine.Fori(2, pairs) as i:
                for parity in range(2):
                    slot(2 * i + parity, parity, i)
            for s in range(2 * pairs, N_SLOTS + 1):
                slot(s, s % 2, s // 2)

        def steps_of(s):
            return [not isinstance(s, int) or 0 <= s + k < N_SLOTS for k in (-1, 0, 1, 2)]

        N_CONST = 10

        def stand_alone(engine):
            engine.sem_inc(waits_passed, 1)

        block = ctx.enter_context(nc.Block())

        @block.sync
        def _(sp):
            def load_x(b, first):
                src_T = xT[:, :, 0:L] if first else xT[:, :, bass.ds(b * L, L)]
                src = x[0] if first else x[bass.ds(b, 1)].rearrange("a t p d -> (a t) p d")
                sp.dma_start(xT_in[:, :, :], src_T).then_inc(xT_landed, 16)
                if first:
                    sp.dma_start(wc[:, :, :], conv_w).then_inc(wc_landed, 16)
                sp.dma_start(x_in[:, :, :], src.rearrange("t p d -> p t d")).then_inc(x_landed, 16)

            load_x(0, True)
            sp.dma_start(bias2[:, :], conv_b.partition_broadcast(128)).then_inc(bias_landed, 16)
            wq_rows = w_qkv.rearrange("(c p) n -> c p n", p=128)
            for i in range(3):
                for c in range(2):
                    cols = slice(i * H * HD, (i + 1) * H * HD)
                    sp.dma_start(wq_raw[:, c, cols], wq_rows[c][:, cols]).then_inc(wq_landed[2 * i + c], 16)
                    if i == 0 and c == 1:
                        for dst, src in ((gam, gamma), (bet, beta)):
                            sp.dma_start(dst[:, :], src.partition_broadcast(128)).then_inc(affine_landed, 16)
            sp.dma_start(rb[:, :], router_b.partition_broadcast(128)).then_inc(router_landed, 16)
            sp.dma_start(rw[:, :, :], router_w.rearrange("(c p) e -> p c e", p=128)).then_inc(router_landed, 16)
            sp.dma_start(wo_raw[:, :, :], w_out.rearrange("(c p) n -> p c n", p=128)).then_inc(wo_landed, 16)

            def of_expert(src, e):
                return src[e] if isinstance(e, int) else src[bass.ds(e, 1)].rearrange("a p n -> (a p) n")

            def load_chunk(e, k):
                if not (isinstance(e, int) and e == 0 and k < N_SPLIT):
                    sp.wait_ge(chunk_stored[k % N_SPLIT], in_place(e, k) * 32 - 32)
                    stand_alone(sp)
                n_w1 = W1C // CHUNK
                if k < n_w1:
                    c, i = divmod(k, n_w1 // 2)
                    sp.dma_start(raw[:, k % N_SPLIT, :],
                                 of_expert(w1, e)[c * 128:(c + 1) * 128, i * CHUNK:(i + 1) * CHUNK])\
                        .then_inc(chunk_landed[k % N_SPLIT], 16)
                else:
                    c = (k - n_w1) * (CHUNK // D)
                    sp.dma_start(raw[:, k % N_SPLIT, :].rearrange("p (c n) -> p c n", n=D),
                                 of_expert(w2, e)[c * 128:(c + CHUNK // D) * 128, :]
                                 .rearrange("(c p) n -> p c n", p=128)).then_inc(chunk_landed[k % N_SPLIT], 16)

            def store_chunk(e, k):
                sp.wait_ge(chunk_lo_made, e * N_CHUNKS + (k + 1))
                stand_alone(sp)
                for half, src in zip(halves, (raw_hi, raw)):
                    sp.dma_start(of_expert(half, e)[:, k * CHUNK:(k + 1) * CHUNK],
                                 src[:, k % N_SPLIT, :].bitcast(F32)).then_inc(chunk_stored[k % N_SPLIT], 16)

            def batch(b, nxt, prev):
                if nxt:
                    sp.wait_ge(pe_done["conv"], nth(b, NT, NT - 1))
                    stand_alone(sp)
                    sp.wait_ge(xsum_step, nth(b, 2, 1))
                    stand_alone(sp)
                    load_x(b + 1, False)
                for k in range(N_CHUNKS):
                    load_chunk(b, k)
                    if k >= 2:
                        store_chunk(b, k - 2)
                    elif prev:
                        store_chunk(b - 1, N_CHUNKS - 2 + k)

            batch(0, True, False)
            with sp.Fori(1, B - 1) as b:
                batch(b, True, True)
            batch(B - 1, False, True)
            store_chunk(E - 1, N_CHUNKS - 2)
            store_chunk(E - 1, N_CHUNKS - 1)
            for i in range(N_SPLIT):
                sp.wait_ge(chunk_stored[i], in_place(E, i - N_SPLIT) * 32)

            def load_halves(e, which):
                for half in which:
                    o = (e % N_EW) * BLOCK + half * WCOLS
                    if e >= 2 and (e >= N_EW or half):
                        sp.wait_ge(weights_landed[e % N_EW], 64 * (e // N_EW) + 16 * half)
                    sp.dma_start(ew[:, o:o + WCOLS], halves[half][e]).then_inc(weights_landed[e % N_EW], 16)

            def load_biases(e):
                o = (e % N_EW) * BLOCK + 2 * WCOLS
                sp.wait_ge(weights_landed[e % N_EW], 64 * (e // N_EW) + 32)
                sp.dma_start(ew[:, o:o + 2 * HID], b1[e].partition_broadcast(128))\
                    .then_inc(weights_landed[e % N_EW], 16)
                o += 2 * HID
                sp.dma_start(ew[:, o:o + D], b2[e].partition_broadcast(128)).then_inc(weights_landed[e % N_EW], 16)

            def ready(e):
                sp.wait_ge(weights_landed[e % N_EW], 64 * (e // N_EW + 1))
                sp.sem_inc(weights_ready, 1)

            for kind in ("q", "k", "v"):
                sp.wait_ge(pe_done[kind], B * PER_BATCH[kind])
            load_halves(0, (0,))
            sp.wait_ge(rows_sent, ((B - 1) * NT + SPARE) * 16)
            load_halves(0, (1,))
            load_biases(0)
            sp.wait_ge(pv_done, B * NP)
            load_halves(1, (0,))
            sp.wait_ge(padrow_made, 1)
            for e in range(E):
                r = sp.value_load(padrow[0:1, e:e + 1], min_val=e * STRIDE, max_val=e * STRIDE + T)
                sp.dma_start(rows[bass.ds(r, SLOT), :], pad[:, :]).then_inc(pads_sent, 16)
            ready(0)
            sp.wait_ge(xs_landed[0], 16)
            load_halves(1, (1,))
            load_biases(1)
            sp.wait_ge(table_made, 1)
            sp.wait_ge(rows_sent, (B * NT + SPARE) * 16)
            load_halves(2, (0, 1))
            load_biases(2)
            ready(1)
            ready(2)
            for e in range(N_EW, E):
                done = sp.value_load(endw[0:1, e - N_EW:e - N_EW + 1], min_val=1, max_val=N_SLOTS + 1)
                sp.wait_ge(slots_done, done)
                load_halves(e, (0, 1))
                load_biases(e)
                ready(e)
            for par in range(2):
                sp.wait_ge(out_sent[par], 16 * ((N_SLOTS + 1 - par) // 2))

        @block.gpsimd
        def _(pool):
            pool.memset(ident[:, :], 0.0).then_inc(pool_const, 1)
            pool.memset(mask[:, :], 0.0).then_inc(pool_const, 1)
            pool.memset(tri[:, :], 1.0).then_inc(pool_const, 1)
            pool.iota(iot[:, 0:NT], pattern=[[TP, NT]], base=0, channel_multiplier=1).then_inc(pool_const, 1)
            pool.iota(iot[:, 8:8 + E], pattern=[[-1, E]], base=E, channel_multiplier=0).then_inc(pool_const, 1)
            pool.iota(iot[:, 16:16 + E], pattern=[[STRIDE, E]], base=0, channel_multiplier=0).then_inc(pool_const, 1)
            pool.iota(iot[:, 32:63], pattern=[[1, 31]], base=0, channel_multiplier=0).then_inc(pool_const, 1)
            pool.wait_ge(pool_const, 7)
            pool.affine_select(out=ident[:, :], in_=ident[:, :], compare_op=ALU.not_equal, fill=1.0,
                               base=0, pattern=[[-1, 128]], channel_multiplier=1).then_inc(pool_const, 1)
            pool.affine_select(out=mask[:, 2 * TP:], in_=mask[:, 2 * TP:], compare_op=ALU.is_ge, fill=MASKED,
                               base=0, pattern=[[-1, TP]], channel_multiplier=1).then_inc(pool_const, 1)
            pool.affine_select(out=tri[:, :], in_=tri[:, :], compare_op=ALU.is_gt, fill=0.0,
                               base=0, pattern=[[1, 128]], channel_multiplier=-1).then_inc(pool_const, 1)

            def split(b, ks, rels):
                for k in ks if 0 in rels else ():
                    pool.wait_ge(chunk_hi_made, b * N_CHUNKS + (k + 1))
                    i = k % N_SPLIT
                    pool.tensor_tensor(raw[:, i, :].bitcast(F32R), raw[:, i, :], raw_hi[:, i, :].bitcast(F32), ALU.subtract)\
                        .then_inc(chunk_lo_made, 1)

            def emit(b, rels):
                if 1 in rels:
                    pool.wait_ge(x_landed, nth(b + 1, 1, 0) * 16)
                    if not (isinstance(b, int) and b < 0):
                        pool.wait_ge(conv_taken, nth(b, NT, NT - 1))
                    pool.tensor_tensor(xsum[:, :, :], x_in[:, :, 0:D], x_in[:, :, D:], ALU.add).then_inc(xsum_step, 1)
                    pool.wait_ge(xsum_step, nth(b + 1, 2, 0))
                    if isinstance(b, int) and b < 0:
                        pool.wait_ge(bias_doubled, 1)
                    pool.tensor_tensor(xsum[:, :, :], xsum[:, :, :],
                                       bias2[0:TP, :].unsqueeze(1).to_broadcast([TP, NT, D]), ALU.add)\
                        .then_inc(xsum_step, 1)
                split(b, (0, 1, 2), rels)
                if -1 in rels:
                    pool.wait_ge(veps_out, nth(b - 1, 1, 0))
                    pool.tensor_tensor(rstd[:, 2, :], veps[:, 2, :], halfs[0:TP, :], ALU.pow).then_inc(rstd_out, 1)
                split(b, (3, 4, 5, 6), rels)
                if 1 in rels:
                    pool.wait_ge(veps_made, nth(b + 1, 2, 0))
                    pool.tensor_tensor(rstd[:, 0, :], veps[:, 0, :], halfs[0:TP, :], ALU.pow).then_inc(rstd_made, 1)
                split(b, (7, 8), rels)
                if 1 in rels:
                    if isinstance(b, int) and b < 0:
                        pool.wait_ge(affine_landed, 32)
                    pool.wait_ge(normed, nth(b + 1, 2, 0))
                    pool.tensor_tensor(z[:, :, :], z[:, :, :],
                                       gam[0:TP, :].unsqueeze(1).to_broadcast([TP, NT, D]), ALU.mult)\
                        .then_inc(affine, 1)
                    pool.wait_ge(affine, nth(b + 1, 2, 0))
                    o = ((b + 1) % 2) * (NT * D)
                    pool.tensor_tensor(h1[:, bass.ds(o, NT * D)].rearrange("p (t d) -> p t d", t=NT), z[:, :, :],
                                       bet[0:TP, :].unsqueeze(1).to_broadcast([TP, NT, D]), ALU.add)\
                        .then_inc(affine, 1)
                split(b, (9, 10), rels)
                if 1 in rels:
                    pool.wait_ge(veps_made, nth(b + 1, 2, 1))
                    pool.tensor_tensor(rstd[:, 1, :], veps[:, 1, :], halfs[0:TP, :], ALU.pow).then_inc(rstd_made, 1)
                if isinstance(b, int) and b < 0:
                    pool.wait_ge(dve_const, 3)
                    for s in range(SPARE):
                        r = E * STRIDE + s * SLOT
                        pool.dma_start(rows[r:r + SLOT, :], pad[:, :]).then_inc(rows_sent, 16)
                    pool.wait_ge(wo_landed, 16)
                    pool.tensor_copy(wo_hi[:, :, :], wo_raw[:, :, :]).then_inc(wo_halved, 1)
                    pool.wait_ge(wo_halved, 1)
                    pool.tensor_tensor(wo_lo[:, :, :], wo_raw[:, :, :], wo_hi[:, :, :].bitcast(F32),
                                       ALU.subtract).then_inc(wo_halved, 1)
                split(b, (11,), rels)
                if -1 in rels:
                    pool.wait_ge(pos_made, nth(b - 1, 1, 0))
                    stand_alone(pool)
                    for t in range(NT):
                        pool.indirect_dma_start(rows, bass.IndirectOffsetOnAxis(pos[:, t:t + 1], 0),
                                                rowbuf[:, t, :], None).then_inc(rows_sent, 16)

            phase_one(pool, emit)

            def slot(s, par):
                pool.wait_ge(y_ready, s + 1)
                stand_alone(pool)
                pool.indirect_dma_start(out, bass.IndirectOffsetOnAxis(ids[:, par:par + 1], 0), yo[:, par, :], None,
                                        bounds_check=T - 1, oob_is_err=False).then_inc(out_sent[par], 16)

            with pool.Fori(0, N_SLOTS // 2) as i:
                for par in range(2):
                    slot(2 * i + par, par)
            for s in range(N_SLOTS // 2 * 2, N_SLOTS):
                slot(s, s % 2)

        @block.scalar
        def _(ac):
            def copy(dst, src):
                return nc.scalar.activation(dst, src, ACT.Copy)

            for i in range(3):
                for c in range(2):
                    cols = slice(i * H * HD, (i + 1) * H * HD)
                    ac.wait_ge(wq_landed[2 * i + c], 16)
                    copy(wq_hi[:, c, cols], wq_raw[:, c, cols]).then_inc(w_hi_made, 1)

            def take(unit, b):
                kind, index, rel = unit
                src = bank_of(unit)
                if kind in ("conv", "wout", "logits", "rank"):
                    return
                ac.wait_ge(pe_done[kind], count_of(kind, index, b + rel))
                if kind == "q":
                    copy(qz[0:HD, index % 4, 0, :], src[0:HD, 0:LP]).then_inc(q_taken_act, 1)
                elif kind == "k":
                    copy(kk[:, index % 4, :], src[:, 0:LP]).then_inc(k_taken, 1)
                elif kind == "v":
                    copy(vv[:, index[0] % 2, index[1], :], src[0:TP, 0:D]).then_inc(v_taken, 1)
                elif kind == "nT":
                    copy(nT_hi[:, :, index * TP:(index + 1) * TP],
                         src[:, 0:2 * TP].rearrange("p (c t) -> p c t", c=2)).then_inc(nT_hi_taken, 1)
                elif kind == "nT2":
                    copy(n2T[:, :, index * TP:(index + 1) * TP],
                         src[:, 0:2 * TP].rearrange("p (c t) -> p c t", c=2)).then_inc(nT2_taken, 1)

            def exps(h, b):
                ac.wait_ge(nmax_made, nth(b, H, h))
                for t in range(NT):
                    o, n = score_cols[t]
                    s = probs[:, h % 4, o:o + n]
                    last = nc.scalar.activation(s, s, ACT.Exp, bias=nmax[:, h % 4, t:t + 1], scale=HD ** -0.5,
                                                accum_out=rsum[:, h % 4, t:t + 1])
                last.then_inc(exp_done, 1)

            def probs_T(h, b):
                ac.wait_ge(probsT_done, nth(b, H, h))
                copy(probsT[:, h % 2, 0:L], tA[0:TP, 0:L]).then_inc(probsT_act, 1)

            def split(b, k, rels):
                if 0 in rels:
                    if isinstance(b, int) and b == 0 and k == 0:
                        ac.wait_ge(wo_halved, 2)
                    ac.wait_ge(chunk_landed[k % N_SPLIT], in_place(b, k) * 16)
                    copy(raw_hi[:, k % N_SPLIT, :], raw[:, k % N_SPLIT, :]).then_inc(chunk_hi_made, 1)

            def emit(b, rels):
                for p in range(NP):
                    pp, pb, prel = before(p, b, 1)
                    vp, vb, vrel = before(p, b, 2)
                    places = UNITS[p]
                    if vrel in rels:
                        ac.wait_ge(pv_done, nth(vb, NP, vp))
                        copy(aT_hi[:, vp, :], pv[:, 0:L]).then_inc(aT_hi_made, 1)
                    for un in units_of(places[0], rels):
                        take(un, b)
                    if 0 in rels:
                        exps(2 * p, b)
                    if prel in rels:
                        probs_T(2 * pp, pb)
                    for un in units_of(places[1], rels):
                        take(un, b)
                    if 2 * p < N_CHUNKS:
                        split(b, 2 * p, rels)
                    for un in units_of(places[2], rels):
                        take(un, b)
                    if 0 in rels:
                        exps(2 * p + 1, b)
                    if prel in rels:
                        probs_T(2 * pp + 1, pb)
                    for un in units_of(places[3], rels):
                        take(un, b)
                    if 2 * p < N_CHUNKS:
                        split(b, 2 * p + 1, rels)

            phase_one(ac, emit)

            def load_xs(s, par):
                row = ac.value_load(table[0:1, 2, bass.ds(s, 1)], min_val=0, max_val=ROWS - SLOT)
                ac.dma_start(xs[:, par, :], rows[bass.ds(row, SLOT), 0:D]).then_inc(xs_landed[par], 16)

            def load_hs(s, par):
                row = ac.value_load(table[0:1, 2, bass.ds(s, 1)], min_val=0, max_val=ROWS - SLOT)
                ac.dma_start(hs[:, par, :], rows[bass.ds(row, SLOT), D:2 * D + 4]).then_inc(hs_landed[par], 16)

            def gate(s, j):
                ac.wait_ge(g_added, 2 * s + j + 1)
                nc.scalar.activation(sg[:, j, :], gs[:, j, :], ACT.Sigmoid).then_inc(gated, 1)

            def take_actT(s, j):
                ac.wait_ge(pe_actT, 2 * s + j + 1)
                copy(actT_hi[:, j, :], (tA, tB)[j][:, :]).then_inc(actT_hi_taken, 1)

            def take_xsT(s, par):
                ac.wait_ge(pe_xsT, s + 1)
                copy(xsT_hi[:, 2 * par:2 * par + 2, :], pv[:, 0:256].rearrange("p (c t) -> p c t", c=2)).then_inc(xsT_hi_taken, 1)

            ac.wait_ge(slot_rows_made, 1)
            ac.wait_ge(rows_sent, (B * NT + SPARE) * 16)
            ac.wait_ge(pads_sent, E * 16)
            load_xs(0, 0)
            load_xs(1, 1)
            take_xsT(0, 0)

            def slot(s, par, pair):
                prev, cur, nxt, nxt2 = steps_of(s)
                if nxt2:
                    load_xs(s + 2, par)
                if cur:
                    if not (isinstance(s, int) and s < 2):
                        ac.wait_ge(y_ready, s - 1)
                    load_hs(s, par)
                    gate(s, 0)
                if prev:
                    take_actT(s - 1, 1)
                if nxt:
                    take_xsT(s + 1, 1 - par)
                if cur:
                    gate(s, 1)
                if cur:
                    take_actT(s, 0)

            phase_two(ac, slot)

        @block.vector
        def _(ve):
            V = nc.vector
            V.memset(pad[:, :], 0.0).then_inc(dve_const, 1)
            V.memset(halfs[:, :], -0.5).then_inc(dve_const, 1)
            ve.wait_ge(dve_const, 2)
            V.memset(pad[:, 2 * D:2 * D + 1].bitcast(I32), NO_TOKEN).then_inc(dve_const, 1)
            V.memset(ones[:, :], 1.0)
            V.memset(qz[HD:, :, 0, :], 0.0)
            V.memset(qz[0:HD, :, 1, :], 0.0)
            V.memset(nT_hi[:, :, L:LP].bitcast(F32), 0.0)
            V.memset(nT_lo[:, :, L:LP].bitcast(F32), 0.0)
            V.memset(rowbuf[:, :, 2 * D:], 0.0)
            ve.wait_ge(pool_const, 7)
            V.tensor_copy(token_of[:, :], iot[:, 0:NT])
            V.tensor_copy(rev[:, :], iot[:, 8:8 + E])
            V.tensor_copy(eoff[:, :], iot[:, 16:16 + E])
            V.tensor_copy(cnt[:, :], iot[:, 16:16 + E])
            V.tensor_copy(slotf[:, :], iot[0:1, 32:32 + N_SLOTS]).then_inc(dve_const, 1)
            ve.wait_ge(dve_const, 4)
            V.tensor_scalar(slot_rows[:, :], slotf[:, :], float(SLOT), None, ALU.mult)
            V.tensor_tensor(upto[:, :, :], slotf[:, 0:E].unsqueeze(2).to_broadcast([1, E, E]),
                            slotf[:, 0:E].unsqueeze(1).to_broadcast([1, E, E]), ALU.is_ge)
            V.memset(rsum[:, :, :], 0.0).then_inc(dve_const, 1)
            ve.wait_ge(bias_landed, 16)
            V.tensor_scalar(bias2[:, :], bias2[:, :], 2.0, None, ALU.mult).then_inc(bias_doubled, 1)

            def low_halves(chunks):
                for n in chunks:
                    i, c = divmod(n, 2)
                    cols = slice(i * H * HD, (i + 1) * H * HD)
                    ve.wait_ge(w_hi_made, n + 1)
                    V.tensor_tensor(wq_lo[:, c, cols], wq_raw[:, c, cols], wq_hi[:, c, cols].bitcast(F32),
                                    ALU.subtract).then_inc(w_lo_made, 1)

            def take(unit, b):
                kind, index, rel = unit
                src = bank_of(unit)
                if kind in ("k", "v", "nT2"):
                    return
                bb = b + rel
                ve.wait_ge(pe_done[kind], count_of(kind, index, bb))
                if kind == "q":
                    V.tensor_copy(qz[HD:, index % 4, 1, :], src[HD:, 0:LP]).then_inc(q_taken_dve, 1)
                elif kind == "nT":
                    cols = slice(index * TP, (index + 1) * TP)
                    ve.wait_ge(nT_hi_taken, count_of(kind, index, bb))
                    V.tensor_tensor(nT_lo[:, :, cols], src[:, 0:2 * TP].rearrange("p (c t) -> p c t", c=2),
                                    nT_hi[:, :, cols].bitcast(F32), ALU.subtract).then_inc(nT_lo_taken, 1)
                elif kind == "conv":
                    ve.wait_ge(xsum_step, nth(bb, 2, 1))
                    V.scalar_tensor_tensor(out=u[:, index, :], in0=xsum[:, index, :], scalar=0.5,
                                           in1=src[0:TP, 0:D], op0=ALU.mult, op1=ALU.add).then_inc(conv_taken, 1)
                    ve.wait_ge(conv_taken, nth(bb, NT, index))
                    V.bn_stats(st6[:, 0, index, :], u[:, index, :]).then_inc(stats_made, 1)
                elif kind == "wout":
                    if index == 0:
                        ve.wait_ge(rows_sent, bb * (NT * 16) + SPARE * 16)
                    o = (bb % 2) * (NT * D) + index * D
                    V.tensor_tensor(rowbuf[:, index, D:2 * D], src[0:TP, 0:D], h1[:, bass.ds(o, D)], ALU.add)\
                        .then_inc(wout_taken, 1)
                    ve.wait_ge(wout_taken, nth(bb, NT, index))
                    V.bn_stats(st6[:, 2, index, :], rowbuf[:, index, D:2 * D]).then_inc(stats_out, 1)
                elif kind == "logits":
                    V.tensor_tensor(lg[:, :, :], src[0:TP, 0:NT * E].rearrange("p (t e) -> p t e", t=NT),
                                    rb[0:TP, :].unsqueeze(1).to_broadcast([TP, NT, E]), ALU.add)\
                        .then_inc(logits_taken, 1)
                elif kind == "rank":
                    V.tensor_tensor(r1[:, :, :], src[0:TP, 0:NT * E].rearrange("p (t e) -> p t e", t=NT),
                                    cnt[0:TP, :].unsqueeze(1).to_broadcast([TP, NT, E]), ALU.add)
                    V.tensor_tensor(cnt_new[:, :], cnt[:, :], src[:, NT * E:(NT + 1) * E], ALU.add)\
                        .then_inc(rank_taken, 1)

            def norm_stats(which, batch, stats, n, made):
                ve.wait_ge(stats, n)
                stand_alone(ve)
                for t in range(NT):
                    V.bn_aggr(mv[:, which, t, :], st6[:, which, t, :]).then_inc(aggr_made[which], 1)
                ve.wait_ge(aggr_made[which], nth(batch, NT, NT - 1))
                V.tensor_scalar(veps[:, which, :], mv[:, which, :, 1], EPS, None, ALU.add).then_inc(made, 1)

            def normalise(dst, src, which):
                for t in range(NT):
                    last = V.tensor_scalar(dst[:, t, 0:D], src(t), mv[:, which, t, 0:1], rstd[:, which, t:t + 1],
                                           ALU.subtract, ALU.mult)
                return last

            def choose(bb):
                def link(ins, k):
                    ins.then_inc(route_step, 1)
                    ve.wait_ge(route_step, nth(bb, 4, k))
                ve.wait_ge(logits_taken, nth(bb, 1, 0))
                link(V.tensor_reduce(rm[:, 0, :], lg[:, :, :], AX.X, ALU.max), 0)
                link(V.tensor_tensor(r1[:, :, :], lg[:, :, :], rm[:, 0, :].unsqueeze(2).to_broadcast([TP, NT, E]),
                                     ALU.is_equal), 1)
                revb = rev[0:TP, :].unsqueeze(1).to_broadcast([TP, NT, E])
                link(V.tensor_tensor(r2[:, :, :], r1[:, :, :], revb, ALU.mult), 2)
                link(V.tensor_reduce(rm[:, 1, :], r2[:, :, :], AX.X, ALU.max), 3)
                V.tensor_tensor(onehot[:, :, :], revb, rm[:, 1, :].unsqueeze(2).to_broadcast([TP, NT, E]),
                                ALU.is_equal).then_inc(onehot_made, 1)

            def place_rows(bb):
                ve.wait_ge(rank_taken, nth(bb, 1, 0))
                V.tensor_copy(cnt[:, :], cnt_new[:, :]).then_inc(cnt_made, 1)
                V.tensor_tensor(r2[:, :, :], r1[:, :, :], onehot[:, :, :], ALU.mult).then_inc(place_step, 1)
                V.tensor_copy(rowbuf[:, :, 2 * D].bitcast(I32), token_of[0:TP, :]).then_inc(place_step, 1)
                ve.wait_ge(place_step, nth(bb, 3, 1))
                V.tensor_reduce(rm[:, 2, :], r2[:, :, :], AX.X, ALU.add).then_inc(place_step, 1)
                V.tensor_scalar(token_of[:, :], token_of[:, :], float(L), None, ALU.add).then_inc(token_made, 1)
                ve.wait_ge(place_step, nth(bb, 3, 2))
                V.tensor_copy(pos[:, :], rm[:, 2, :]).then_inc(pos_made, 1)
                ve.wait_ge(cnt_made, nth(bb, 1, 0))
                ve.wait_ge(token_made, nth(bb, 1, 0))

            def mask_max(h, b):
                ve.wait_ge(scores_done, nth(b, H, h))
                stand_alone(ve)
                for t in range(NT):
                    o, n = score_cols[t]
                    bk, bo = score_bank[t]
                    V.tensor_tensor_reduce(out=probs[:, h % 4, o:o + n], in0=bk[0:TP, bo:bo + n],
                                           in1=mask[0:TP, L - n:L], scale=1.0, scalar=-3e38, op0=ALU.add,
                                           op1=ALU.max, accum_out=rmax[:, h % 4, t:t + 1]).then_inc(masked, 1)
                ve.wait_ge(masked, nth(b, NT * H, NT * h + 2))
                V.tensor_scalar(nmax[:, h % 4, :], rmax[:, h % 4, :], -HD ** -0.5, None, ALU.mult)\
                    .then_inc(nmax_made, 1)

            def divide(h, b):
                ve.wait_ge(exp_done, nth(b, H, h))
                V.reciprocal(rinv[:, h % 4, :], rsum[:, h % 4, :]).then_inc(rinv_made, 1)
                ve.wait_ge(rinv_made, nth(b, H, h))
                for t in range(NT):
                    o, n = score_cols[t]
                    s = probs[:, h % 4, o:o + n]
                    last = V.tensor_scalar(s, s, rinv[:, h % 4, t:t + 1], None, ALU.mult)
                last.then_inc(probs_ready, 1)

            def probs_T(h, b):
                ve.wait_ge(probsT_done, nth(b, H, h))
                V.tensor_copy(probsT[:, h % 2, L:2 * L], tB[0:TP, 0:L]).then_inc(probsT_dve, 1)

            def emit(b, rels):
                for p in range(NP):
                    pp, pb, prel = before(p, b, 1)
                    vp, vb, vrel = before(p, b, 2)
                    places = UNITS[p]
                    if 0 in rels:
                        mask_max(2 * p, b)
                    if vrel in rels:
                        ve.wait_ge(pv_done, nth(vb, NP, vp))
                        ve.wait_ge(aT_hi_made, nth(vb, NP, vp))
                        V.tensor_tensor(aT_lo[:, vp, :], pv[:, 0:L], aT_hi[:, vp, :].bitcast(F32), ALU.subtract)\
                            .then_inc(aT_lo_made, 1)
                    for un in units_of(places[0], rels):
                        take(un, b)
                    if prel in rels:
                        probs_T(2 * pp, pb)
                    for un in units_of(places[1], rels):
                        take(un, b)
                    if prel in rels:
                        divide(2 * pp + 1, pb)
                    if 0 in rels:
                        mask_max(2 * p + 1, b)
                    if p == 4 and 1 in rels:
                        ve.wait_ge(rstd_made, nth(b + 1, 2, 0))
                        normalise(z, lambda t: u[:, t, :], 0).then_inc(normed, 1)
                        if 0 not in rels:
                            low_halves(range(1, 4))
                    if p == 6 and 1 in rels:
                        ve.wait_ge(rstd_made, nth(b + 1, 2, 1))
                        normalise(n1, lambda t: h1[:, bass.ds(((b + 1) % 2) * (NT * D) + t * D, D)], 1)\
                            .then_inc(normed, 1)
                    if p == 7 and 0 not in rels and 1 in rels:
                        low_halves(range(5, 6))
                        ve.wait_ge(router_landed, 32)
                    for un in units_of(places[2], rels):
                        take(un, b)
                    if prel in rels:
                        probs_T(2 * pp + 1, pb)
                    for un in units_of(places[3], rels):
                        take(un, b)
                    if 0 in rels:
                        divide(2 * p, b)
                    if p == 1 and -1 in rels:
                        norm_stats(2, b - 1, stats_out, nth(b - 1, NT, NT - 1), veps_out)
                    if p == 2 and -1 in rels:
                        ve.wait_ge(rstd_out, nth(b - 1, 1, 0))
                        normalise(rowbuf, lambda t: rowbuf[:, t, D:2 * D], 2).then_inc(normed_out, 1)
                    if p == 3 and 1 in rels:
                        norm_stats(0, b + 1, stats_made, nth(b + 1, 2 * NT, NT - 1), veps_made)
                        if 0 not in rels:
                            low_halves(range(1))
                    if p == 5 and -1 in rels:
                        choose(b - 1)
                    if p == 5 and 1 in rels:
                        ve.wait_ge(affine, nth(b + 1, 2, 1))
                        for t in range(NT):
                            V.bn_stats(st6[:, 1, t, :], h1[:, bass.ds(((b + 1) % 2) * (NT * D) + t * D, D)])\
                                .then_inc(stats_made, 1)
                        norm_stats(1, b + 1, stats_made, nth(b + 1, 2 * NT, 2 * NT - 1), veps_made)
                        if 0 not in rels:
                            low_halves(range(4, 5))
                    if p == 7 and -1 in rels:
                        place_rows(b - 1)

            ve.wait_ge(pool_const, N_CONST)
            phase_one(ve, emit)

            steps = [0]

            def step(ins):
                steps[0] += 1
                ins.then_inc(table_step, 1)

            def settle():
                ve.wait_ge(table_step, steps[0])

            NS = N_SLOTS
            c8 = lambda i: tb[:, i, 0:E]
            by_slot = lambda i: tb[:, i, 32:32 + NS]
            ends = tb[:, 3, 0:E]
            ve.wait_ge(cnt_made, B)
            V.tensor_copy(padrow[:, :], cnt[0:1, :]).then_inc(padrow_made, 1)
            step(V.tensor_tensor(c8(0), cnt[0:1, :], eoff[0:1, :], ALU.subtract))
            settle()
            step(V.tensor_scalar(tbi[:, 0, 0:E], c8(0), float(SLOT - 1), None, ALU.add))
            settle()
            step(V.tensor_scalar(tbi[:, 1, 0:E], tbi[:, 0, 0:E], 7, None, ALU.arith_shift_right))
            settle()
            step(V.tensor_copy(c8(1), tbi[:, 1, 0:E]))
            settle()
            step(V.tensor_scalar(c8(2), c8(1), float(-SLOT), float(STRIDE), ALU.mult, ALU.add))
            step(V.tensor_tensor(ends8[:, :, :], upto[:, :, :], c8(1).unsqueeze(1).to_broadcast([1, E, E]), ALU.mult))
            settle()
            step(V.tensor_reduce(ends, ends8[:, :, :], AX.X, ALU.add))
            settle()
            step(V.tensor_tensor(reached[:, :, :], slotf[:, :].unsqueeze(2).to_broadcast([1, NS, E]),
                                 ends.unsqueeze(1).to_broadcast([1, NS, E]), ALU.is_ge))
            settle()
            step(V.tensor_tensor(jump[:, :, :], reached[:, :, :], c8(2).unsqueeze(1).to_broadcast([1, NS, E]), ALU.mult))
            settle()
            step(V.tensor_reduce(by_slot(1), jump[:, :, :], AX.X, ALU.add))
            settle()
            V.tensor_tensor(table[:, 2, 0:NS], by_slot(1), slot_rows[:, :], ALU.add).then_inc(slot_rows_made, 1)
            step(V.tensor_reduce(by_slot(0), reached[:, :, :], AX.X, ALU.add))
            step(V.tensor_scalar(endw[:, :], ends, 1.0, None, ALU.add))
            settle()
            step(V.tensor_scalar(by_slot(2), by_slot(0), float(E - 1), None, ALU.min))
            settle()
            step(V.tensor_scalar(table[:, 0, 0:NS], by_slot(2), 1.0, None, ALU.add))
            step(V.tensor_scalar(by_slot(0), by_slot(2), 3.0, -3.0, ALU.is_ge, ALU.mult))
            step(V.tensor_scalar(by_slot(1), by_slot(2), 6.0, -3.0, ALU.is_ge, ALU.mult))
            settle()
            step(V.tensor_tensor(by_slot(3), by_slot(0), by_slot(1), ALU.add))
            settle()
            step(V.tensor_tensor(by_slot(0), by_slot(2), by_slot(3), ALU.add))
            settle()
            step(V.tensor_scalar(table[:, 1, 0:NS], by_slot(0), float(BLOCK), None, ALU.mult))
            settle()
            ve.sem_inc(table_made, 1)
            ve.sem_inc(slots_done, 1)

            def block_of(s):
                return ve.value_load(table[0:1, 1, bass.ds(s, 1)], min_val=0, max_val=(N_EW - 1) * BLOCK)

            B1 = 2 * WCOLS

            def low_xsT(s, par):
                ve.wait_ge(xsT_hi_taken, s + 1)
                V.tensor_tensor(xsT_lo[:, 2 * par:2 * par + 2, :], pv[:, 0:256].rearrange("p (c t) -> p c t", c=2),
                                xsT_hi[:, 2 * par:2 * par + 2, :].bitcast(F32), ALU.subtract).then_inc(xsT_lo_taken, 1)

            def low_actT(s, j):
                ve.wait_ge(actT_hi_taken, 2 * s + j + 1)
                V.tensor_tensor(actT_lo[:, j, :], (tA, tB)[j][:, :], actT_hi[:, j, :].bitcast(F32), ALU.subtract)\
                    .then_inc(actT_lo_taken, 1)

            def up(s, j, buf):
                if j == 0:
                    e1 = ve.value_load(table[0:1, 0, bass.ds(s, 1)], min_val=1, max_val=E)
                    ve.wait_ge(weights_ready, e1)
                ve.wait_ge(pe_up, 4 * s + 2 * j + 1)
                V.tensor_tensor(gs[:, j, :], up_bank[2 * j][:, :], ew[:, bass.ds(buf + (B1 + HID + 512 * j), 512)],
                                ALU.add).then_inc(g_added, 1)
                ve.wait_ge(pe_up, 4 * s + 2 * j + 2)
                V.tensor_tensor(as_[:, j, :], up_bank[2 * j + 1][:, :], ew[:, bass.ds(buf + (B1 + 512 * j), 512)],
                                ALU.add).then_inc(a_added, 1)
                ve.wait_ge(a_added, 2 * s + j + 1)
                ve.wait_ge(gated, 2 * s + j + 1)
                V.tensor_tensor(act[:, j, :], as_[:, j, :], sg[:, j, :], ALU.mult).then_inc(act_ready, 1)

            def finish(s, par, n, buf):
                ve.wait_ge(pe_y, s + 1)
                ve.wait_ge(hs_landed[par], n * 16)
                V.tensor_tensor(ys[:, :], y_bank[:, 0:D], ew[:, bass.ds(buf + (B1 + 2 * HID), D)], ALU.add).then_inc(y_biased, 1)
                ve.wait_ge(y_biased, s + 1)
                if not (isinstance(s, int) and s < 2):
                    ve.wait_ge(out_sent[par], 16 * (n - 1))
                V.tensor_copy(ids[:, par:par + 1], hs[:, par, D:D + 1].bitcast(U32)).then_inc(slots_done, 1)
                V.tensor_tensor(yo[:, par, :], ys[:, :], hs[:, par, 0:D], ALU.add).then_inc(y_ready, 1)

            def slot(s, par, pair):
                prev, cur, nxt, _ = steps_of(s)
                if cur:
                    buf = block_of(s)
                    up(s, 0, buf)
                if prev:
                    low_actT(s - 1, 1)
                if nxt:
                    low_xsT(s + 1, 1 - par)
                if cur:
                    up(s, 1, buf)
                if cur:
                    low_actT(s, 0)
                if prev:
                    finish(s - 1, 1 - par, pair + par, block_of(s - 1))

            low_xsT(0, 0)
            phase_two(ve, slot)

        @block.tensor
        def _(pe):
            def mm(o, l, r, start, stop):
                return nc.tensor.matmul(o, l, r, start=start, stop=stop)

            def mm3(o, lh, ll, rh, rl, start, stop):
                mm(o, lh, rh, start, False)
                mm(o, lh, rl, False, False)
                return mm(o, ll, rh, False, stop)

            def wout_part(index, bb, pairs):
                dst = bank_of(("wout", index, -1))
                tok = slice(index * TP, (index + 1) * TP)
                if isinstance(bb, int) and bb == 0:
                    pe.wait_ge(wo_halved, 2)
                for c in pairs:
                    if c == pairs[0] or c == NP - 1:
                        pe.wait_ge(aT_lo_made, nth(bb, NP, max(c, NP - 3)))
                    last = mm3(dst[0:TP, 0:D], aT_hi[:, c, tok], aT_lo[:, c, tok], wo_hi[:, c, :], wo_lo[:, c, :],
                               c == 0, c == NP - 1)
                return last

            def free_bank(un, b):
                i = ORDER.index(un)
                dst = bank_of(un)
                for back in range(1, 2 * len(ORDER)):
                    j = i - back
                    it = b if j >= 0 else b - 1
                    other = ORDER[j % len(ORDER)]
                    if bank_of(other) is not dst:
                        continue
                    if isinstance(b, int) and not 0 <= it + other[2] < B:
                        if it < -1:
                            break
                        continue
                    for s_ in taken[other[0]]:
                        pe.wait_ge(s_, count_of(other[0], other[1], it + other[2]))
                    break

            def unit(un, b):
                kind, index, rel = un
                dst = bank_of(un)
                bb = b + rel
                if kind == "wout" and isinstance(b, int) and b == B:
                    wout_part(index, bb, range(NP - 2, NP)).then_inc(pe_done[kind], 1)
                    return
                free_bank(un, b)
                if kind == "wout":
                    last = wout_part(index, bb, range(NP))
                elif kind in ("q", "k", "v"):
                    pe.wait_ge(nT_lo_taken, nth(bb, NT, NT - 1))
                    if isinstance(b, int) and b < 0:
                        pe.wait_ge(w_lo_made, {"q": 2, "k": 4, "v": 6}[kind])
                if kind in ("q", "k"):
                    o = index * 2 * HD + (H * HD if kind == "k" else 0)
                    for c in range(2):
                        last = mm3(dst[:, 0:LP], wq_hi[:, c, o:o + 128], wq_lo[:, c, o:o + 128],
                                   nT_hi[:, c, :], nT_lo[:, c, :], c == 0, c == 1)
                elif kind == "v":
                    g, t = index
                    o = 2 * H * HD + g * D
                    tok = slice(t * TP, (t + 1) * TP)
                    for c in range(2):
                        last = mm3(dst[0:TP, 0:D], nT_hi[:, c, tok], nT_lo[:, c, tok],
                                   wq_hi[:, c, o:o + D], wq_lo[:, c, o:o + D], c == 0, c == 1)
                elif kind == "conv":
                    pe.wait_ge(xT_landed, nth(bb, 1, 0) * 16)
                    if isinstance(b, int) and b < 0:
                        pe.wait_ge(wc_landed, 16)
                    for c in range(4):
                        last = mm(dst[0:TP, 0:D], xT_in[:, c, index * TP:(index + 1) * TP], wc[:, c, :],
                                  c == 0, c == 3)
                elif kind in ("nT", "nT2"):
                    if kind == "nT":
                        pe.wait_ge(normed, nth(bb, 2, 1))
                        if isinstance(b, int) and b < 0 and index == 0:
                            pe.wait_ge(pool_const, N_CONST)
                            pe.wait_ge(dve_const, 5)
                            pe.wait_ge(router_landed, 32)
                    else:
                        pe.wait_ge(normed_out, nth(bb, 1, 0))
                    src = n1 if kind == "nT" else rowbuf
                    for c in range(2):
                        last = nc.tensor.transpose(dst[:, c * TP:(c + 1) * TP], src[:, index, c * 128:(c + 1) * 128],
                                                   ident[0:TP, 0:TP])
                elif kind == "logits":
                    pe.wait_ge(nT2_taken, nth(bb, NT, NT - 1))
                    for t in range(NT):
                        for c in range(2):
                            last = mm(dst[0:TP, t * E:(t + 1) * E], n2T[:, c, t * TP:(t + 1) * TP], rw[:, c, :],
                                      c == 0, c == 1)
                elif kind == "rank":
                    pe.wait_ge(onehot_made, nth(bb, 1, 0))
                    for t in range(NT + 1):
                        o = dst[:, t * E:(t + 1) * E]
                        for t2 in range(min(t, NT)):
                            last = mm(o, ones[0:TP, :], onehot[:, t2, :], t2 == 0, t == NT and t2 == NT - 1)
                        if t < NT:
                            last = mm(o, tri[0:TP, :], onehot[:, t, :], t == 0, True)
                last.then_inc(pe_done[kind], 1)

            def scores(h, b):
                p = h // 2
                pe.wait_ge(q_taken_act, nth(b, NP, p))
                pe.wait_ge(q_taken_dve, nth(b, NP, p))
                pe.wait_ge(k_taken, nth(b, NP, p))
                if not (isinstance(b, int) and b == 0 and h == 0):
                    pe.wait_ge(masked, b * (NT * H) + NT * h)
                for t in (0, 2, 1):
                    bk, o = score_bank[t]
                    n = (t + 1) * TP
                    last = mm(bk[0:TP, o:o + n], qz[:, p % 4, h % 2, t * TP:n], kk[:, p % 4, 0:n], True, True)
                last.then_inc(scores_done, 1)

            def transposes(h, b):
                pe.wait_ge(probs_ready, nth(b, H, h))
                if not (isinstance(b, int) and b == 0 and h == 0):
                    pe.wait_ge(probsT_act, b * H + h)
                    pe.wait_ge(probsT_dve, b * H + h)
                for j in range(NT):
                    for t in range(j, NT):
                        bk, o = ((tA, t * TP), (tB, (t - 1) * TP), (tB, 2 * TP))[j]
                        c = score_cols[t][0] + j * TP
                        last = nc.tensor.transpose(bk[0:TP, o:o + TP], probs[:, h % 4, c:c + TP], ident[0:TP, 0:TP])
                last.then_inc(probsT_done, 1)

            def values(p, b):
                pe.wait_ge(probsT_act, nth(b, H, 2 * p + 1))
                pe.wait_ge(probsT_dve, nth(b, H, 2 * p + 1))
                pe.wait_ge(v_taken, nth(b, NG * NT, p // 2 * NT + 2))
                if not (isinstance(b, int) and b == 0 and p == 0):
                    pe.wait_ge(aT_lo_made, b * NP + p)
                for j, (o, n, first) in enumerate(((0, L, 0), (L, 2 * TP, TP), (L + 2 * TP, TP, 2 * TP))):
                    for a in range(2):
                        c = (p % 2) * 2 * HD + a * HD
                        last = nc.tensor.matmul(pv[a * HD:(a + 1) * HD, first:L], vv[:, p // 2 % 2, j, c:c + HD],
                                                probsT[:, a, o:o + n], start=(j == 0), stop=(j == NT - 1))
                last.then_inc(pv_done, 1)

            def emit(b, rels):
                for p in range(NP):
                    pp, pb, prel = before(p, b, 1)
                    vp, vb, vrel = before(p, b, 2)
                    places = UNITS[p]
                    if 0 in rels:
                        scores(2 * p, b)
                    if p == 0 and 0 not in rels and -1 in rels:
                        for t in range(NT):
                            free_bank(("wout", t, -1), b)
                            wout_part(t, b - 1, range(NP - 2))
                    if vrel in rels:
                        values(vp, vb)
                    for un in units_of(places[0], rels):
                        unit(un, b)
                    if prel in rels:
                        transposes(2 * pp, pb)
                    for un in units_of(places[1], rels):
                        unit(un, b)
                    if 0 in rels:
                        scores(2 * p + 1, b)
                    for un in units_of(places[2], rels):
                        unit(un, b)
                    if prel in rels:
                        transposes(2 * pp + 1, pb)
                    for un in units_of(places[3], rels):
                        unit(un, b)

            phase_one(pe, emit)

            pe.wait_ge(table_made, 1)

            def weights(s):
                return pe.value_load(table[0:1, 1, bass.ds(s, 1)], min_val=0, max_val=(N_EW - 1) * BLOCK)

            def w_halves(w, o, n):
                return [ew[:, bass.ds(w + (half * WCOLS + o), n)].bitcast(F32R) for half in range(2)]

            def transpose_x(par, n):
                pe.wait_ge(xs_landed[par], n * 16)
                for c in range(2):
                    last = nc.tensor.transpose(pv[:, c * 128:(c + 1) * 128], xs[:, par, c * 128:(c + 1) * 128], ident[:, :])
                last.then_inc(pe_xsT, 1)

            def up(s, j, par, w):
                if j == 0:
                    e1 = pe.value_load(table[0:1, 0, bass.ds(s, 1)], min_val=1, max_val=E)
                    pe.wait_ge(weights_ready, e1)
                    pe.wait_ge(xsT_lo_taken, s + 1)
                for i, col in enumerate((HID + 512 * j, 512 * j)):
                    if not (isinstance(s, int) and s == 0):
                        pe.wait_ge((g_added, a_added)[i], 2 * s + j - 1)
                    for c in range(2):
                        o = c * 2 * HID + col
                        last = mm3(up_bank[2 * j + i][:, :], xsT_hi[:, 2 * par + c, :], xsT_lo[:, 2 * par + c, :],
                                   *w_halves(w, o, 512),
                                   c == 0, c == 1)
                    last.then_inc(pe_up, 1)

            def transpose_act(s, j):
                pe.wait_ge(act_ready, 2 * s + j + 1)
                if not (isinstance(s, int) and s == 0):
                    pe.wait_ge(actT_lo_taken, 2 * s + j - 1)
                for c in range(4):
                    cols = slice(c * 128, (c + 1) * 128)
                    last = nc.tensor.transpose((tA, tB)[j][:, cols], act[:, j, cols], ident[:, :])
                last.then_inc(pe_actT, 1)

            def down(s, j, w):
                pe.wait_ge(actT_lo_taken, 2 * s + j + 1)
                if j == 0 and not (isinstance(s, int) and s == 0):
                    pe.wait_ge(y_biased, s)
                for c in range(4):
                    cols = slice(c * 128, (c + 1) * 128)
                    o = W1C + (4 * j + c) * D
                    last = mm3(y_bank[:, 0:D], actT_hi[:, j, cols], actT_lo[:, j, cols],
                               *w_halves(w, o, D),
                               j == 0 and c == 0, j == 1 and c == 3)
                if j == 1:
                    last.then_inc(pe_y, 1)

            def slot(s, par, pair):
                prev, cur, nxt, _ = steps_of(s)
                if cur:
                    w = weights(s)
                    up(s, 0, par, w)
                if prev:
                    w_prev = weights(s - 1)
                    transpose_act(s - 1, 1)
                if nxt:
                    transpose_x(1 - par, pair + par + 1)
                if prev:
                    down(s - 1, 0, w_prev)
                if cur:
                    up(s, 1, par, w)
                if cur:
                    transpose_act(s, 0)
                if prev:
                    down(s - 1, 1, w_prev)

            transpose_x(0, 1)
            phase_two(pe, slot)


INS = ["xT", "x", "conv_w", "conv_b", "gamma", "beta", "w_qkv", "w_out", "router_w", "router_b",
       "w1", "b1", "w2", "b2"]


def kernel(x, L0_tok_conv_w, L0_tok_conv_b, L0_tok_ln_gamma, L0_tok_ln_beta, L0_attn_W_qkv, L0_attn_W_out,
           L0_ffn_router_w, L0_ffn_router_b, L0_ffn_w1, L0_ffn_b1, L0_ffn_w2, L0_ffn_b2):
    import numpy as np
    import concourse.bacc as bacc
    from concourse.bass_utils import run_bass_kernel_spmd

    x = np.asarray(x)
    pairs = x.reshape(T, 2 * D)
    values = {
        "xT": pairs.T.reshape(4, 128, T).transpose(1, 0, 2),
        "x": pairs.reshape(B, NT, TP, 2 * D),
        "conv_w": np.asarray(L0_tok_conv_w).transpose(2, 1, 0).reshape(4, 128, D).transpose(1, 0, 2),
        "conv_b": L0_tok_conv_b, "gamma": L0_tok_ln_gamma, "beta": L0_tok_ln_beta,
        "w_qkv": L0_attn_W_qkv, "w_out": L0_attn_W_out,
        "router_w": L0_ffn_router_w, "router_b": L0_ffn_router_b,
        "w1": L0_ffn_w1, "b1": L0_ffn_b1, "w2": L0_ffn_w2, "b2": L0_ffn_b2,
    }
    nc = bacc.Bacc("TRN2", target_bir_lowering=False, num_devices=1)
    arrays, args = {}, []
    for name in INS:
        a = np.ascontiguousarray(values[name])
        arrays[f"in_{name}"] = a
        args.append(nc.dram_tensor(f"in_{name}", a.shape, mybir.dt.from_np(a.dtype), kind="ExternalInput").ap())
    args.append(nc.dram_tensor("out_rows", (T, D), F32, kind="ExternalOutput").ap())
    tower(nc, *args)
    r = run_bass_kernel_spmd(nc, [arrays], core_ids=[0])
    return r.results[0]["out_rows"].reshape(B, L, D)
```

```python
from contextlib import ExitStack

import concourse.bass as bass
from concourse import mybir
from concourse.alu_op_type import AluOpType as ALU

ACT = mybir.ActivationFunctionType
AX = mybir.AxisListType
F32 = mybir.dt.float32
F32R = mybir.dt.float32r
BF16 = mybir.dt.bfloat16
I32 = mybir.dt.int32
U32 = mybir.dt.uint32

B, L, D = 8, 375, 256
T = B * L
TP, NT = 125, 3
LP = L + 1
H, HD = 16, 64
NP = H // 2
NG = NP // 2
HID = 1024
E = 8
SLOT = 128
STRIDE = T + SLOT
N_SLOTS = (T + E * (SLOT - 1)) // SLOT
MIN_SLOTS = -(-T // SLOT)
SPARE = N_SLOTS - MIN_SLOTS
ROWS = E * STRIDE + SPARE * SLOT
ROW = 516
NO_TOKEN = 2 * T
EPS = 1e-5
MASKED = -1e30

W1C = 2 * 2 * HID
WCOLS = W1C + HID // 128 * D
N_EW = 3
BLOCK = 2 * WCOLS + 2 * HID + D
CHUNK = 512
N_CHUNKS = WCOLS // CHUNK
N_SPLIT = 4

UNITS = [
    [[("q", 1, 0)], [], [("k", 1, 0), ("q", 2, 0), ("v", (0, 2), 0)], [("k", 2, 0)]],
    [[("wout", 0, -1)], [], [("wout", 1, -1)], [("wout", 2, -1)]],
    [[], [("q", 3, 0), ("conv", 0, 1)], [("k", 3, 0)], [("conv", 1, 1), ("conv", 2, 1)]],
    [[], [("q", 4, 0), ("v", (1, 0), 0)], [("k", 4, 0), ("v", (1, 1), 0)], [("q", 5, 0), ("v", (1, 2), 0)]],
    [[], [("nT2", 0, -1), ("v", (2, 0), 0), ("nT2", 1, -1)], [("k", 5, 0), ("nT2", 2, -1)], [("v", (2, 1), 0)]],
    [[("q", 6, 0)], [("v", (2, 2), 0)], [("k", 6, 0)], [("logits", 0, -1), ("v", (3, 0), 0)]],
    [[("q", 7, 0)], [("k", 7, 0)], [("v", (3, 1), 0), ("nT", 0, 1)], [("v", (3, 2), 0), ("nT", 1, 1), ("nT", 2, 1)]],
    [[], [("rank", 0, -1)], [("q", 0, 1), ("k", 0, 1)], [("v", (0, 0), 1), ("v", (0, 1), 1)]],
]
ORDER = [u for pair in UNITS for place in pair for u in place]
PER_BATCH = {"q": NP, "k": NP, "v": NG * NT, "wout": NT, "nT2": NT, "conv": NT, "nT": NT,
             "logits": 1, "rank": 1}
N_AUX = 3


def event(kind, index):
    return index[0] * NT + index[1] if kind == "v" else index


def tower(nc, xT, x, conv_w, conv_b, gamma, beta, w_qkv, w_out, router_w, router_b,
          w1, b1, w2, b2, out):
    ctx = ExitStack()
    with ctx:
        rows = nc.dram_tensor("token_rows", [ROWS, ROW], F32)
        rows = rows.ap()
        halves = [nc.dram_tensor(f"expert_w_{n}", [E, 128, WCOLS], F32).ap() for n in ("hi", "lo")]

        cursor = [nc.sbuf_base + (-nc.sbuf_base) % 64]

        def at_offset(name, shape, dt, offset):
            return nc.alloc_sbuf_tensor_at(name, shape, dt, offset=offset)

        def size(shape, dt):
            n = 2 if dt == BF16 else 4
            for s in shape[1:]:
                n *= s
            return n + (-n) % 32

        def sb(name, shape, dt=F32):
            o = cursor[0]
            cursor[0] += size(shape, dt)
            return at_offset(name, shape, dt, o)

        def bank(name):
            return ctx.enter_context(nc.psum_tensor(name, [128, 512], F32))

        def sem(name):
            return ctx.enter_context(nc.semaphore(name))

        ident = sb("ident", [128, 128])
        endw = sb("endw", [1, E], I32)
        expert_of = sb("expert_of", [1, E], I32)
        table = sb("table", [1, 3, 32], I32)
        padrow = sb("padrow", [1, E], I32)
        phase_start = cursor[0]

        wq_hi = sb("wq_hi", [128, 2, 3 * H * HD], F32R)
        wq_lo = sb("wq_lo", [128, 2, 3 * H * HD], F32R)
        xT_in = sb("xT_in", [128, 4, L])
        x_in = sb("x_in", [TP, NT, 2 * D])
        x_end = cursor[0]
        wc = sb("wc", [128, 4, D])
        xsum = sb("xsum", [TP, NT, D])
        u = sb("u", [TP, NT, D])
        z = sb("z", [TP, NT, D])
        n1 = sb("n1", [TP, NT, D])
        nT_hi = sb("nT_hi", [128, 2, LP], F32R)
        nT_lo = sb("nT_lo", [128, 2, LP], F32R)
        qz_hi = sb("qz_hi", [128, 2, 2, LP], F32R)
        qz_lo = sb("qz_lo", [128, 2, 2, LP], F32R)
        kk_hi = sb("kk_hi", [128, 2, LP], F32R)
        kk_lo = sb("kk_lo", [128, 2, LP], F32R)
        vv = sb("vv", [TP, 2, NT, D])
        probs = sb("probs", [TP, 4, 2 * L])
        attention_end = cursor[0]
        probsT = sb("probsT", [TP, 2, 2 * L])
        n2T_start = cursor[0]
        n2T = sb("n2T", [128, 2, L])
        wo_hi = sb("wo_hi", [128, NP, D], F32R)
        wo_lo = sb("wo_lo", [128, NP, D], F32R)
        h1 = sb("h1", [TP, 2 * NT * D])
        rw = sb("rw", [128, 2, E])
        bias2 = sb("bias2", [128, D])
        gam = sb("gam", [128, D])
        bet = sb("bet", [128, D])
        rb = sb("rb", [128, E])
        mask = sb("mask", [128, L])
        tri = sb("tri", [128, 128], BF16)
        ones = sb("ones", [128, 128], BF16)
        rev = sb("rev", [128, E])
        token_of = sb("token_of", [128, NT])
        halfs = sb("halfs", [128, NT])
        rowbuf = sb("rowbuf", [TP, NT, ROW])
        cnt = sb("cnt", [128, E])
        eoff = sb("eoff", [128, E])
        iot = sb("iot", [128, 64], I32)
        st6 = sb("st6", [TP, 3, NT, 6])
        mv = sb("mv", [TP, 3, NT, 2])
        veps = sb("veps", [TP, 3, NT])
        rstd = sb("rstd", [TP, 3, NT])
        nmax = sb("nmax", [TP, 4, NT])
        rsum = sb("rsum", [TP, 4, NT])
        rinv = sb("rinv", [TP, 4, NT])
        lg = sb("lg", [TP, NT, E])
        r1 = sb("r1", [TP, NT, E])
        r2 = sb("r2", [TP, NT, E])
        rm = sb("rm", [TP, 4, NT])
        onehot = sb("onehot", [TP, NT, E], BF16)
        pos = sb("pos", [TP, NT], U32)
        cnt_new = sb("cnt_new", [128, E])
        tb = sb("tb", [1, 4, 64])
        tbi = sb("tbi", [1, 2, 64], I32)
        slotf = sb("slotf", [1, N_SLOTS])
        slot_rows = sb("slot_rows", [1, N_SLOTS])
        upto = sb("upto", [1, E, E])
        ends8 = sb("ends8", [1, E, E])
        reached = sb("reached", [1, N_SLOTS, E])
        jump = at_offset("jump", [1, N_SLOTS, E], F32, n2T_start)
        before8 = at_offset("before8", [1, E, E], F32, n2T_start + size([1, N_SLOTS * E], F32))
        through8 = at_offset("through8", [1, E, E], F32, n2T_start + size([1, (N_SLOTS + E) * E], F32))
        attn_start = cursor[0]
        assert x_end - phase_start >= BLOCK * 4 and attention_end - phase_start >= 2 * BLOCK * 4
        aT_hi = sb("aT_hi", [128, NP, L], F32R)
        aT_lo = sb("aT_lo", [128, NP, L], F32R)
        attn_end = cursor[0]
        cursor[0] = attn_start
        wq_raw = sb("wq_raw", [128, 2, 3 * H * HD])
        wo_raw = sb("wo_raw", [128, NP, D])
        pad_start = cursor[0]
        pad = sb("pad", [128, ROW])
        raw = sb("raw", [128, N_SPLIT, CHUNK])
        assert cursor[0] <= nc.sbuf_usable_end, (cursor[0], nc.sbuf_usable_end)
        raw_hi = at_offset("raw_hi", [128, N_SPLIT, CHUNK], F32R, attn_end)
        assert attn_end + N_SPLIT * CHUNK * 4 <= pad_start

        cursor[0] = phase_start
        ew = sb("ew", [128, N_EW * BLOCK])
        xs = sb("xs", [128, 2, D])
        hs = sb("hs", [128, 2, D + 4])
        xsT_hi = sb("xsT_hi", [128, 4, 128], F32R)
        xsT_lo = sb("xsT_lo", [128, 4, 128], F32R)
        gs = sb("gs", [128, 2, 512])
        sg = sb("sg", [128, 2, 512])
        as_ = sb("as_", [128, 2, 512])
        act = sb("act", [128, 2, 512])
        actT_hi = sb("actT_hi", [128, 2, 512], F32R)
        actT_lo = sb("actT_lo", [128, 2, 512], F32R)
        ys = sb("ys", [128, D])
        yo = sb("yo", [128, 2, D])
        ids = sb("ids", [128, 2], U32)
        assert attn_start <= phase_start + N_EW * BLOCK * 4 and cursor[0] <= nc.sbuf_usable_end, cursor[0]

        sA, sB, tA, tB, pv = (bank(n) for n in ("sA", "sB", "tA", "tB", "pv"))
        aux = [bank(f"aux{i}") for i in range(N_AUX)]
        up_bank = [sA, sB, aux[1], aux[2]]
        y_bank = aux[0]

        score_cols = {0: (0, TP), 2: (TP, 3 * TP), 1: (4 * TP, 2 * TP)}
        FEW = 130
        score_bank = {0: (sA, 0), 2: (sA, FEW), 1: (sB, 0)}

        xT_landed, x_landed = sem("xT_landed"), sem("x_landed")
        wc_landed, affine_landed, router_landed = sem("wc_landed"), sem("affine_landed"), sem("router_landed")
        bias_landed, bias_doubled = sem("bias_landed"), sem("bias_doubled")
        wq_landed, wo_landed = [sem(f"wq_landed{i}") for i in range(6)], sem("wo_landed")
        pool_const, dve_const = sem("pool_const"), sem("dve_const")
        w_hi_made, w_lo_made, w_lo_v_made = sem("w_hi_made"), sem("w_lo_made"), sem("w_lo_v_made")
        xsum_step, wo_halved = sem("xsum_step"), sem("wo_halved")
        pe_done = {k: sem(f"pe_{k}") for k in PER_BATCH}
        q_hi_taken, q_lo_taken = sem("q_hi_taken"), sem("q_lo_taken")
        k_hi_taken, k_lo_taken, v_taken = sem("k_hi_taken"), sem("k_lo_taken"), sem("v_taken")
        nT_hi_taken, nT_lo_taken = sem("nT_hi_taken"), sem("nT_lo_taken")
        conv_taken, wout_taken, nT2_taken = sem("conv_taken"), sem("wout_taken"), sem("nT2_taken")
        logits_taken, rank_taken = sem("logits_taken"), sem("rank_taken")
        stats_made, veps_made, rstd_made = sem("stats_made"), sem("veps_made"), sem("rstd_made")
        normed = sem("normed")
        affine = sem("affine")
        scores_done, masked = sem("scores_done"), sem("masked")
        exp_done, rinv_made, probs_ready = sem("exp_done"), sem("rinv_made"), sem("probs_ready")
        probsT_done, probsT_act, probsT_dve = sem("probsT_done"), sem("probsT_act"), sem("probsT_dve")
        pv_done, aT_hi_made, aT_lo_made = sem("pv_done"), sem("aT_hi_made"), sem("aT_lo_made")
        route_step = sem("route_step")
        onehot_made, pos_made, cnt_made = sem("onehot_made"), sem("pos_made"), sem("cnt_made")
        place_step, token_made = sem("place_step"), sem("token_made")
        waits_passed = sem("waits_passed")
        stats_out, veps_out = sem("stats_out"), sem("veps_out")
        rstd_out, normed_out = sem("rstd_out"), sem("normed_out")
        aggr_made = [sem(f"aggr_made{i}") for i in range(3)]
        rows_sent, pads_sent = sem("rows_sent"), sem("pads_sent")
        table_step, table_made = sem("table_step"), sem("table_made")
        padrow_made, slot_rows_made = sem("padrow_made"), sem("slot_rows_made")
        slots_done, weights_ready = sem("slots_done"), sem("weights_ready")
        weights_landed = [sem(f"weights_landed{i}") for i in range(N_EW)]
        out_sent = [sem("out_sent_even"), sem("out_sent_odd")]
        xs_landed = [sem("xs_landed_even"), sem("xs_landed_odd")]
        hs_landed = [sem("hs_landed_even"), sem("hs_landed_odd")]
        pe_xsT, xsT_hi_taken, xsT_lo_taken = sem("pe_xsT"), sem("xsT_hi_taken"), sem("xsT_lo_taken")
        chunk_landed = [sem(f"chunk_landed{i}") for i in range(N_SPLIT)]
        chunk_stored = [sem(f"chunk_stored{i}") for i in range(N_SPLIT)]
        chunk_hi_made, chunk_lo_made = sem("chunk_hi_made"), sem("chunk_lo_made")
        pe_up, g_added, a_added = sem("pe_up"), sem("g_added"), sem("a_added")
        gated, act_ready = sem("gated"), sem("act_ready")
        pe_actT, actT_hi_taken, actT_lo_taken = sem("pe_actT"), sem("actT_hi_taken"), sem("actT_lo_taken")
        pe_y, y_biased, y_ready = sem("pe_y"), sem("y_biased"), sem("y_ready")

        taken = {
            "q": [q_lo_taken], "k": [k_lo_taken], "v": [v_taken], "wout": [wout_taken],
            "nT2": [nT2_taken], "conv": [conv_taken], "nT": [nT_lo_taken],
            "logits": [logits_taken], "rank": [rank_taken],
        }

        def nth(batch, per, k):
            return batch * per + (k + 1)

        def in_place(e, k):
            return e * (N_CHUNKS // N_SPLIT) + (k // N_SPLIT + 1)

        def count_of(kind, index, batch):
            return nth(batch, PER_BATCH[kind], event(kind, index))

        def bank_of(unit):
            return aux[ORDER.index(unit) % N_AUX]

        def before(p, b, n):
            return (p - n, b, 0) if p >= n else (NP + p - n, b - 1, -1)

        def units_of(place, rels):
            return [u_ for u_ in place if u_[2] in rels]

        def phase_one(engine, emit):
            emit(-1, (1,))
            emit(0, (0, 1))
            with engine.Fori(1, B - 1) as b:
                emit(b, (-1, 0, 1))
            emit(B - 1, (-1, 0))
            emit(B, (-1,))

        def phase_two(engine, slot):
            for s in range(4):
                slot(s, s % 2, s // 2)
            pairs = (N_SLOTS - 3) // 2
            with engine.Fori(2, pairs) as i:
                for parity in range(2):
                    slot(2 * i + parity, parity, i)
            for s in range(2 * pairs, N_SLOTS + 1):
                slot(s, s % 2, s // 2)

        def steps_of(s):
            return [not isinstance(s, int) or 0 <= s + k < N_SLOTS for k in (-1, 0, 1, 2)]

        def sum_steps(engine, bb):
            engine.wait_ge(x_landed, nth(bb, 1, 0) * 16)
            engine.tensor_tensor(xsum[:, :, :], x_in[:, :, 0:D], x_in[:, :, D:], ALU.add).then_inc(xsum_step, 1)
            engine.wait_ge(xsum_step, nth(bb, 2, 0))
            engine.tensor_tensor(xsum[:, :, :], xsum[:, :, :],
                                 bias2[0:TP, :].unsqueeze(1).to_broadcast([TP, NT, D]), ALU.add)\
                .then_inc(xsum_step, 1)

        def scale_shift(engine, bb):
            engine.wait_ge(normed, nth(bb, 2, 0))
            engine.tensor_tensor(z[:, :, :], z[:, :, :],
                                 gam[0:TP, :].unsqueeze(1).to_broadcast([TP, NT, D]), ALU.mult).then_inc(affine, 1)
            engine.wait_ge(affine, nth(bb, 2, 0))
            o = (bb % 2) * (NT * D)
            engine.tensor_tensor(h1[:, bass.ds(o, NT * D)].rearrange("p (t d) -> p t d", t=NT), z[:, :, :],
                                 bet[0:TP, :].unsqueeze(1).to_broadcast([TP, NT, D]), ALU.add).then_inc(affine, 1)

        N_CONST = 10

        def stand_alone(engine):
            engine.sem_inc(waits_passed, 1)

        block = ctx.enter_context(nc.Block())

        @block.sync
        def _(sp):
            def load_x(b, first):
                src_T = xT[:, :, 0:L] if first else xT[:, :, bass.ds(b * L, L)]
                src = x[0] if first else x[bass.ds(b, 1)].rearrange("a t p d -> (a t) p d")
                sp.dma_start(xT_in[:, :, :], src_T).then_inc(xT_landed, 16)
                if first:
                    sp.dma_start(wc[:, :, :], conv_w).then_inc(wc_landed, 16)
                sp.dma_start(x_in[:, :, :], src.rearrange("t p d -> p t d")).then_inc(x_landed, 16)

            load_x(0, True)
            sp.dma_start(bias2[:, :], conv_b.partition_broadcast(128)).then_inc(bias_landed, 16)
            wq_rows = w_qkv.rearrange("(c p) n -> c p n", p=128)
            for i in range(3):
                for c in range(2):
                    cols = slice(i * H * HD, (i + 1) * H * HD)
                    sp.dma_start(wq_raw[:, c, cols], wq_rows[c][:, cols]).then_inc(wq_landed[2 * i + c], 16)
                    if i == 0 and c == 1:
                        for dst, src in ((gam, gamma), (bet, beta)):
                            sp.dma_start(dst[:, :], src.partition_broadcast(128)).then_inc(affine_landed, 16)
            sp.dma_start(rb[:, :], router_b.partition_broadcast(128)).then_inc(router_landed, 16)
            sp.dma_start(rw[:, :, :], router_w.rearrange("(c p) e -> p c e", p=128)).then_inc(router_landed, 16)
            sp.dma_start(wo_raw[:, :, :], w_out.rearrange("(c p) n -> p c n", p=128)).then_inc(wo_landed, 16)

            def of_expert(src, e):
                return src[e] if isinstance(e, int) else src[bass.ds(e, 1)].rearrange("a p n -> (a p) n")

            def load_chunk(e, k):
                if not (isinstance(e, int) and e == 0 and k < N_SPLIT):
                    sp.wait_ge(chunk_stored[k % N_SPLIT], in_place(e, k) * 32 - 32)
                    stand_alone(sp)
                n_w1 = W1C // CHUNK
                if k < n_w1:
                    c, i = divmod(k, n_w1 // 2)
                    sp.dma_start(raw[:, k % N_SPLIT, :],
                                 of_expert(w1, e)[c * 128:(c + 1) * 128, i * CHUNK:(i + 1) * CHUNK])\
                        .then_inc(chunk_landed[k % N_SPLIT], 16)
                else:
                    c = (k - n_w1) * (CHUNK // D)
                    sp.dma_start(raw[:, k % N_SPLIT, :].rearrange("p (c n) -> p c n", n=D),
                                 of_expert(w2, e)[c * 128:(c + CHUNK // D) * 128, :]
                                 .rearrange("(c p) n -> p c n", p=128)).then_inc(chunk_landed[k % N_SPLIT], 16)

            def store_chunk(e, k):
                sp.wait_ge(chunk_lo_made, e * N_CHUNKS + (k + 1))
                stand_alone(sp)
                for half, src in zip(halves, (raw_hi, raw)):
                    sp.dma_start(of_expert(half, e)[:, k * CHUNK:(k + 1) * CHUNK],
                                 src[:, k % N_SPLIT, :].bitcast(F32)).then_inc(chunk_stored[k % N_SPLIT], 16)

            def batch(b, nxt, prev):
                if nxt:
                    sp.wait_ge(pe_done["conv"], nth(b, NT, NT - 1))
                    stand_alone(sp)
                    sp.wait_ge(xsum_step, nth(b, 2, 1))
                    stand_alone(sp)
                    load_x(b + 1, False)
                for k in range(N_CHUNKS):
                    load_chunk(b, k)
                    if k >= 2:
                        store_chunk(b, k - 2)
                    elif prev:
                        store_chunk(b - 1, N_CHUNKS - 2 + k)

            batch(0, True, False)
            with sp.Fori(1, B - 1) as b:
                batch(b, True, True)
            batch(B - 1, False, True)
            store_chunk(E - 1, N_CHUNKS - 2)
            store_chunk(E - 1, N_CHUNKS - 1)
            for i in range(N_SPLIT):
                sp.wait_ge(chunk_stored[i], in_place(E, i - N_SPLIT) * 32)

            def load_halves(e, which):
                x = e if e < 2 else sp.value_load(expert_of[0:1, e:e + 1], min_val=0, max_val=E - 1)
                for half in which:
                    o = (e % N_EW) * BLOCK + half * WCOLS
                    if e >= 1 and (e >= N_EW or half):
                        sp.wait_ge(weights_landed[e % N_EW], 64 * (e // N_EW) + 16 * half)
                    sp.dma_start(ew[:, o:o + WCOLS], of_expert(halves[half], x)).then_inc(weights_landed[e % N_EW], 16)

            def load_biases(e):
                x = e if e < 2 else sp.value_load(expert_of[0:1, e:e + 1], min_val=0, max_val=E - 1)
                b1_row, b2_row = ((b_[x] if e < 2 else b_[bass.ds(x, 1)].rearrange("a n -> (a n)")) for b_ in (b1, b2))
                o = (e % N_EW) * BLOCK + 2 * WCOLS
                if e >= 1:
                    sp.wait_ge(weights_landed[e % N_EW], 64 * (e // N_EW) + 32)
                sp.dma_start(ew[:, o:o + 2 * HID], b1_row.partition_broadcast(128))\
                    .then_inc(weights_landed[e % N_EW], 16)
                o += 2 * HID
                sp.dma_start(ew[:, o:o + D], b2_row.partition_broadcast(128)).then_inc(weights_landed[e % N_EW], 16)

            def ready(e):
                sp.wait_ge(weights_landed[e % N_EW], 64 * (e // N_EW + 1))
                sp.sem_inc(weights_ready, 1)

            for kind in ("q", "k", "v"):
                sp.wait_ge(pe_done[kind], B * PER_BATCH[kind])
            load_halves(0, (0,))
            sp.wait_ge(rows_sent, ((B - 1) * NT + SPARE) * 16)
            load_halves(0, (1,))
            load_biases(0)
            sp.wait_ge(pv_done, B * NP)
            load_halves(1, (0,))
            sp.wait_ge(padrow_made, 1)
            for e in range(E):
                r = sp.value_load(padrow[0:1, e:e + 1], min_val=e * STRIDE, max_val=e * STRIDE + T)
                sp.dma_start(rows[bass.ds(r, SLOT), :], pad[:, :]).then_inc(pads_sent, 16)
            ready(0)
            sp.wait_ge(xs_landed[0], 16)
            load_halves(1, (1,))
            load_biases(1)
            sp.wait_ge(table_made, 1)
            sp.wait_ge(rows_sent, (B * NT + SPARE) * 16)
            load_halves(2, (0, 1))
            load_biases(2)
            ready(1)
            ready(2)
            for e in range(N_EW, E):
                done = sp.value_load(endw[0:1, e - N_EW:e - N_EW + 1], min_val=1, max_val=N_SLOTS + 1)
                sp.wait_ge(slots_done, done)
                stand_alone(sp)
                load_halves(e, (0, 1))
                load_biases(e)
                ready(e)
            for par in range(2):
                sp.wait_ge(out_sent[par], 16 * ((N_SLOTS + 1 - par) // 2))

        @block.gpsimd
        def _(pool):
            pool.memset(ident[:, :], 0.0).then_inc(pool_const, 1)
            pool.memset(mask[:, :], 0.0).then_inc(pool_const, 1)
            pool.memset(tri[:, :], 1.0).then_inc(pool_const, 1)
            pool.iota(iot[:, 0:NT], pattern=[[TP, NT]], base=0, channel_multiplier=1).then_inc(pool_const, 1)
            pool.iota(iot[:, 8:8 + E], pattern=[[-1, E]], base=E, channel_multiplier=0).then_inc(pool_const, 1)
            pool.iota(iot[:, 16:16 + E], pattern=[[STRIDE, E]], base=0, channel_multiplier=0).then_inc(pool_const, 1)
            pool.iota(iot[:, 32:63], pattern=[[1, 31]], base=0, channel_multiplier=0).then_inc(pool_const, 1)
            pool.wait_ge(pool_const, 7)
            pool.affine_select(out=ident[:, :], in_=ident[:, :], compare_op=ALU.not_equal, fill=1.0,
                               base=0, pattern=[[-1, 128]], channel_multiplier=1).then_inc(pool_const, 1)
            pool.affine_select(out=mask[:, 2 * TP:], in_=mask[:, 2 * TP:], compare_op=ALU.is_ge, fill=MASKED,
                               base=0, pattern=[[-1, TP]], channel_multiplier=1).then_inc(pool_const, 1)
            pool.affine_select(out=tri[:, :], in_=tri[:, :], compare_op=ALU.is_gt, fill=0.0,
                               base=0, pattern=[[1, 128]], channel_multiplier=-1).then_inc(pool_const, 1)

            def low_half_v(c):
                cols = slice(2 * H * HD, 3 * H * HD)
                pool.wait_ge(w_hi_made, 5 + c)
                pool.tensor_tensor(wq_lo[:, c, cols], wq_raw[:, c, cols], wq_hi[:, c, cols].bitcast(F32),
                                   ALU.subtract).then_inc(w_lo_v_made, 1)

            def split(b, ks, rels):
                for k in ks if 0 in rels else ():
                    pool.wait_ge(chunk_hi_made, b * N_CHUNKS + (k + 1))
                    i = k % N_SPLIT
                    pool.tensor_tensor(raw[:, i, :].bitcast(F32R), raw[:, i, :], raw_hi[:, i, :].bitcast(F32),
                                       ALU.subtract).then_inc(chunk_lo_made, 1)

            def emit(b, rels):
                first = isinstance(b, int) and b < 0
                if 1 in rels and not first:
                    pool.wait_ge(conv_taken, nth(b, NT, NT - 1))
                    sum_steps(pool, b + 1)
                split(b, (0, 1, 2), rels)
                if -1 in rels:
                    pool.wait_ge(veps_out, nth(b - 1, 1, 0))
                    pool.tensor_tensor(rstd[:, 2, :], veps[:, 2, :], halfs[0:TP, :], ALU.pow).then_inc(rstd_out, 1)
                split(b, (3, 4), rels)
                if 1 in rels:
                    pool.wait_ge(veps_made, nth(b + 1, 2, 0))
                    pool.tensor_tensor(rstd[:, 0, :], veps[:, 0, :], halfs[0:TP, :], ALU.pow).then_inc(rstd_made, 1)
                split(b, (5, 6), rels)
                if 1 in rels and not first:
                    scale_shift(pool, b + 1)
                if first:
                    low_half_v(0)
                split(b, (7, 8), rels)
                if 1 in rels:
                    pool.wait_ge(veps_made, nth(b + 1, 2, 1))
                    pool.tensor_tensor(rstd[:, 1, :], veps[:, 1, :], halfs[0:TP, :], ALU.pow).then_inc(rstd_made, 1)
                if first:
                    low_half_v(1)
                    pool.wait_ge(wo_halved, 1)
                    pool.tensor_tensor(wo_lo[:, :, :], wo_raw[:, :, :], wo_hi[:, :, :].bitcast(F32),
                                       ALU.subtract).then_inc(wo_halved, 1)
                split(b, (9, 10, 11), rels)
                if -1 in rels:
                    pool.wait_ge(pos_made, nth(b - 1, 1, 0))
                    stand_alone(pool)
                    for t in range(NT):
                        pool.indirect_dma_start(rows, bass.IndirectOffsetOnAxis(pos[:, t:t + 1], 0),
                                                rowbuf[:, t, :], None).then_inc(rows_sent, 16)
                if isinstance(b, int) and b == 0:
                    pool.wait_ge(dve_const, 3)
                    for s in range(SPARE):
                        r = E * STRIDE + s * SLOT
                        pool.dma_start(rows[r:r + SLOT, :], pad[:, :]).then_inc(rows_sent, 16)

            phase_one(pool, emit)

            def slot(s, par):
                pool.wait_ge(y_ready, s + 1)
                stand_alone(pool)
                pool.indirect_dma_start(out, bass.IndirectOffsetOnAxis(ids[:, par:par + 1], 0), yo[:, par, :], None,
                                        bounds_check=T - 1, oob_is_err=False).then_inc(out_sent[par], 16)

            with pool.Fori(0, N_SLOTS // 2) as i:
                for par in range(2):
                    slot(2 * i + par, par)
            for s in range(N_SLOTS // 2 * 2, N_SLOTS):
                slot(s, s % 2)

        @block.scalar
        def _(ac):
            def copy(dst, src):
                return nc.scalar.activation(dst, src, ACT.Copy)

            for i in range(3):
                for c in range(2):
                    cols = slice(i * H * HD, (i + 1) * H * HD)
                    ac.wait_ge(wq_landed[2 * i + c], 16)
                    copy(wq_hi[:, c, cols], wq_raw[:, c, cols]).then_inc(w_hi_made, 1)
            ac.wait_ge(wo_landed, 16)
            copy(wo_hi[:, :, :], wo_raw[:, :, :]).then_inc(wo_halved, 1)

            def take(unit, b):
                kind, index, rel = unit
                src = bank_of(unit)
                if kind in ("conv", "wout", "logits", "rank"):
                    return
                ac.wait_ge(pe_done[kind], count_of(kind, index, b + rel))
                if kind == "q":
                    copy(qz_hi[0:HD, index % 2, 0, :], src[0:HD, 0:LP])
                    copy(qz_hi[HD:, index % 2, 1, :], src[HD:, 0:LP]).then_inc(q_hi_taken, 1)
                elif kind == "k":
                    copy(kk_hi[:, index % 2, :], src[:, 0:LP]).then_inc(k_hi_taken, 1)
                elif kind == "v":
                    copy(vv[:, index[0] % 2, index[1], :], src[0:TP, 0:D]).then_inc(v_taken, 1)
                elif kind == "nT":
                    copy(nT_hi[:, :, index * TP:(index + 1) * TP],
                         src[:, 0:2 * TP].rearrange("p (c t) -> p c t", c=2)).then_inc(nT_hi_taken, 1)
                elif kind == "nT2":
                    copy(n2T[:, :, index * TP:(index + 1) * TP],
                         src[:, 0:2 * TP].rearrange("p (c t) -> p c t", c=2)).then_inc(nT2_taken, 1)

            def exps(h, b):
                ac.wait_ge(masked, nth(b, NT * H, NT * h + 2))
                for t in range(NT):
                    o, n = score_cols[t]
                    s = probs[:, h % 4, o:o + n]
                    last = nc.scalar.activation(s, s, ACT.Exp, bias=nmax[:, h % 4, t:t + 1], scale=-1.0,
                                                accum_out=rsum[:, h % 4, t:t + 1])
                last.then_inc(exp_done, 1)

            def probs_T(h, b):
                ac.wait_ge(probsT_done, nth(b, H, h))
                copy(probsT[:, h % 2, 0:L], tA[0:TP, 0:L]).then_inc(probsT_act, 1)

            def split(b, k, rels):
                if 0 in rels:
                    if isinstance(b, int) and b == 0 and k == 0:
                        ac.wait_ge(wo_halved, 2)
                    ac.wait_ge(chunk_landed[k % N_SPLIT], in_place(b, k) * 16)
                    copy(raw_hi[:, k % N_SPLIT, :], raw[:, k % N_SPLIT, :]).then_inc(chunk_hi_made, 1)

            def emit(b, rels):
                for p in range(NP):
                    pp, pb, prel = before(p, b, 1)
                    vp, vb, vrel = before(p, b, 2)
                    places = UNITS[p]
                    if vrel in rels:
                        ac.wait_ge(pv_done, nth(vb, NP, vp))
                        copy(aT_hi[:, vp, :], pv[:, 0:L]).then_inc(aT_hi_made, 1)
                    for un in units_of(places[0], rels):
                        take(un, b)
                    if 0 in rels:
                        exps(2 * p, b)
                    if prel in rels:
                        probs_T(2 * pp, pb)
                    for un in units_of(places[1], rels):
                        take(un, b)
                    if 2 * p < N_CHUNKS:
                        split(b, 2 * p, rels)
                    for un in units_of(places[2], rels):
                        take(un, b)
                    if 0 in rels:
                        exps(2 * p + 1, b)
                    if prel in rels:
                        probs_T(2 * pp + 1, pb)
                    for un in units_of(places[3], rels):
                        take(un, b)
                    if 2 * p < N_CHUNKS:
                        split(b, 2 * p + 1, rels)

            phase_one(ac, emit)

            def load_xs(s, par):
                row = ac.value_load(table[0:1, 2, bass.ds(s, 1)], min_val=0, max_val=ROWS - SLOT)
                ac.dma_start(xs[:, par, :], rows[bass.ds(row, SLOT), 0:D]).then_inc(xs_landed[par], 16)

            def load_hs(s, par):
                row = ac.value_load(table[0:1, 2, bass.ds(s, 1)], min_val=0, max_val=ROWS - SLOT)
                ac.dma_start(hs[:, par, :], rows[bass.ds(row, SLOT), D:2 * D + 4]).then_inc(hs_landed[par], 16)

            def gate(s, j):
                ac.wait_ge(g_added, 2 * s + j + 1)
                nc.scalar.activation(sg[:, j, :], gs[:, j, :], ACT.Sigmoid).then_inc(gated, 1)

            def take_actT(s, j):
                ac.wait_ge(pe_actT, 2 * s + j + 1)
                copy(actT_hi[:, j, :], (tA, tB)[j][:, :]).then_inc(actT_hi_taken, 1)

            def take_xsT(s, par):
                ac.wait_ge(pe_xsT, s + 1)
                copy(xsT_hi[:, 2 * par:2 * par + 2, :], pv[:, 0:256].rearrange("p (c t) -> p c t", c=2))\
                    .then_inc(xsT_hi_taken, 1)

            ac.wait_ge(slot_rows_made, 1)
            ac.wait_ge(rows_sent, (B * NT + SPARE) * 16)
            ac.wait_ge(pads_sent, E * 16)
            load_xs(0, 0)
            load_xs(1, 1)
            take_xsT(0, 0)

            def slot(s, par, pair):
                prev, cur, nxt, nxt2 = steps_of(s)
                if nxt2:
                    load_xs(s + 2, par)
                if cur:
                    if not (isinstance(s, int) and s < 2):
                        ac.wait_ge(y_ready, s - 1)
                    load_hs(s, par)
                    gate(s, 0)
                if prev:
                    take_actT(s - 1, 1)
                if nxt:
                    take_xsT(s + 1, 1 - par)
                if cur:
                    gate(s, 1)
                if cur:
                    take_actT(s, 0)

            phase_two(ac, slot)

        @block.vector
        def _(ve):
            V = nc.vector
            V.memset(pad[:, :], 0.0).then_inc(dve_const, 1)
            V.memset(halfs[:, :], -0.5).then_inc(dve_const, 1)
            ve.wait_ge(dve_const, 2)
            V.memset(pad[:, 2 * D:2 * D + 1].bitcast(I32), NO_TOKEN).then_inc(dve_const, 1)
            V.memset(ones[:, :], 1.0)
            for qz in (qz_hi, qz_lo):
                V.memset(qz[HD:, :, 0, :].bitcast(F32), 0.0)
                V.memset(qz[0:HD, :, 1, :].bitcast(F32), 0.0)
            V.memset(nT_hi[:, :, L:LP].bitcast(F32), 0.0)
            V.memset(nT_lo[:, :, L:LP].bitcast(F32), 0.0)
            V.memset(rowbuf[:, :, 2 * D:], 0.0)
            ve.wait_ge(pool_const, 7)
            V.tensor_copy(token_of[:, :], iot[:, 0:NT])
            V.tensor_copy(rev[:, :], iot[:, 8:8 + E])
            V.tensor_copy(eoff[:, :], iot[:, 16:16 + E])
            V.tensor_copy(cnt[:, :], iot[:, 16:16 + E])
            V.tensor_copy(slotf[:, :], iot[0:1, 32:32 + N_SLOTS]).then_inc(dve_const, 1)
            ve.wait_ge(dve_const, 4)
            V.tensor_scalar(slot_rows[:, :], slotf[:, :], float(SLOT), None, ALU.mult)
            V.tensor_tensor(upto[:, :, :], slotf[:, 0:E].unsqueeze(2).to_broadcast([1, E, E]),
                            slotf[:, 0:E].unsqueeze(1).to_broadcast([1, E, E]), ALU.is_ge)
            V.memset(rsum[:, :, :], 0.0).then_inc(dve_const, 1)
            ve.wait_ge(bias_landed, 16)
            V.tensor_scalar(bias2[:, :], bias2[:, :], 2.0, None, ALU.mult).then_inc(bias_doubled, 1)

            def low_halves(chunks):
                for n in chunks:
                    i, c = divmod(n, 2)
                    cols = slice(i * H * HD, (i + 1) * H * HD)
                    ve.wait_ge(w_hi_made, n + 1)
                    V.tensor_tensor(wq_lo[:, c, cols], wq_raw[:, c, cols], wq_hi[:, c, cols].bitcast(F32),
                                    ALU.subtract).then_inc(w_lo_made, 1)

            def take(unit, b):
                kind, index, rel = unit
                src = bank_of(unit)
                if kind in ("v", "nT2"):
                    return
                bb = b + rel
                ve.wait_ge(pe_done[kind], count_of(kind, index, bb))
                if kind == "q":
                    ve.wait_ge(q_hi_taken, count_of(kind, index, bb))
                    for a, half in enumerate((slice(0, HD), slice(HD, 2 * HD))):
                        last = V.tensor_tensor(qz_lo[half, index % 2, a, :], src[half, 0:LP],
                                               qz_hi[half, index % 2, a, :].bitcast(F32), ALU.subtract)
                    last.then_inc(q_lo_taken, 1)
                elif kind == "k":
                    ve.wait_ge(k_hi_taken, count_of(kind, index, bb))
                    V.tensor_tensor(kk_lo[:, index % 2, :], src[:, 0:LP], kk_hi[:, index % 2, :].bitcast(F32),
                                    ALU.subtract).then_inc(k_lo_taken, 1)
                elif kind == "nT":
                    cols = slice(index * TP, (index + 1) * TP)
                    ve.wait_ge(nT_hi_taken, count_of(kind, index, bb))
                    V.tensor_tensor(nT_lo[:, :, cols], src[:, 0:2 * TP].rearrange("p (c t) -> p c t", c=2),
                                    nT_hi[:, :, cols].bitcast(F32), ALU.subtract).then_inc(nT_lo_taken, 1)
                elif kind == "conv":
                    ve.wait_ge(xsum_step, nth(bb, 2, 1))
                    V.scalar_tensor_tensor(out=u[:, index, :], in0=xsum[:, index, :], scalar=0.5,
                                           in1=src[0:TP, 0:D], op0=ALU.mult, op1=ALU.add).then_inc(conv_taken, 1)
                    ve.wait_ge(conv_taken, nth(bb, NT, index))
                    V.bn_stats(st6[:, 0, index, :], u[:, index, :]).then_inc(stats_made, 1)
                elif kind == "wout":
                    if index == 0:
                        ve.wait_ge(rows_sent, bb * (NT * 16) + SPARE * 16)
                    o = (bb % 2) * (NT * D) + index * D
                    V.tensor_tensor(rowbuf[:, index, D:2 * D], src[0:TP, 0:D], h1[:, bass.ds(o, D)], ALU.add)\
                        .then_inc(wout_taken, 1)
                    ve.wait_ge(wout_taken, nth(bb, NT, index))
                    V.bn_stats(st6[:, 2, index, :], rowbuf[:, index, D:2 * D]).then_inc(stats_out, 1)
                elif kind == "logits":
                    V.tensor_tensor(lg[:, :, :], src[0:TP, 0:NT * E].rearrange("p (t e) -> p t e", t=NT),
                                    rb[0:TP, :].unsqueeze(1).to_broadcast([TP, NT, E]), ALU.add)\
                        .then_inc(logits_taken, 1)
                elif kind == "rank":
                    V.tensor_tensor(r1[:, :, :], src[0:TP, 0:NT * E].rearrange("p (t e) -> p t e", t=NT),
                                    cnt[0:TP, :].unsqueeze(1).to_broadcast([TP, NT, E]), ALU.add)
                    V.tensor_tensor(cnt_new[:, :], cnt[:, :], src[:, NT * E:(NT + 1) * E], ALU.add)\
                        .then_inc(rank_taken, 1)

            def norm_stats(which, batch, stats, n, made):
                ve.wait_ge(stats, n)
                stand_alone(ve)
                for t in range(NT):
                    V.bn_aggr(mv[:, which, t, :], st6[:, which, t, :]).then_inc(aggr_made[which], 1)
                ve.wait_ge(aggr_made[which], nth(batch, NT, NT - 1))
                V.tensor_scalar(veps[:, which, :], mv[:, which, :, 1], EPS, None, ALU.add).then_inc(made, 1)

            def normalise(dst, src, which):
                for t in range(NT):
                    last = V.tensor_scalar(dst[:, t, 0:D], src(t), mv[:, which, t, 0:1], rstd[:, which, t:t + 1],
                                           ALU.subtract, ALU.mult)
                return last

            def choose(bb):
                def link(ins, k):
                    ins.then_inc(route_step, 1)
                    ve.wait_ge(route_step, nth(bb, 4, k))
                ve.wait_ge(logits_taken, nth(bb, 1, 0))
                link(V.tensor_reduce(rm[:, 0, :], lg[:, :, :], AX.X, ALU.max), 0)
                link(V.tensor_tensor(r1[:, :, :], lg[:, :, :], rm[:, 0, :].unsqueeze(2).to_broadcast([TP, NT, E]),
                                     ALU.is_equal), 1)
                revb = rev[0:TP, :].unsqueeze(1).to_broadcast([TP, NT, E])
                link(V.tensor_tensor(r2[:, :, :], r1[:, :, :], revb, ALU.mult), 2)
                link(V.tensor_reduce(rm[:, 1, :], r2[:, :, :], AX.X, ALU.max), 3)
                V.tensor_tensor(onehot[:, :, :], revb, rm[:, 1, :].unsqueeze(2).to_broadcast([TP, NT, E]),
                                ALU.is_equal).then_inc(onehot_made, 1)

            def place_rows(bb):
                ve.wait_ge(rank_taken, nth(bb, 1, 0))
                V.tensor_copy(cnt[:, :], cnt_new[:, :]).then_inc(cnt_made, 1)
                V.tensor_tensor(r2[:, :, :], r1[:, :, :], onehot[:, :, :], ALU.mult).then_inc(place_step, 1)
                V.tensor_copy(rowbuf[:, :, 2 * D].bitcast(I32), token_of[0:TP, :]).then_inc(place_step, 1)
                ve.wait_ge(place_step, nth(bb, 3, 1))
                V.tensor_reduce(rm[:, 2, :], r2[:, :, :], AX.X, ALU.add).then_inc(place_step, 1)
                V.tensor_scalar(token_of[:, :], token_of[:, :], float(L), None, ALU.add).then_inc(token_made, 1)
                ve.wait_ge(place_step, nth(bb, 3, 2))
                V.tensor_copy(pos[:, :], rm[:, 2, :]).then_inc(pos_made, 1)
                ve.wait_ge(cnt_made, nth(bb, 1, 0))
                ve.wait_ge(token_made, nth(bb, 1, 0))

            def mask_max(h, b):
                ve.wait_ge(scores_done, nth(b, H, h))
                stand_alone(ve)
                for t in range(NT):
                    o, n = score_cols[t]
                    bk, bo = score_bank[t]
                    V.tensor_tensor_reduce(out=probs[:, h % 4, o:o + n], in0=bk[0:TP, bo:bo + n],
                                           in1=mask[0:TP, L - n:L], scale=-HD ** -0.5, scalar=3e38, op0=ALU.add,
                                           op1=ALU.min, accum_out=nmax[:, h % 4, t:t + 1]).then_inc(masked, 1)

            def divide(h, b):
                ve.wait_ge(exp_done, nth(b, H, h))
                V.reciprocal(rinv[:, h % 4, :], rsum[:, h % 4, :]).then_inc(rinv_made, 1)
                ve.wait_ge(rinv_made, nth(b, H, h))
                for t in range(NT):
                    o, n = score_cols[t]
                    s = probs[:, h % 4, o:o + n]
                    last = V.tensor_scalar(s, s, rinv[:, h % 4, t:t + 1], None, ALU.mult)
                last.then_inc(probs_ready, 1)

            def probs_T(h, b):
                ve.wait_ge(probsT_done, nth(b, H, h))
                V.tensor_copy(probsT[:, h % 2, L:2 * L], tB[0:TP, 0:L]).then_inc(probsT_dve, 1)

            def emit(b, rels):
                for p in range(NP):
                    pp, pb, prel = before(p, b, 1)
                    vp, vb, vrel = before(p, b, 2)
                    places = UNITS[p]
                    if 0 in rels:
                        mask_max(2 * p, b)
                    if vrel in rels:
                        ve.wait_ge(pv_done, nth(vb, NP, vp))
                        ve.wait_ge(aT_hi_made, nth(vb, NP, vp))
                        V.tensor_tensor(aT_lo[:, vp, :], pv[:, 0:L], aT_hi[:, vp, :].bitcast(F32), ALU.subtract)\
                            .then_inc(aT_lo_made, 1)
                    if prel in rels:
                        probs_T(2 * pp, pb)
                    for un in units_of(places[0], rels):
                        take(un, b)
                    if prel in rels:
                        divide(2 * pp + 1, pb)
                    for un in units_of(places[1], rels):
                        take(un, b)
                    if 0 in rels:
                        mask_max(2 * p + 1, b)
                    if p == 3 and 1 in rels:
                        ve.wait_ge(rstd_made, nth(b + 1, 2, 0))
                        normalise(z, lambda t: u[:, t, :], 0).then_inc(normed, 1)
                        if 0 not in rels:
                            ve.wait_ge(affine_landed, 32)
                            scale_shift(ve, b + 1)
                    if p == 7 and 0 not in rels and 1 in rels:
                        low_halves(range(3, 4))
                        ve.wait_ge(router_landed, 32)
                    if p == 5 and 1 in rels:
                        ve.wait_ge(rstd_made, nth(b + 1, 2, 1))
                        normalise(n1, lambda t: h1[:, bass.ds(((b + 1) % 2) * (NT * D) + t * D, D)], 1)\
                            .then_inc(normed, 1)
                        if 0 not in rels:
                            low_halves(range(2, 3))
                    for un in units_of(places[2], rels):
                        take(un, b)
                    if prel in rels:
                        probs_T(2 * pp + 1, pb)
                    if 0 in rels:
                        divide(2 * p, b)
                    for un in units_of(places[3], rels):
                        take(un, b)
                    if p == 1 and -1 in rels:
                        norm_stats(2, b - 1, stats_out, nth(b - 1, NT, NT - 1), veps_out)
                    if p == 2 and -1 in rels:
                        ve.wait_ge(rstd_out, nth(b - 1, 1, 0))
                        normalise(rowbuf, lambda t: rowbuf[:, t, D:2 * D], 2).then_inc(normed_out, 1)
                    if p == 2 and 1 in rels:
                        norm_stats(0, b + 1, stats_made, nth(b + 1, 2 * NT, NT - 1), veps_made)
                        if 0 not in rels:
                            low_halves(range(1))
                    if p == 5 and -1 in rels:
                        choose(b - 1)
                    if p == 4 and 1 in rels:
                        ve.wait_ge(affine, nth(b + 1, 2, 1))
                        for t in range(NT):
                            V.bn_stats(st6[:, 1, t, :], h1[:, bass.ds(((b + 1) % 2) * (NT * D) + t * D, D)])\
                                .then_inc(stats_made, 1)
                        norm_stats(1, b + 1, stats_made, nth(b + 1, 2 * NT, 2 * NT - 1), veps_made)
                        if 0 not in rels:
                            low_halves(range(1, 2))
                    if p == 7 and -1 in rels:
                        place_rows(b - 1)

            ve.wait_ge(pool_const, N_CONST)
            ve.wait_ge(bias_doubled, 1)
            sum_steps(ve, 0)
            phase_one(ve, emit)

            steps = [0]

            def step(ins):
                steps[0] += 1
                ins.then_inc(table_step, 1)

            def settle():
                ve.wait_ge(table_step, steps[0])

            NS = N_SLOTS
            c8 = lambda i: tb[:, i, 0:E]
            by_slot = lambda i: tb[:, i, 32:32 + NS]
            ends = tb[:, 3, 0:E]
            ve.wait_ge(cnt_made, B)
            V.tensor_copy(padrow[:, :], cnt[0:1, :]).then_inc(padrow_made, 1)
            step(V.tensor_tensor(c8(0), cnt[0:1, :], eoff[0:1, :], ALU.subtract))
            settle()
            step(V.tensor_scalar(tbi[:, 0, 0:E], c8(0), float(SLOT - 1), None, ALU.add))
            settle()
            step(V.tensor_scalar(tbi[:, 1, 0:E], tbi[:, 0, 0:E], 7, None, ALU.arith_shift_right))
            settle()
            step(V.tensor_copy(c8(1), tbi[:, 1, 0:E]))
            settle()
            step(V.tensor_scalar(c8(2), c8(1), float(-SLOT), float(STRIDE), ALU.mult, ALU.add))
            step(V.tensor_tensor(ends8[:, :, :], upto[:, :, :], c8(1).unsqueeze(1).to_broadcast([1, E, E]), ALU.mult))
            settle()
            step(V.tensor_reduce(ends, ends8[:, :, :], AX.X, ALU.add))
            settle()
            step(V.tensor_tensor(reached[:, :, :], slotf[:, :].unsqueeze(2).to_broadcast([1, NS, E]),
                                 ends.unsqueeze(1).to_broadcast([1, NS, E]), ALU.is_ge))
            settle()
            step(V.tensor_tensor(jump[:, :, :], reached[:, :, :],
                                 c8(2).unsqueeze(1).to_broadcast([1, NS, E]), ALU.mult))
            settle()
            step(V.tensor_reduce(by_slot(1), jump[:, :, :], AX.X, ALU.add))
            settle()
            V.tensor_tensor(table[:, 2, 0:NS], by_slot(1), slot_rows[:, :], ALU.add).then_inc(slot_rows_made, 1)
            has, rank, past = tb[:, 0, 8:16], tb[:, 1, 8:16], tb[:, 2, 8:16]
            last_load = tb[:, 3, 8:9]
            by_load = lambda i: tb[:, i, 16:24]
            step(V.tensor_scalar(has, c8(1), 1.0, None, ALU.min))
            settle()
            step(V.memset(has[:, 0:2], 1.0))
            settle()
            step(V.tensor_tensor(ends8[:, :, :], upto[:, :, :], has.unsqueeze(1).to_broadcast([1, E, E]), ALU.mult))
            step(V.tensor_tensor(jump[:, :, :], reached[:, :, :], has.unsqueeze(1).to_broadcast([1, NS, E]), ALU.mult))
            settle()
            step(V.tensor_reduce(rank, ends8[:, :, :], AX.X, ALU.add))
            step(V.tensor_reduce(by_slot(0), jump[:, :, :], AX.X, ALU.add))
            settle()
            step(V.tensor_scalar(last_load, rank[:, E - 1:E], -1.0, None, ALU.add))
            step(V.tensor_tensor(before8[:, :, :], slotf[:, 0:E].unsqueeze(2).to_broadcast([1, E, E]),
                                 rank.unsqueeze(1).to_broadcast([1, E, E]), ALU.is_ge))
            step(V.tensor_tensor(through8[:, :, :], slotf[:, 1:E + 1].unsqueeze(2).to_broadcast([1, E, E]),
                                 rank.unsqueeze(1).to_broadcast([1, E, E]), ALU.is_ge))
            settle()
            step(V.tensor_scalar(by_slot(2), by_slot(0), last_load, None, ALU.min))
            step(V.tensor_reduce(by_load(0), before8[:, :, :], AX.X, ALU.add))
            step(V.tensor_tensor(ends8[:, :, :], through8[:, :, :],
                                 c8(1).unsqueeze(1).to_broadcast([1, E, E]), ALU.mult))
            step(V.tensor_scalar(past, slotf[:, 0:E], last_load, float(NS), ALU.is_ge, ALU.mult))
            settle()
            step(V.tensor_scalar(expert_of[:, :], by_load(0), float(E - 1), None, ALU.min))
            step(V.tensor_reduce(by_load(1), ends8[:, :, :], AX.X, ALU.add))
            settle()
            step(V.tensor_tensor(by_load(2), by_load(1), past, ALU.add))
            settle()
            step(V.tensor_scalar(endw[:, :], by_load(2), float(NS), 1.0, ALU.min, ALU.add))
            step(V.tensor_scalar(table[:, 0, 0:NS], by_slot(2), 1.0, None, ALU.add))
            step(V.tensor_scalar(by_slot(0), by_slot(2), 3.0, -3.0, ALU.is_ge, ALU.mult))
            step(V.tensor_scalar(by_slot(1), by_slot(2), 6.0, -3.0, ALU.is_ge, ALU.mult))
            settle()
            step(V.tensor_tensor(by_slot(3), by_slot(0), by_slot(1), ALU.add))
            settle()
            step(V.tensor_tensor(by_slot(0), by_slot(2), by_slot(3), ALU.add))
            settle()
            step(V.tensor_scalar(table[:, 1, 0:NS], by_slot(0), float(BLOCK), None, ALU.mult))
            settle()
            ve.sem_inc(table_made, 1)
            ve.sem_inc(slots_done, 1)

            def block_of(s):
                return ve.value_load(table[0:1, 1, bass.ds(s, 1)], min_val=0, max_val=(N_EW - 1) * BLOCK)

            B1 = 2 * WCOLS

            def low_xsT(s, par):
                ve.wait_ge(xsT_hi_taken, s + 1)
                V.tensor_tensor(xsT_lo[:, 2 * par:2 * par + 2, :], pv[:, 0:256].rearrange("p (c t) -> p c t", c=2),
                                xsT_hi[:, 2 * par:2 * par + 2, :].bitcast(F32), ALU.subtract).then_inc(xsT_lo_taken, 1)

            def low_actT(s, j):
                ve.wait_ge(actT_hi_taken, 2 * s + j + 1)
                V.tensor_tensor(actT_lo[:, j, :], (tA, tB)[j][:, :], actT_hi[:, j, :].bitcast(F32), ALU.subtract)\
                    .then_inc(actT_lo_taken, 1)

            def up(s, j, block_col):
                if j == 0:
                    e1 = ve.value_load(table[0:1, 0, bass.ds(s, 1)], min_val=1, max_val=E)
                    ve.wait_ge(weights_ready, e1)
                ve.wait_ge(pe_up, 4 * s + 2 * j + 1)
                V.tensor_tensor(gs[:, j, :], up_bank[2 * j][:, :],
                                ew[:, bass.ds(block_col + (B1 + HID + 512 * j), 512)], ALU.add).then_inc(g_added, 1)
                ve.wait_ge(pe_up, 4 * s + 2 * j + 2)
                V.tensor_tensor(as_[:, j, :], up_bank[2 * j + 1][:, :], ew[:, bass.ds(block_col + (B1 + 512 * j), 512)],
                                ALU.add).then_inc(a_added, 1)
                ve.wait_ge(a_added, 2 * s + j + 1)
                ve.wait_ge(gated, 2 * s + j + 1)
                V.tensor_tensor(act[:, j, :], as_[:, j, :], sg[:, j, :], ALU.mult).then_inc(act_ready, 1)

            def finish(s, par, n, block_col):
                ve.wait_ge(pe_y, s + 1)
                ve.wait_ge(hs_landed[par], n * 16)
                V.tensor_tensor(ys[:, :], y_bank[:, 0:D], ew[:, bass.ds(block_col + (B1 + 2 * HID), D)], ALU.add)\
                    .then_inc(y_biased, 1)
                ve.wait_ge(y_biased, s + 1)
                if not (isinstance(s, int) and s < 2):
                    ve.wait_ge(out_sent[par], 16 * (n - 1))
                V.tensor_copy(ids[:, par:par + 1], hs[:, par, D:D + 1].bitcast(U32)).then_inc(slots_done, 1)
                V.tensor_tensor(yo[:, par, :], ys[:, :], hs[:, par, 0:D], ALU.add).then_inc(y_ready, 1)

            def slot(s, par, pair):
                prev, cur, nxt, _ = steps_of(s)
                if cur:
                    block_col = block_of(s)
                    up(s, 0, block_col)
                if prev:
                    low_actT(s - 1, 1)
                if nxt:
                    low_xsT(s + 1, 1 - par)
                if cur:
                    up(s, 1, block_col)
                if cur:
                    low_actT(s, 0)
                if prev:
                    finish(s - 1, 1 - par, pair + par, block_of(s - 1))

            low_xsT(0, 0)
            phase_two(ve, slot)

        @block.tensor
        def _(pe):
            def mm(o, l, r, start, stop):
                return nc.tensor.matmul(o, l, r, start=start, stop=stop)

            def mm3(o, lh, ll, rh, rl, start, stop):
                mm(o, lh, rh, start, False)
                mm(o, lh, rl, False, False)
                return mm(o, ll, rh, False, stop)

            def wout_part(index, bb, pairs):
                dst = bank_of(("wout", index, -1))
                tok = slice(index * TP, (index + 1) * TP)
                if isinstance(bb, int) and bb == 0:
                    pe.wait_ge(wo_halved, 2)
                for c in pairs:
                    if c == pairs[0] or c == NP - 1:
                        pe.wait_ge(aT_lo_made, nth(bb, NP, max(c, NP - 3)))
                    last = mm3(dst[0:TP, 0:D], aT_hi[:, c, tok], aT_lo[:, c, tok], wo_hi[:, c, :], wo_lo[:, c, :],
                               c == 0, c == NP - 1)
                return last

            def free_bank(un, b):
                i = ORDER.index(un)
                dst = bank_of(un)
                for back in range(1, 2 * len(ORDER)):
                    j = i - back
                    it = b if j >= 0 else b - 1
                    other = ORDER[j % len(ORDER)]
                    if bank_of(other) is not dst:
                        continue
                    if isinstance(b, int) and not 0 <= it + other[2] < B:
                        if it < -1:
                            break
                        continue
                    for s_ in taken[other[0]]:
                        pe.wait_ge(s_, count_of(other[0], other[1], it + other[2]))
                    break

            def unit(un, b):
                kind, index, rel = un
                dst = bank_of(un)
                bb = b + rel
                if kind == "wout" and isinstance(b, int) and b == B:
                    wout_part(index, bb, range(NP - 2, NP)).then_inc(pe_done[kind], 1)
                    return
                free_bank(un, b)
                if kind == "wout":
                    last = wout_part(index, bb, range(NP))
                elif kind in ("q", "k", "v"):
                    pe.wait_ge(nT_lo_taken, nth(bb, NT, NT - 1))
                    if isinstance(b, int) and b < 0:
                        pe.wait_ge(*{"q": (w_lo_made, 2), "k": (w_lo_made, 4), "v": (w_lo_v_made, 2)}[kind])
                if kind in ("q", "k"):
                    o = index * 2 * HD + (H * HD if kind == "k" else 0)
                    for c in range(2):
                        last = mm3(dst[:, 0:LP], wq_hi[:, c, o:o + 128], wq_lo[:, c, o:o + 128],
                                   nT_hi[:, c, :], nT_lo[:, c, :], c == 0, c == 1)
                elif kind == "v":
                    g, t = index
                    o = 2 * H * HD + g * D
                    tok = slice(t * TP, (t + 1) * TP)
                    for c in range(2):
                        last = mm3(dst[0:TP, 0:D], nT_hi[:, c, tok], nT_lo[:, c, tok],
                                   wq_hi[:, c, o:o + D], wq_lo[:, c, o:o + D], c == 0, c == 1)
                elif kind == "conv":
                    pe.wait_ge(xT_landed, nth(bb, 1, 0) * 16)
                    if isinstance(b, int) and b < 0:
                        pe.wait_ge(wc_landed, 16)
                    for c in range(4):
                        last = mm(dst[0:TP, 0:D], xT_in[:, c, index * TP:(index + 1) * TP], wc[:, c, :],
                                  c == 0, c == 3)
                elif kind in ("nT", "nT2"):
                    if kind == "nT":
                        pe.wait_ge(normed, nth(bb, 2, 1))
                        if isinstance(b, int) and b < 0 and index == 0:
                            pe.wait_ge(pool_const, N_CONST)
                            pe.wait_ge(dve_const, 5)
                            pe.wait_ge(router_landed, 32)
                    else:
                        pe.wait_ge(normed_out, nth(bb, 1, 0))
                    src = n1 if kind == "nT" else rowbuf
                    for c in range(2):
                        last = nc.tensor.transpose(dst[:, c * TP:(c + 1) * TP], src[:, index, c * 128:(c + 1) * 128],
                                                   ident[0:TP, 0:TP])
                elif kind == "logits":
                    pe.wait_ge(nT2_taken, nth(bb, NT, NT - 1))
                    for t in range(NT):
                        for c in range(2):
                            last = mm(dst[0:TP, t * E:(t + 1) * E], n2T[:, c, t * TP:(t + 1) * TP], rw[:, c, :],
                                      c == 0, c == 1)
                elif kind == "rank":
                    pe.wait_ge(onehot_made, nth(bb, 1, 0))
                    for t in range(NT + 1):
                        o = dst[:, t * E:(t + 1) * E]
                        for t2 in range(min(t, NT)):
                            last = mm(o, ones[0:TP, :], onehot[:, t2, :], t2 == 0, t == NT and t2 == NT - 1)
                        if t < NT:
                            last = mm(o, tri[0:TP, :], onehot[:, t, :], t == 0, True)
                last.then_inc(pe_done[kind], 1)

            def scores(h, b):
                p = h // 2
                pe.wait_ge(q_lo_taken, nth(b, NP, p))
                pe.wait_ge(k_lo_taken, nth(b, NP, p))
                if not (isinstance(b, int) and b == 0 and h == 0):
                    pe.wait_ge(masked, b * (NT * H) + NT * h)
                for t in (0, 2, 1):
                    bk, o = score_bank[t]
                    n = (FEW, 2 * TP, LP)[t]
                    q = slice(t * TP, (t + 1) * TP)
                    last = mm3(bk[0:TP, o:o + n], qz_hi[:, p % 2, h % 2, q], qz_lo[:, p % 2, h % 2, q],
                               kk_hi[:, p % 2, 0:n], kk_lo[:, p % 2, 0:n], True, True)
                last.then_inc(scores_done, 1)

            def transposes(h, b):
                pe.wait_ge(probs_ready, nth(b, H, h))
                if not (isinstance(b, int) and b == 0 and h == 0):
                    pe.wait_ge(probsT_act, b * H + h)
                    pe.wait_ge(probsT_dve, b * H + h)
                for j in range(NT):
                    for t in range(j, NT):
                        bk, o = ((tA, t * TP), (tB, (t - 1) * TP), (tB, 2 * TP))[j]
                        c = score_cols[t][0] + j * TP
                        last = nc.tensor.transpose(bk[0:TP, o:o + TP], probs[:, h % 4, c:c + TP], ident[0:TP, 0:TP])
                last.then_inc(probsT_done, 1)

            def values(p, b):
                pe.wait_ge(probsT_act, nth(b, H, 2 * p + 1))
                pe.wait_ge(probsT_dve, nth(b, H, 2 * p + 1))
                pe.wait_ge(v_taken, nth(b, NG * NT, p // 2 * NT + 2))
                if not (isinstance(b, int) and b == 0 and p == 0):
                    pe.wait_ge(aT_lo_made, b * NP + p)
                for j, (o, n, first) in enumerate(((0, L, 0), (L, 2 * TP, TP), (L + 2 * TP, TP, 2 * TP))):
                    for a in range(2):
                        c = (p % 2) * 2 * HD + a * HD
                        last = nc.tensor.matmul(pv[a * HD:(a + 1) * HD, first:L], vv[:, p // 2 % 2, j, c:c + HD],
                                                probsT[:, a, o:o + n], start=(j == 0), stop=(j == NT - 1))
                last.then_inc(pv_done, 1)

            def emit(b, rels):
                for p in range(NP):
                    pp, pb, prel = before(p, b, 1)
                    vp, vb, vrel = before(p, b, 2)
                    places = UNITS[p]
                    if 0 in rels:
                        scores(2 * p, b)
                    if p == 0 and 0 not in rels and -1 in rels:
                        for t in range(NT):
                            free_bank(("wout", t, -1), b)
                            wout_part(t, b - 1, range(NP - 2))
                    if vrel in rels:
                        values(vp, vb)
                    for un in units_of(places[0], rels):
                        unit(un, b)
                    if prel in rels:
                        transposes(2 * pp, pb)
                    for un in units_of(places[1], rels):
                        unit(un, b)
                    if 0 in rels:
                        scores(2 * p + 1, b)
                    for un in units_of(places[2], rels):
                        unit(un, b)
                    if prel in rels:
                        transposes(2 * pp + 1, pb)
                    for un in units_of(places[3], rels):
                        unit(un, b)

            phase_one(pe, emit)

            pe.wait_ge(table_made, 1)

            def weights(s):
                return pe.value_load(table[0:1, 1, bass.ds(s, 1)], min_val=0, max_val=(N_EW - 1) * BLOCK)

            def w_halves(w, o, n):
                return [ew[:, bass.ds(w + (half * WCOLS + o), n)].bitcast(F32R) for half in range(2)]

            def transpose_x(par, n):
                pe.wait_ge(xs_landed[par], n * 16)
                for c in range(2):
                    cols = slice(c * 128, (c + 1) * 128)
                    last = nc.tensor.transpose(pv[:, cols], xs[:, par, cols], ident[:, :])
                last.then_inc(pe_xsT, 1)

            def up(s, j, par, w):
                if j == 0:
                    e1 = pe.value_load(table[0:1, 0, bass.ds(s, 1)], min_val=1, max_val=E)
                    pe.wait_ge(weights_ready, e1)
                    pe.wait_ge(xsT_lo_taken, s + 1)
                for i, col in enumerate((HID + 512 * j, 512 * j)):
                    if not (isinstance(s, int) and s == 0):
                        pe.wait_ge((g_added, a_added)[i], 2 * s + j - 1)
                    for c in range(2):
                        o = c * 2 * HID + col
                        last = mm3(up_bank[2 * j + i][:, :], xsT_hi[:, 2 * par + c, :], xsT_lo[:, 2 * par + c, :],
                                   *w_halves(w, o, 512),
                                   c == 0, c == 1)
                    last.then_inc(pe_up, 1)

            def transpose_act(s, j):
                pe.wait_ge(act_ready, 2 * s + j + 1)
                if not (isinstance(s, int) and s == 0):
                    pe.wait_ge(actT_lo_taken, 2 * s + j - 1)
                for c in range(4):
                    cols = slice(c * 128, (c + 1) * 128)
                    last = nc.tensor.transpose((tA, tB)[j][:, cols], act[:, j, cols], ident[:, :])
                last.then_inc(pe_actT, 1)

            def down(s, j, w):
                pe.wait_ge(actT_lo_taken, 2 * s + j + 1)
                if j == 0 and not (isinstance(s, int) and s == 0):
                    pe.wait_ge(y_biased, s)
                for c in range(4):
                    cols = slice(c * 128, (c + 1) * 128)
                    o = W1C + (4 * j + c) * D
                    last = mm3(y_bank[:, 0:D], actT_hi[:, j, cols], actT_lo[:, j, cols],
                               *w_halves(w, o, D),
                               j == 0 and c == 0, j == 1 and c == 3)
                if j == 1:
                    last.then_inc(pe_y, 1)

            def slot(s, par, pair):
                prev, cur, nxt, _ = steps_of(s)
                if cur:
                    w = weights(s)
                    up(s, 0, par, w)
                if prev:
                    w_prev = weights(s - 1)
                    transpose_act(s - 1, 1)
                if nxt:
                    transpose_x(1 - par, pair + par + 1)
                if prev:
                    down(s - 1, 0, w_prev)
                if cur:
                    up(s, 1, par, w)
                if cur:
                    transpose_act(s, 0)
                if prev:
                    down(s - 1, 1, w_prev)

            transpose_x(0, 1)
            phase_two(pe, slot)


INS = ["xT", "x", "conv_w", "conv_b", "gamma", "beta", "w_qkv", "w_out", "router_w", "router_b",
       "w1", "b1", "w2", "b2"]


def kernel(x, L0_tok_conv_w, L0_tok_conv_b, L0_tok_ln_gamma, L0_tok_ln_beta, L0_attn_W_qkv, L0_attn_W_out,
           L0_ffn_router_w, L0_ffn_router_b, L0_ffn_w1, L0_ffn_b1, L0_ffn_w2, L0_ffn_b2):
    import numpy as np
    import concourse.bacc as bacc
    from concourse.bass_utils import run_bass_kernel_spmd

    x = np.asarray(x)
    pairs = x.reshape(T, 2 * D)
    values = {
        "xT": pairs.T.reshape(4, 128, T).transpose(1, 0, 2),
        "x": pairs.reshape(B, NT, TP, 2 * D),
        "conv_w": np.asarray(L0_tok_conv_w).transpose(2, 1, 0).reshape(4, 128, D).transpose(1, 0, 2),
        "conv_b": L0_tok_conv_b, "gamma": L0_tok_ln_gamma, "beta": L0_tok_ln_beta,
        "w_qkv": L0_attn_W_qkv, "w_out": L0_attn_W_out,
        "router_w": L0_ffn_router_w, "router_b": L0_ffn_router_b,
        "w1": L0_ffn_w1, "b1": L0_ffn_b1, "w2": L0_ffn_w2, "b2": L0_ffn_b2,
    }
    nc = bacc.Bacc("TRN2", target_bir_lowering=False, num_devices=1)
    arrays, args = {}, []
    for name in INS:
        a = np.ascontiguousarray(values[name])
        arrays[f"in_{name}"] = a
        args.append(nc.dram_tensor(f"in_{name}", a.shape, mybir.dt.from_np(a.dtype), kind="ExternalInput").ap())
    args.append(nc.dram_tensor("out_rows", (T, D), F32, kind="ExternalOutput").ap())
    tower(nc, *args)
    r = run_bass_kernel_spmd(nc, [arrays], core_ids=[0])
    return r.results[0]["out_rows"].reshape(B, L, D)
```
